# Optimizing a Trainium2 kernel written in Bass

```python
import numpy as np
import jax
import jax.numpy as jnp

def _softmax(x, axis=-1):
    return jax.nn.softmax(x, axis=axis)

def _gelu(x):
    return jax.nn.gelu(x, approximate=True)

def _silu(x):
    return jax.nn.silu(x)

def _sigmoid(x):
    return jax.nn.sigmoid(x)

def _layernorm(x, axis=-1, eps=1e-05):
    m = jnp.mean(x, axis=axis, keepdims=True)
    v = jnp.var(x, axis=axis, keepdims=True)
    return (x - m) / jnp.sqrt(v + eps)

def _scatter_add(tgt, idx, src, axis=0):
    return tgt.at[idx].add(src)

def _segment_sum(src, seg, n):
    return jax.ops.segment_sum(src, seg, n)
kernel_name = 'mk_flamingo_gated_d2_seqx_r8_19c38b'

def setup_inputs(seed: int=0):
    np.random.seed(seed)
    _w = jnp.asarray

    def _rec_inputs():
        import jax
        import jax.numpy as jnp
        _rk = jax.random.key(seed)
        x = -0.0002928 + 1 * jax.random.normal(jax.random.fold_in(_rk, 1), (8, 128, 512), jnp.float32)
        _lenS = 128 - jax.random.randint(jax.random.fold_in(_rk, 7), (8,), 0, max(1, 128 // 4) + 1, jnp.int32)
        _lenS2 = 128 - jax.random.randint(jax.random.fold_in(_rk, 8), (8,), 0, max(1, 128 // 4) + 1, jnp.int32)
        _ctx_4096P = jax.random.normal(jax.random.fold_in(_rk, 11), (8, 16, 512), jnp.float32)
        _ctx_4096c = jax.random.dirichlet(jax.random.fold_in(_rk, 511), 0.3 * jnp.ones((16,), jnp.float32), (8, 128))
        _ctx_4096t = jnp.einsum('bsk,bkd->bsd', _ctx_4096c, _ctx_4096P)
        _ctx_4096t = _ctx_4096t * jax.lax.rsqrt(jnp.mean(jnp.square(_ctx_4096t)) + 1e-12) * 0.953939
        ctx_4096 = -2.8382e-05 + 0.999851 * (_ctx_4096t + 0.3 * jax.random.normal(jax.random.fold_in(_rk, 611), (8, 128, 512), jnp.float32))
        _validS = jnp.arange(128)[None, :] < _lenS[:, None]
        _validS2 = jnp.arange(128)[None, :] < _lenS2[:, None]
        _causal = jnp.tril(jnp.ones((128, 128), dtype=bool))
        mask_1x1xSxS2_ff0 = jnp.where(jnp.ones((1, 1, 128, 128), dtype=bool), 0.0, -1000000000.0).astype(jnp.float32)
        _g = jax.random.normal(jax.random.fold_in(_rk, 9001), (2, 2), jnp.float32)
        _g = jnp.sign(_g) * jnp.maximum(jnp.abs(_g), 1.0) + (_g == 0) * 1.0
        g_xattn = _g[0]
        g_ffn = _g[1]
        return (x, ctx_4096, mask_1x1xSxS2_ff0, g_xattn, g_ffn)
    x, ctx_4096, mask_1x1xSxS2_ff0, g_xattn, g_ffn = _rec_inputs()

    def _L0_xattn_setup():
        import jax, jax.numpy as jnp
        import numpy as np
        NUM_HEADS = 32
        NUM_KV_HEADS = 8
        HEAD_DIM = 128
        HIDDEN = 512
        EPS = 1e-05

        def rmsnorm(x, w, eps=EPS):
            xf = x.astype(jnp.float32)
            var = jnp.mean(xf * xf, axis=-1, keepdims=True)
            return w * (xf * jax.lax.rsqrt(var + eps)).astype(x.dtype)
        key = jax.random.key(seed)
        ks = jax.random.split(key, 10)
        B, Q, KV = (1, 128, 6404)
        s = 1.0 / np.sqrt(HIDDEN)
        return {'hidden_states': jax.random.normal(ks[0], (B, Q, HIDDEN), jnp.float32), 'cross_attention_states': jax.random.normal(ks[1], (B, KV, HIDDEN), jnp.float32), 'attention_mask': jnp.zeros((B, 1, Q, KV), jnp.float32), 'q_proj_w': jax.random.normal(ks[2], (NUM_HEADS * HEAD_DIM, HIDDEN), jnp.float32) * s, 'k_proj_w': jax.random.normal(ks[3], (NUM_KV_HEADS * HEAD_DIM, HIDDEN), jnp.float32) * s, 'v_proj_w': jax.random.normal(ks[4], (NUM_KV_HEADS * HEAD_DIM, HIDDEN), jnp.float32) * s, 'o_proj_w': jax.random.normal(ks[5], (HIDDEN, NUM_HEADS * HEAD_DIM), jnp.float32) * s, 'q_norm_w': jnp.ones((HEAD_DIM,), jnp.float32), 'k_norm_w': jnp.ones((HEAD_DIM,), jnp.float32)}
    _L0_xattn_all = _L0_xattn_setup()
    _L0_xattn_in = {k: v for k, v in _L0_xattn_all.items() if k in ('q_proj_w', 'k_proj_w', 'v_proj_w', 'o_proj_w', 'q_norm_w', 'k_norm_w')}
    del _L0_xattn_all

    def _L0_ffn_setup():
        import jax, jax.numpy as jnp
        import numpy as np
        B, L, H, Dh, M = (4, 256, 16, 32, 128)
        D = H * Dh
        key = jax.random.key(seed)
        kx, ku, kd, kp = jax.random.split(key, 4)
        x = jax.random.normal(kx, (B, L, D), dtype=jnp.float32)
        up = jax.random.normal(ku, (H, Dh, M), dtype=jnp.float32)
        down = jax.random.normal(kd, (H, M, Dh), dtype=jnp.float32)
        perm = jax.random.permutation(kp, D)
        return {'x': x, 'up': up, 'down': down, 'perm': perm}
    _L0_ffn_all = _L0_ffn_setup()
    _L0_ffn_in = {k: v for k, v in _L0_ffn_all.items() if k in ('up', 'down', 'perm')}
    del _L0_ffn_all

    def _L1_xattn_setup():
        import jax, jax.numpy as jnp
        import numpy as np
        B, C, D = (8, 128, 512)
        GROUPS = 8
        ATTN_SCALE = 1.0
        RESID = 1.0
        EPS = 1e-05
        key = jax.random.key(seed)
        ks = jax.random.split(key, 9)
        s = 1.0 / np.sqrt(C)
        return {'inp_q': jax.random.normal(ks[0], (B, C, D), jnp.float32), 'inp_k': jax.random.normal(ks[1], (B, C, D), jnp.float32), 'inp_v': jax.random.normal(ks[2], (B, C, D), jnp.float32), 'Wt': jax.random.normal(ks[3], (C, C), jnp.float32) * s, 'Wp': jax.random.normal(ks[4], (C, C), jnp.float32) * s, 'Wg': jax.random.normal(ks[5], (C, C), jnp.float32) * s, 'Wz': jax.random.normal(ks[6], (C, C // GROUPS), jnp.float32) * s, 'gn_w': jax.random.normal(ks[7], (C,), jnp.float32), 'gn_b': jax.random.normal(ks[8], (C,), jnp.float32)}
    _L1_xattn_all = _L1_xattn_setup()
    _L1_xattn_in = {k: v for k, v in _L1_xattn_all.items() if k in ('Wt', 'Wp', 'Wg', 'Wz', 'gn_w', 'gn_b')}
    del _L1_xattn_all

    def _L1_ffn_setup():
        import jax, jax.numpy as jnp
        import numpy as np
        NUM_EXPERTS = 8
        D_IN = 512
        D_OUT = 512
        key = jax.random.key(seed)
        k_x, k_gw, k_gb, k_ew, k_eb = jax.random.split(key, 5)
        x = jax.random.normal(k_x, (4, 256, D_IN), dtype=jnp.float32)
        gate_w = jax.random.normal(k_gw, (NUM_EXPERTS, D_IN), dtype=jnp.float32) * 0.02
        gate_b = jax.random.normal(k_gb, (NUM_EXPERTS,), dtype=jnp.float32) * 0.02
        expert_w = jax.random.normal(k_ew, (NUM_EXPERTS, D_OUT, D_IN), dtype=jnp.float32) * 0.02
        expert_b = jax.random.normal(k_eb, (NUM_EXPERTS, D_OUT), dtype=jnp.float32) * 0.02
        return {'x': x, 'gate_w': gate_w, 'gate_b': gate_b, 'expert_w': expert_w, 'expert_b': expert_b}
    _L1_ffn_all = _L1_ffn_setup()
    _L1_ffn_in = {k: v for k, v in _L1_ffn_all.items() if k in ('gate_w', 'gate_b', 'expert_w', 'expert_b')}
    del _L1_ffn_all
    return {'x': x, 'ctx_4096': ctx_4096, 'mask_1x1xSxS2_ff0': mask_1x1xSxS2_ff0, 'g_xattn': g_xattn, 'g_ffn': g_ffn, 'L0_xattn_q_proj_w': _L0_xattn_in['q_proj_w'], 'L0_xattn_k_proj_w': _L0_xattn_in['k_proj_w'], 'L0_xattn_v_proj_w': _L0_xattn_in['v_proj_w'], 'L0_xattn_o_proj_w': _L0_xattn_in['o_proj_w'], 'L0_xattn_q_norm_w': _L0_xattn_in['q_norm_w'], 'L0_xattn_k_norm_w': _L0_xattn_in['k_norm_w'], 'L0_ffn_up': _L0_ffn_in['up'], 'L0_ffn_down': _L0_ffn_in['down'], 'L0_ffn_perm': _L0_ffn_in['perm'], 'L1_xattn_Wt': _L1_xattn_in['Wt'], 'L1_xattn_Wp': _L1_xattn_in['Wp'], 'L1_xattn_Wg': _L1_xattn_in['Wg'], 'L1_xattn_Wz': _L1_xattn_in['Wz'], 'L1_xattn_gn_w': _L1_xattn_in['gn_w'], 'L1_xattn_gn_b': _L1_xattn_in['gn_b'], 'L1_ffn_gate_w': _L1_ffn_in['gate_w'], 'L1_ffn_gate_b': _L1_ffn_in['gate_b'], 'L1_ffn_expert_w': _L1_ffn_in['expert_w'], 'L1_ffn_expert_b': _L1_ffn_in['expert_b']}

def reference(x, ctx_4096, mask_1x1xSxS2_ff0, g_xattn, g_ffn, L0_xattn_q_proj_w, L0_xattn_k_proj_w, L0_xattn_v_proj_w, L0_xattn_o_proj_w, L0_xattn_q_norm_w, L0_xattn_k_norm_w, L0_ffn_up, L0_ffn_down, L0_ffn_perm, L1_xattn_Wt, L1_xattn_Wp, L1_xattn_Wg, L1_xattn_Wz, L1_xattn_gn_w, L1_xattn_gn_b, L1_ffn_gate_w, L1_ffn_gate_b, L1_ffn_expert_w, L1_ffn_expert_b):
    import jax
    import jax.numpy as jnp

    def _L0_xattn_ref(hidden_states, cross_attention_states, attention_mask, q_proj_w, k_proj_w, v_proj_w, o_proj_w, q_norm_w, k_norm_w):
        import jax, jax.numpy as jnp
        import numpy as np
        NUM_HEADS = 32
        NUM_KV_HEADS = 8
        HEAD_DIM = 128
        HIDDEN = 512
        EPS = 1e-05

        def rmsnorm(x, w, eps=EPS):
            xf = x.astype(jnp.float32)
            var = jnp.mean(xf * xf, axis=-1, keepdims=True)
            return w * (xf * jax.lax.rsqrt(var + eps)).astype(x.dtype)
        B, Q, _ = hidden_states.shape
        KV = cross_attention_states.shape[1]
        n_rep = NUM_HEADS // NUM_KV_HEADS
        q = (hidden_states @ q_proj_w.T).reshape(B, Q, NUM_HEADS, HEAD_DIM).transpose(0, 2, 1, 3)
        k = (cross_attention_states @ k_proj_w.T).reshape(B, KV, NUM_KV_HEADS, HEAD_DIM).transpose(0, 2, 1, 3)
        v = (cross_attention_states @ v_proj_w.T).reshape(B, KV, NUM_KV_HEADS, HEAD_DIM).transpose(0, 2, 1, 3)
        q = rmsnorm(q, q_norm_w)
        k = jnp.repeat(k, n_rep, axis=1)
        v = jnp.repeat(v, n_rep, axis=1)
        k = rmsnorm(k, k_norm_w)
        scale = 1.0 / np.sqrt(HEAD_DIM)
        scores = jnp.einsum('bhqd,bhkd->bhqk', q, k) * scale + attention_mask
        attn = jax.nn.softmax(scores.astype(jnp.float32), axis=-1).astype(q.dtype)
        out = jnp.einsum('bhqk,bhkd->bhqd', attn, v)
        out = out.transpose(0, 2, 1, 3).reshape(B, Q, NUM_HEADS * HEAD_DIM)
        return out @ o_proj_w.T

    def _L0_ffn_ref(x, up, down, perm):
        import jax, jax.numpy as jnp
        import numpy as np
        B, L, H, Dh, M = (4, 256, 16, 32, 128)
        D = H * Dh
        b, l, Dm = x.shape
        h, d = (up.shape[0], up.shape[1])
        unperm = jnp.argsort(perm)
        t = x.reshape(b * l, Dm)
        t = t[:, perm]
        t = t.reshape(b * l, h, d)
        t = jnp.einsum('bhd,hdm->bhm', t, up)
        t = jax.nn.gelu(t, approximate=False)
        t = jnp.einsum('bhm,hmd->bhd', t, down)
        t = t.reshape(b * l, h * d)
        t = t[:, unperm]
        out = t.reshape(b, l, Dm)
        return out

    def _L1_xattn_ref(inp_q, inp_k, inp_v, Wt, Wp, Wg, Wz, gn_w, gn_b):
        import jax, jax.numpy as jnp
        import numpy as np
        B, C, D = (8, 128, 512)
        GROUPS = 8
        ATTN_SCALE = 1.0
        RESID = 1.0
        EPS = 1e-05
        residual = inp_v * RESID
        t = jnp.einsum('oc,bcd->bod', Wt, inp_v)
        p = jnp.einsum('oc,bcd->bod', Wp, inp_q)
        g = jnp.einsum('oc,bcd->bod', Wg, inp_k)
        b, c, d = t.shape
        cg = c // GROUPS
        tg = t.reshape(b, GROUPS, cg * d)
        pg = p.reshape(b, GROUPS, cg * d)
        gg = g.reshape(b, GROUPS, cg * d)
        att = jnp.sum(pg * gg, axis=-1, keepdims=True) * ATTN_SCALE
        x = (att * tg).reshape(b, c, d)
        xg = x.reshape(b, GROUPS, cg, d)
        Wzg = Wz.reshape(GROUPS, cg, cg)
        y = jnp.einsum('goi,bgid->bgod', Wzg, xg).reshape(b, c, d)
        yg = y.reshape(b, GROUPS, cg * d)
        mu = jnp.mean(yg, axis=-1, keepdims=True)
        var = jnp.var(yg, axis=-1, keepdims=True)
        yn = ((yg - mu) * jax.lax.rsqrt(var + EPS)).reshape(b, c, d)
        return yn * gn_w[None, :, None] + gn_b[None, :, None] + residual

    def _L1_ffn_ref(x, gate_w, gate_b, expert_w, expert_b):
        import jax, jax.numpy as jnp
        import numpy as np
        NUM_EXPERTS = 8
        D_IN = 512
        D_OUT = 512
        orig_shape = x.shape
        xf = x.reshape(-1, x.shape[-1])
        gate_logits = xf @ gate_w.T + gate_b
        gates = jax.nn.softmax(gate_logits, axis=-1)
        selected = jnp.argmax(gates, axis=-1)
        out = jnp.zeros((xf.shape[0], expert_w.shape[1]), dtype=xf.dtype)
        for j in range(expert_w.shape[0]):
            yj = xf @ expert_w[j].T + expert_b[j]
            out = out + jnp.where((selected == j)[:, None], yj, 0.0)
        return out.reshape(*orig_shape[:-1], expert_w.shape[1])
    x = x + jnp.tanh(g_xattn[0]) * _L0_xattn_ref(_layernorm(x, axis=-1), ctx_4096, mask_1x1xSxS2_ff0, L0_xattn_q_proj_w, L0_xattn_k_proj_w, L0_xattn_v_proj_w, L0_xattn_o_proj_w, L0_xattn_q_norm_w, L0_xattn_k_norm_w)
    x = x + jnp.tanh(g_ffn[0]) * _L0_ffn_ref(_layernorm(x, axis=-1), L0_ffn_up, L0_ffn_down, L0_ffn_perm)
    x = x + jnp.tanh(g_xattn[1]) * _L1_xattn_ref(_layernorm(x, axis=-1), ctx_4096, ctx_4096, L1_xattn_Wt, L1_xattn_Wp, L1_xattn_Wg, L1_xattn_Wz, L1_xattn_gn_w, L1_xattn_gn_b)
    x = x + jnp.tanh(g_ffn[1]) * _L1_ffn_ref(_layernorm(x, axis=-1), L1_ffn_gate_w, L1_ffn_gate_b, L1_ffn_expert_w, L1_ffn_expert_b)
    return x

_drawn_inputs = setup_inputs


def setup_inputs(seed=0):
    import zlib

    import numpy as np

    out = dict(_drawn_inputs(seed))
    spreads = {'g_ffn': (-1.0, 0.6), 'L0_xattn_q_norm_w': (1.0, 0.2), 'L0_xattn_k_norm_w': (1.0, 0.2)}
    factors = {'L1_ffn_gate_w': 5.518,
     'L1_ffn_gate_b': 32.116,
     'L1_ffn_expert_w': 5.19,
     'L1_ffn_expert_b': 64.0}
    for name, (base, spread) in spreads.items():
        noise = np.random.default_rng([zlib.crc32(name.encode()), seed]).standard_normal(out[name].shape)
        drawn = base * np.exp(spread * noise) if base else spread * noise
        out[name] = jnp.asarray(drawn.astype(out[name].dtype))
    for name, factor in factors.items():
        out[name] = (out[name] * factor).astype(out[name].dtype)
    return out
```

```python
from contextlib import ExitStack

import concourse.bass as bass
from concourse import mybir

F32 = mybir.dt.float32
F32R = mybir.dt.float32r
I32 = mybir.dt.int32
ALU = mybir.AluOpType
ACT = mybir.ActivationFunctionType
LN_EXP_SET = "natural_log_exp_and_others"
AX_X = mybir.AxisListType.X

P = 128
B = 8
D = 512
KT = D // P
T = B * P
HG = 4
G = 8
UNITS = G * B
E = 8
FH = 16
FD = D // FH
HALF = 512
EPS = 1e-5


def reached(eng, sem, value):
    if not (isinstance(value, int) and value <= 0):
        eng.wait_ge(sem, value)


def per_block(col, n):
    return col.unsqueeze(2).to_broadcast([P, col.shape[1], n])


def blocks(ap, k=HG):
    return ap.rearrange("p (k n) -> p k n", k=k)


def newton_rsqrt(eng, sem, count, half, seed, tmp, out, three_halves):
    eng.tensor_tensor(tmp, seed, seed, ALU.mult).then_inc(sem, 1)
    eng.wait_ge(sem, count + 1)
    eng.tensor_tensor(tmp, tmp, half, ALU.mult).then_inc(sem, 1)
    eng.wait_ge(sem, count + 2)
    eng.tensor_tensor(tmp, three_halves[:, 0:tmp.shape[1]], tmp, ALU.subtract).then_inc(sem, 1)
    eng.wait_ge(sem, count + 3)
    return eng.tensor_tensor(out, seed, tmp, ALU.mult)


class Mem:

    def __init__(self, nc, ctx):
        self.nc, self.ctx, self.sems = nc, ctx, []

    def sb(self, name, shape, dt=F32):
        return self.ctx.enter_context(self.nc.sbuf_tensor(name, shape, dt))

    def sem(self, name):
        self.sems.append(self.nc.alloc_semaphore(name))
        return self.sems[-1]

    def clear_sems(self):
        self.nc.clear_and_free_semaphores(self.sems)
        self.nc.all_engine_barrier()


def project_kv(nc, d, s):
    with ExitStack() as ctx:
        m = Mem(nc, ctx)
        ctx_raw = m.sb("ctx_raw", [P, KT, T])
        ctx_hi = m.sb("ctx_hi", [P, KT, T], F32R)
        ctx_lo = m.sb("ctx_lo", [P, KT, T], F32R)
        w_raw = m.sb("kvw_raw", [P, 2, KT, D])
        w_hi = m.sb("kvw_hi", [P, 2, KT, D], F32R)
        w_lo = m.sb("kvw_lo", [P, 2, KT, D], F32R)
        xln = m.sb("xln1", [P, 2, D])
        junk = m.sb("kv_junk", [P, D])
        k_sb = m.sb("k_sb", [P, 2, D])
        kT_st = m.sb("kT_st", [P, 2, D])
        v_st = m.sb("v_st", [P, 3, D])
        qw = m.sb("qw", [P, 1])
        kw = m.sb("kw", [P, 1])
        qkw = m.sb("qkw", [P, 1])
        ss = m.sb("k_ss", [P, 2, HG])
        lnss = m.sb("k_lnss", [P, 2, HG])
        seed = m.sb("k_seed", [P, 2, HG])
        val = m.sb("k_val", [P, 2, HG])
        tmp = m.sb("k_tmp", [P, 2, HG])
        rstd = m.sb("k_rstd", [P, 2, HG])
        bn = m.sb("bn1", [P, B, 6])
        mv = m.sb("mv1", [P, B, 2])
        xval = m.sb("xval1", [P, B])
        xseed = m.sb("xseed1", [P, B])
        xtmp = m.sb("xtmp1", [P, B])
        xrstd = m.sb("xrstd1", [P, B])

        ctx_ld = [m.sem(f"ctx_ld{i}") for i in range(2)]
        w_ld = [m.sem(f"kvw_ld{i}") for i in range(2)]
        x_ld = m.sem("x_ld")
        small_ld = m.sem("small_ld")
        gates_ready = m.sem("gates_ready")
        ctx_hi_done, ctx_lo_done = m.sem("ctx_hi_done"), m.sem("ctx_lo_done")
        w_hi_done, w_lo_done = m.sem("kvw_hi_done"), m.sem("kvw_lo_done")
        kv_done = m.sem("kv_done")
        kv_free = m.sem("kv_free")
        k_scaled = m.sem("k_scaled")
        v_copied = m.sem("v_copied")
        sumsq_done, ln_done, seed_done = m.sem("k_sumsq"), m.sem("k_ln"), m.sem("k_seeded")
        newton, rstd_done = m.sem("k_newton"), m.sem("k_rstd_done")
        kT_done, kT_copied = m.sem("kT_done"), m.sem("kT_copied")
        kT_stored = [m.sem(f"kT_stored{i}") for i in range(2)]
        v_stored = [m.sem(f"v_stored{i}") for i in range(3)]
        stats_step, qkw_done = m.sem("stats1_step"), m.sem("qkw_done")
        xval_done, xln_ln, xseed_done = m.sem("xval1_done"), m.sem("xln1_ln"), m.sem("xseed1_done")
        xrstd_done, xln_done = m.sem("xrstd1_done"), m.sem("xln1_done")
        xT_done, xT_hi_done, xT_lo_done = m.sem("xT1_done"), m.sem("xT1_hi_done"), m.sem("xT1_lo_done")
        kv_ps = s.ps[0:3]
        kT_ps = s.ps[3:5]
        xT_ps = s.ps[5:7]
        NU = 4 * B
        NK = 2 * B
        XT0 = NK + 2

        stage = ExitStack()
        block = stage.enter_context(nc.Block())

        @block.sync
        def _(sp):
            for c in range(2):
                sp.dma_start(ctx_raw[:, :, c * HALF:(c + 1) * HALF], d.ctxT[:, :, c * HALF:(c + 1) * HALF])\
                    .then_inc(ctx_ld[c], 16)
                sp.dma_start(w_raw[:, c, :, :], d.kv_w[c]).then_inc(w_ld[c], 16)
                if c == 0:
                    for dst, src in ((s.ident[:, :], d.ident), (qw[:, :], d.qw), (kw[:, :], d.kw),
                                     (s.gates[:, 0:2], d.g_xattn), (s.gates[:, 2:4], d.g_ffn)):
                        sp.dma_start(dst, src).then_inc(small_ld, 16)
            sp.dma_start(s.x[:, :, :], d.x).then_inc(x_ld, 16)
            for i in range(NU):
                w, b = divmod(i, B)
                if i in (0, B - 2):
                    n = 2 if i == 0 else 3
                    sp.wait_ge(w_hi_done, KT * (n - 1))
                    sp.wait_ge(w_lo_done, KT * (n - 1))
                    sp.dma_start(w_raw[:, n % 2, :, :], d.kv_w[n]).then_inc(w_ld[n % 2], 16)
                if i < NK:
                    sp.wait_ge(kT_copied, i + 1)
                    sp.dma_start(d.kT_scr[4 * w:4 * w + 4, :, b * P:(b + 1) * P].rearrange("g d t -> d g t"),
                                 blocks(kT_st[:, i % 2, :])).then_inc(kT_stored[i % 2], 16)
                else:
                    sp.wait_ge(v_copied, i - NK + 1)
                    sp.dma_start(d.v_scr[4 * (w - 2):4 * (w - 2) + 4, :, b, :].rearrange("g t d -> t g d"),
                                 blocks(v_st[:, i % 3, :])).then_inc(v_stored[i % 3], 16)
            for q in range(2):
                sp.wait_ge(kT_stored[q], 16 * (NK // 2))
            for q in range(3):
                sp.wait_ge(v_stored[q], 16 * len([i for i in range(NK, NU) if i % 3 == q]))

        @block.scalar
        def _(act):
            act.wait_ge(small_ld, 16 * 5)
            act.activation(s.tgates[:, :], s.gates[:, :], ACT.Tanh).then_inc(gates_ready, 1)
            act.preload_act_table_set(LN_EXP_SET)
            act.wait_ge(ctx_ld[0], 16)
            act.activation(ctx_hi[:, :, 0:HALF], ctx_raw[:, :, 0:HALF], ACT.Copy).then_inc(ctx_hi_done, 1)
            act.wait_ge(ctx_ld[1], 16)
            act.activation(ctx_hi[:, :, HALF:T], ctx_raw[:, :, HALF:T], ACT.Copy).then_inc(ctx_hi_done, 1)
            for i in range(NU):
                if i < NK:
                    act.wait_ge(kv_done, i + 1)
                    if i == 0:
                        act.wait_ge(s.eps_set, 1)
                    reached(act, rstd_done, i - 1)
                    reached(act, sumsq_done, i)
                    for h in range(HG):
                        last = act.activation(junk[:, h * P:(h + 1) * P], kv_ps[i % 3][:, h * P:(h + 1) * P],
                                              ACT.Square, accum_out=ss[:, i % 2, h:h + 1])
                    last.then_inc(sumsq_done, 1)
                    act.wait_ge(sumsq_done, i + 1)
                    act.activation(lnss[:, i % 2, :], ss[:, i % 2, :], ACT.Ln, bias=s.eps[:, 0:1], scale=1.0 / P)\
                        .then_inc(ln_done, 1)
                    act.wait_ge(ln_done, i + 1)
                    act.activation(seed[:, i % 2, :], lnss[:, i % 2, :], ACT.Exp, scale=-0.5).then_inc(seed_done, 1)
                else:
                    n = i - NK
                    act.wait_ge(kv_done, i + 1)
                    if n >= 3:
                        act.wait_ge(v_stored[i % 3], 16 * (n // 3))
                    act.activation(v_st[:, i % 3, :], kv_ps[i % 3][:, :], ACT.Copy).then_inc(v_copied, 1)
                if i == NK - 1:
                    act.wait_ge(xval_done, 1)
                    act.activation(xtmp[:, :], xval[:, :], ACT.Ln, scale=2.0).then_inc(xln_ln, 1)
                    act.wait_ge(xln_ln, 1)
                    act.activation(xseed[:, :], xtmp[:, :], ACT.Exp, scale=-0.5).then_inc(xseed_done, 1)
                if XT0 <= i < XT0 + B:
                    b = i - XT0
                    act.wait_ge(xT_done, b + 1)
                    act.activation(s.xT_hi[:, :, b * P:(b + 1) * P], blocks(xT_ps[b % 2][:, :]), ACT.Copy)\
                        .then_inc(xT_hi_done, 1)

        @block.gpsimd
        def _(pool):
            pool.memset(s.c15[:, :], 1.5).then_inc(s.c15_set, 1)
            pool.wait_ge(s.c15_set, 1)
            for i in range(NK):
                pool.wait_ge(sumsq_done, i + 1)
                reached(pool, rstd_done, i)
                pool.tensor_scalar(val[:, i % 2, :], ss[:, i % 2, :], 0.5 / P, 0.5 * EPS, ALU.mult, ALU.add)\
                    .then_inc(newton, 1)
                pool.wait_ge(seed_done, i + 1)
                pool.wait_ge(newton, 4 * i + 1)
                reached(pool, k_scaled, i - 1)
                newton_rsqrt(pool, newton, 4 * i + 1, val[:, i % 2, :], seed[:, i % 2, :], tmp[:, i % 2, :],
                             rstd[:, i % 2, :], s.c15).then_inc(rstd_done, 1)
            pool.wait_ge(xseed_done, 1)
            newton_rsqrt(pool, newton, 4 * NK, xval[:, :], xseed[:, :], xtmp[:, :], xrstd[:, :], s.c15)\
                .then_inc(xrstd_done, 1)

        @block.vector
        def _(dve):
            dve.memset(s.eps[:, :], EPS).then_inc(s.eps_set, 1)

            def split_w(w, kts):
                for kt in kts:
                    dve.wait_ge(w_ld[w % 2], 16 * (w // 2 + 1))
                    if w >= 2:
                        dve.wait_ge(kv_done, B * (w - 1))
                    dve.tensor_copy(w_hi[:, w % 2, kt, :], w_raw[:, w % 2, kt, :]).then_inc(w_hi_done, 1)
                    dve.wait_ge(w_hi_done, KT * w + kt + 1)
                    dve.tensor_tensor(w_lo[:, w % 2, kt, :], w_raw[:, w % 2, kt, :],
                                      w_hi[:, w % 2, kt, :].bitcast(F32), ALU.subtract).then_inc(w_lo_done, 1)

            dve.wait_ge(ctx_hi_done, 1)
            dve.tensor_tensor(ctx_lo[:, :, 0:HALF], ctx_raw[:, :, 0:HALF], ctx_hi[:, :, 0:HALF].bitcast(F32),
                              ALU.subtract).then_inc(ctx_lo_done, 1)
            split_w(0, range(KT))
            dve.wait_ge(small_ld, 16 * 5)
            dve.tensor_tensor(qkw[:, :], qw[:, :], kw[:, :], ALU.mult).then_inc(qkw_done, 1)
            dve.wait_ge(ctx_hi_done, 2)
            dve.tensor_tensor(ctx_lo[:, :, HALF:T], ctx_raw[:, :, HALF:T], ctx_hi[:, :, HALF:T].bitcast(F32),
                              ALU.subtract).then_inc(ctx_lo_done, 1)
            dve.wait_ge(x_ld, 16)
            dve.wait_ge(qkw_done, 1)
            for i in range(NU):
                w, b = divmod(i, B)
                if i < NK:
                    dve.wait_ge(rstd_done, i + 1)
                    dve.wait_ge(kv_done, i + 1)
                    reached(dve, kT_done, i - 1)
                    dve.tensor_tensor(blocks(k_sb[:, i % 2, :]), blocks(kv_ps[i % 3][:, :]),
                                      per_block(rstd[:, i % 2, :], P), ALU.mult).then_inc(k_scaled, 1)
                if w < 3 and 1 <= b <= KT:
                    split_w(w + 1, [b - 1])
                if 1 <= i <= NK:
                    n = i - 1
                    dve.wait_ge(kT_done, n + 1)
                    if n >= 2:
                        dve.wait_ge(kT_stored[n % 2], 16 * (n // 2))
                    dve.tensor_scalar(kT_st[:, n % 2, :], kT_ps[n % 2][:, :], qkw[:, 0:1], None, ALU.mult)\
                        .then_inc(kT_copied, 1)
                if i < B:
                    dve.bn_stats(bn[:, i, :], s.x[:, i, :]).then_inc(stats_step, 1)
                    dve.wait_ge(stats_step, 2 * i + 1)
                    dve.bn_aggr(mv[:, i, :], bn[:, i, :]).then_inc(stats_step, 1)
                if i == B:
                    dve.wait_ge(stats_step, 2 * B)
                    dve.tensor_scalar(xval[:, :], mv[:, :, 1], EPS, 0.5, ALU.add, ALU.mult).then_inc(xval_done, 1)
                if XT0 - 1 <= i < XT0 - 1 + B:
                    n = i - XT0 + 1
                    dve.wait_ge(xrstd_done, 1)
                    reached(dve, xT_done, n - 1)
                    dve.tensor_scalar(xln[:, n % 2, :], s.x[:, n, :], mv[:, n, 0:1], xrstd[:, n:n + 1],
                                      ALU.subtract, ALU.mult).then_inc(xln_done, 1)
                if XT0 <= i < XT0 + B:
                    n = i - XT0
                    dve.wait_ge(xT_hi_done, n + 1)
                    dve.tensor_tensor(s.xT_lo[:, :, n * P:(n + 1) * P], blocks(xT_ps[n % 2][:, :]),
                                      s.xT_hi[:, :, n * P:(n + 1) * P].bitcast(F32), ALU.subtract)\
                        .then_inc(xT_lo_done, 1)

        @block.tensor
        def _(pe):
            for i in range(NU):
                w, b = divmod(i, B)
                if b in (0, B // 2):
                    pe.wait_ge(ctx_lo_done, 2 if w or b else 1)
                    pe.wait_ge(ctx_hi_done, 2 if w or b else 1)
                if i >= 3:
                    if i - 3 < NK:
                        pe.wait_ge(k_scaled, i - 2)
                    else:
                        pe.wait_ge(v_copied, i - 2 - NK)
                tok = slice(b * P, (b + 1) * P)
                for kt in range(KT):
                    if b == 0:
                        pe.wait_ge(w_lo_done, KT * w + kt + 1)
                    hi, lo = w_hi[:, w % 2, kt, :], w_lo[:, w % 2, kt, :]
                    pe.matmul(kv_ps[i % 3][:, :], ctx_hi[:, kt, tok], hi, start=(kt == 0), stop=False)
                    pe.matmul(kv_ps[i % 3][:, :], ctx_lo[:, kt, tok], hi, start=False, stop=False)
                    last = pe.matmul(kv_ps[i % 3][:, :], ctx_hi[:, kt, tok], lo, start=False, stop=(kt == KT - 1))
                last.then_inc(kv_done, 1)
                if 2 <= i < NK + 2:
                    n = i - 2
                    if n == 0:
                        pe.wait_ge(small_ld, 16 * 5)
                    pe.wait_ge(k_scaled, n + 1)
                    reached(pe, kT_copied, n - 1)
                    for h in range(HG):
                        last = pe.transpose(kT_ps[n % 2][:, h * P:(h + 1) * P], k_sb[:, n % 2, h * P:(h + 1) * P],
                                            s.ident[:, :])
                    last.then_inc(kT_done, 1)
                if XT0 <= i < XT0 + B:
                    n = i - XT0
                    pe.wait_ge(xln_done, n + 1)
                    reached(pe, xT_lo_done, n - 1)
                    for kt in range(KT):
                        last = pe.transpose(xT_ps[n % 2][:, kt * P:(kt + 1) * P], xln[:, n % 2, kt * P:(kt + 1) * P],
                                            s.ident[:, :])
                    last.then_inc(xT_done, 1)

        stage.close()
        m.clear_sems()


def attention(nc, d, s):
    with ExitStack() as ctx:
        m = Mem(nc, ctx)
        wq_raw = m.sb("wq_raw", [P, KT, D])
        wq_hi = m.sb("wq_hi", [P, KT, D], F32R)
        wq_lo = m.sb("wq_lo", [P, KT, D], F32R)
        wo_raw = m.sb("wo_raw", [P, HG, D])
        wo_hi = m.sb("wo_hi", [P, HG, D], F32R)
        wo_lo = m.sb("wo_lo", [P, HG, D], F32R)
        kT = m.sb("kT", [P, T])
        v_raw = m.sb("v_raw", [P, B, P])
        v_hi = m.sb("v_hi", [P, B, P], F32R)
        v_lo = m.sb("v_lo", [P, B, P], F32R)
        mask = m.sb("mask", [P, P])
        junk = m.sb("q_junk", [P, D])
        q_sb = m.sb("q_sb", [P, 2, D])
        qT_sb = m.sb("qT_sb", [P, 2, D])
        p_sb = m.sb("p_sb", [P, 2, D])
        pT_hi = m.sb("pT_hi", [P, D], F32R)
        pT_lo = m.sb("pT_lo", [P, D], F32R)
        oT_hi = m.sb("oT_hi", [P, D], F32R)
        oT_lo = m.sb("oT_lo", [P, D], F32R)
        ss = m.sb("q_ss", [P, 2, HG])
        lnss = m.sb("q_lnss", [P, 2, HG])
        seed = m.sb("q_seed", [P, 2, HG])
        val = m.sb("q_val", [P, 2, HG])
        tmp = m.sb("q_tmp", [P, 2, HG])
        rstd = m.sb("q_rstd", [P, 2, HG])
        nmax = m.sb("nmax", [P, 2, HG])
        psum_ = m.sb("prob_sum", [P, 2, HG])
        rsum = m.sb("rsum", [P, 2, HG])
        qeps = m.sb("qeps", [P, 1])

        mask_ld = m.sem("mask_ld")
        qeps_set = m.sem("qeps_set")
        wq_ld, wo_ld = m.sem("wq_ld"), m.sem("wo_ld")
        kT_ld = [m.sem(f"kT_ld{i}") for i in range(2)]
        v_ld = [m.sem(f"v_ld{i}") for i in range(2)]
        wq_hi_done, wq_lo_done = m.sem("wq_hi_done"), m.sem("wq_lo_done")
        wo_hi_done, wo_lo_done = m.sem("wo_hi_done"), m.sem("wo_lo_done")
        wq_used, wo_used = m.sem("wq_used"), m.sem("wo_used")
        v_hi_done, v_lo_done = m.sem("v_hi_done"), m.sem("v_lo_done")
        q_done, q_scaled = m.sem("q_done"), m.sem("q_scaled")
        sumsq_done, ln_done, seed_done = m.sem("q_sumsq"), m.sem("q_ln"), m.sem("q_seeded")
        newton, rstd_done = m.sem("q_newton"), m.sem("q_rstd_done")
        half_done = m.sem("q_half_done")
        qT_done, qT_copied = m.sem("qT_done"), m.sem("qT_copied")
        s_done, masked, max_done = m.sem("s_done"), m.sem("masked"), m.sem("max_done")
        exp_done, rsum_done, p_done = m.sem("exp_done"), m.sem("rsum_done"), m.sem("p_done")
        pT_done, pT_hi_done, pT_lo_done = m.sem("pT_done"), m.sem("pT_hi_done"), m.sem("pT_lo_done")
        pv_done, oT_hi_done, oT_lo_done = m.sem("pv_done"), m.sem("oT_hi_done"), m.sem("oT_lo_done")
        o_done, acc_done = m.sem("o_done"), m.sem("acc_done")

        q_ps, o_ps = s.ps[0:2], s.ps[2:4]
        qT_ps, s_ps, pT_ps, oT_ps = s.ps[4], s.ps[5], s.ps[6], s.ps[7]

        def run(eng, stages):

            def step(g, b):
                for stage, ahead in stages:
                    u = 8 * g + b + ahead
                    if not isinstance(u, int) or 0 <= u < UNITS:
                        stage(u, (b + ahead) % B, g + (b + ahead) // B)

            for b in range(2, B):
                step(-1, b)
            for b in range(B):
                step(0, b)
            with eng.Fori(1, G - 1) as g:
                for b in range(B):
                    step(g, b)
            for b in range(B):
                step(G - 1, b)
            for b in range(2):
                step(G, b)

        stage = ExitStack()
        block = stage.enter_context(nc.Block())

        @block.sync
        def _(sp):
            sp.dma_start(mask[:, :], d.mask).then_inc(mask_ld, 16)

            def loads(g):
                def v_half(c):
                    reached(sp, v_hi_done, 8 * g - 4 + 4 * c)
                    reached(sp, v_lo_done, 8 * g - 4 + 4 * c)
                    sp.dma_start(v_raw[:, 4 * c:4 * c + 4, :], d.v_scr[g, :, 4 * c:4 * c + 4, :])\
                        .then_inc(v_ld[c], 16)

                def kT_half(c):
                    reached(sp, s_done, 8 * g - 4 + 4 * c)
                    sp.dma_start(kT[:, c * HALF:(c + 1) * HALF], d.kT_scr[g, :, c * HALF:(c + 1) * HALF])\
                        .then_inc(kT_ld[c], 16)

                v_half(0)
                reached(sp, wq_hi_done, 4 * g)
                reached(sp, wq_lo_done, 4 * g)
                sp.dma_start(wq_raw[:, :, :], d.wq[g, :, :, :]).then_inc(wq_ld, 16)
                v_half(1)
                reached(sp, wo_hi_done, 4 * g)
                reached(sp, wo_lo_done, 4 * g)
                sp.dma_start(wo_raw[:, :, :], d.wo[g, :, :, :]).then_inc(wo_ld, 16)
                kT_half(0)
                kT_half(1)

            sp_first = 0
            for c in range(2):
                sp.dma_start(v_raw[:, 4 * c:4 * c + 4, :], d.v_scr[sp_first, :, 4 * c:4 * c + 4, :])\
                    .then_inc(v_ld[c], 16)
            sp.dma_start(wq_raw[:, :, :], d.wq[0, :, :, :]).then_inc(wq_ld, 16)
            for c in range(2):
                sp.dma_start(kT[:, c * HALF:(c + 1) * HALF], d.kT_scr[0, :, c * HALF:(c + 1) * HALF])\
                    .then_inc(kT_ld[c], 16)
            sp.dma_start(wo_raw[:, :, :], d.wo[0, :, :, :]).then_inc(wo_ld, 16)
            with sp.Fori(1, G) as g:
                loads(g)

        @block.scalar
        def _(act):
            act.wait_ge(qeps_set, 1)

            def oT_split(u, b, g):
                act.wait_ge(pv_done, u + 1)
                reached(act, o_done, u)
                act.activation(oT_hi[:, :], oT_ps[:, :], ACT.Copy).then_inc(oT_hi_done, 1)

            def exps(u, b, g):
                act.wait_ge(max_done, u + 1)
                for h in range(HG):
                    last = act.activation(p_sb[:, b % 2, h * P:(h + 1) * P], p_sb[:, b % 2, h * P:(h + 1) * P],
                                          ACT.Exp, bias=nmax[:, b % 2, h:h + 1],
                                          accum_out=psum_[:, b % 2, h:h + 1])
                last.then_inc(exp_done, 1)

            def qT_copy(u, b, g):
                act.wait_ge(qT_done, u + 1)
                reached(act, s_done, u - 1)
                act.activation(qT_sb[:, b % 2, :], qT_ps[:, :], ACT.Copy).then_inc(qT_copied, 1)

            def pT_split(u, b, g):
                act.wait_ge(pT_done, u + 1)
                reached(act, pv_done, u)
                act.activation(pT_hi[:, :], pT_ps[:, :], ACT.Copy).then_inc(pT_hi_done, 1)

            def wq_split(u, b, g):
                if b:
                    return
                act.wait_ge(wq_ld, 16 * g + 16)
                for kt in range(KT):
                    if kt < KT - 1:
                        reached(act, wq_used, 3 * g - 2 + kt if not isinstance(g, int) or g else 0)
                    else:
                        reached(act, q_done, 8 * g)
                    act.activation(wq_hi[:, kt, :], wq_raw[:, kt, :], ACT.Copy).then_inc(wq_hi_done, 1)

            def wo_split(u, b, g):
                if b:
                    return
                act.wait_ge(wo_ld, 16 * g + 16)
                for h in range(HG):
                    if h < HG - 1:
                        reached(act, wo_used, 3 * g - 2 + h if not isinstance(g, int) or g else 0)
                    else:
                        reached(act, o_done, 8 * g)
                    act.activation(wo_hi[:, h, :], wo_raw[:, h, :], ACT.Copy).then_inc(wo_hi_done, 1)

            def v_split(u, b, g):
                act.wait_ge(v_ld[b // 4], 16 * g + 16)
                reached(act, pv_done, u - 7)
                act.activation(v_hi[:, b, :], v_raw[:, b, :], ACT.Copy).then_inc(v_hi_done, 1)

            def q_stats(u, b, g):
                act.wait_ge(q_done, u + 1)
                reached(act, half_done, u - 1)
                reached(act, sumsq_done, u)
                for h in range(HG):
                    last = act.activation(junk[:, h * P:(h + 1) * P], q_ps[b % 2][:, h * P:(h + 1) * P],
                                          ACT.Square, accum_out=ss[:, b % 2, h:h + 1])
                last.then_inc(sumsq_done, 1)
                act.wait_ge(sumsq_done, u + 1)
                act.activation(lnss[:, b % 2, :], ss[:, b % 2, :], ACT.Ln, bias=qeps[:, 0:1]).then_inc(ln_done, 1)
                act.wait_ge(ln_done, u + 1)
                act.activation(seed[:, b % 2, :], lnss[:, b % 2, :], ACT.Exp, scale=-0.5).then_inc(seed_done, 1)

            run(act, [(oT_split, -2), (exps, 0), (qT_copy, 1), (pT_split, -1), (wq_split, 3), (v_split, 6),
                      (q_stats, 2), (wo_split, -1)])

        @block.gpsimd
        def _(pool):
            def v_split(u, b, g):
                pool.wait_ge(v_hi_done, u + 1)
                pool.tensor_tensor(v_lo[:, b, :], v_raw[:, b, :], v_hi[:, b, :].bitcast(F32), ALU.subtract)\
                    .then_inc(v_lo_done, 1)

            def normalize(u, b, g):
                pool.wait_ge(rsum_done, u + 1)
                pool.tensor_tensor(blocks(p_sb[:, b % 2, :]), blocks(p_sb[:, b % 2, :]),
                                   per_block(rsum[:, b % 2, :], P), ALU.mult).then_inc(p_done, 1)

            def wq_split(u, b, g):
                if b:
                    return
                for kt in range(KT):
                    pool.wait_ge(wq_hi_done, 4 * g + kt + 1)
                    pool.tensor_tensor(wq_lo[:, kt, :], wq_raw[:, kt, :], wq_hi[:, kt, :].bitcast(F32),
                                       ALU.subtract).then_inc(wq_lo_done, 1)

            def wo_split(u, b, g):
                if b:
                    return
                for h in range(HG):
                    pool.wait_ge(wo_hi_done, 4 * g + h + 1)
                    pool.tensor_tensor(wo_lo[:, h, :], wo_raw[:, h, :], wo_hi[:, h, :].bitcast(F32),
                                       ALU.subtract).then_inc(wo_lo_done, 1)

            def q_rstd(u, b, g):
                pool.wait_ge(half_done, u + 1)
                pool.wait_ge(seed_done, u + 1)
                reached(pool, rstd_done, u)
                reached(pool, q_scaled, u - 1)
                newton_rsqrt(pool, newton, 3 * u, val[:, b % 2, :], seed[:, b % 2, :], tmp[:, b % 2, :],
                             rstd[:, b % 2, :], s.c15).then_inc(rstd_done, 1)

            run(pool, [(v_split, 6), (normalize, 0), (wq_split, 3), (q_rstd, 2), (wo_split, -1)])

        @block.vector
        def _(dve):
            dve.memset(qeps[:, :], P * EPS).then_inc(qeps_set, 1)
            for b in range(B):
                dve.memset(s.acc[:, b, :], 0.0).then_inc(acc_done, 1)

            def oT_split(u, b, g):
                dve.wait_ge(oT_hi_done, u + 1)
                dve.tensor_tensor(oT_lo[:, :], oT_ps[:, :], oT_hi[:, :].bitcast(F32), ALU.subtract)\
                    .then_inc(oT_lo_done, 1)

            def mask_max(u, b, g):
                dve.wait_ge(s_done, u + 1)
                if isinstance(u, int) and u == 0:
                    dve.wait_ge(mask_ld, 16)
                reached(dve, pT_done, u - 1)
                dve.tensor_tensor(blocks(p_sb[:, b % 2, :]), blocks(s_ps[:, :]),
                                  mask[:, :].unsqueeze(1).to_broadcast([P, HG, P]), ALU.add).then_inc(masked, 1)
                dve.wait_ge(masked, u + 1)
                dve.tensor_reduce(nmax[:, b % 2, :], blocks(p_sb[:, b % 2, :]), axis=AX_X, op=ALU.max,
                                  negate=True).then_inc(max_done, 1)

            def q_half(u, b, g):
                dve.wait_ge(sumsq_done, u + 1)
                reached(dve, rstd_done, u - 1)
                dve.tensor_scalar(val[:, b % 2, :], ss[:, b % 2, :], 0.5, 0.5 * P * EPS, ALU.mult, ALU.add)\
                    .then_inc(half_done, 1)

            def q_scale(u, b, g):
                dve.wait_ge(rstd_done, u + 1)
                reached(dve, qT_done, u - 1)
                dve.tensor_tensor(blocks(q_sb[:, b % 2, :]), blocks(q_ps[b % 2][:, :]),
                                  per_block(rstd[:, b % 2, :], P), ALU.mult).then_inc(q_scaled, 1)

            def p_recip(u, b, g):
                dve.wait_ge(exp_done, u + 1)
                reached(dve, p_done, u - 1)
                dve.reciprocal(rsum[:, b % 2, :], psum_[:, b % 2, :]).then_inc(rsum_done, 1)

            def pT_split(u, b, g):
                dve.wait_ge(pT_hi_done, u + 1)
                dve.tensor_tensor(pT_lo[:, :], pT_ps[:, :], pT_hi[:, :].bitcast(F32), ALU.subtract)\
                    .then_inc(pT_lo_done, 1)

            def accumulate(u, b, g):
                dve.wait_ge(o_done, u + 1)
                dve.wait_ge(acc_done, u + 1)
                dve.tensor_tensor(s.acc[:, b, :], o_ps[b % 2][:, :], s.acc[:, b, :], ALU.add)\
                    .then_inc(acc_done, 1)

            run(dve, [(oT_split, -2), (mask_max, 0), (q_scale, 1), (p_recip, 0), (pT_split, -1),
                      (q_half, 2), (accumulate, -2)])

        @block.tensor
        def _(pe):
            def scores(u, b, g):
                pe.wait_ge(qT_copied, u + 1)
                if b % 4 == 0:
                    pe.wait_ge(kT_ld[b // 4], 16 * g + 16)
                reached(pe, masked, u)
                for h in range(HG):
                    last = pe.matmul(s_ps[:, h * P:(h + 1) * P], qT_sb[:, b % 2, h * P:(h + 1) * P],
                                     kT[:, b * P:(b + 1) * P], start=True, stop=True)
                last.then_inc(s_done, 1)

            def q_proj(u, b, g):
                reached(pe, q_scaled, u - 1)
                for kt in range(KT):
                    if b == 0:
                        pe.wait_ge(wq_lo_done, 4 * g + kt + 1)
                    xh, xl = s.xT_hi[:, kt, b * P:(b + 1) * P], s.xT_lo[:, kt, b * P:(b + 1) * P]
                    pe.matmul(q_ps[b % 2][:, :], xh, wq_hi[:, kt, :], start=(kt == 0), stop=False)
                    pe.matmul(q_ps[b % 2][:, :], xl, wq_hi[:, kt, :], start=False, stop=False)
                    last = pe.matmul(q_ps[b % 2][:, :], xh, wq_lo[:, kt, :], start=False, stop=(kt == KT - 1))
                    if b == B - 1 and kt < KT - 1:
                        last.then_inc(wq_used, 1)
                last.then_inc(q_done, 1)

            def q_transpose(u, b, g):
                pe.wait_ge(q_scaled, u + 1)
                reached(pe, qT_copied, u)
                for h in range(HG):
                    last = pe.transpose(qT_ps[:, h * P:(h + 1) * P], q_sb[:, b % 2, h * P:(h + 1) * P],
                                        s.ident[:, :])
                last.then_inc(qT_done, 1)

            def p_transpose(u, b, g):
                pe.wait_ge(p_done, u + 1)
                reached(pe, pT_lo_done, u)
                for h in range(HG):
                    last = pe.transpose(pT_ps[:, h * P:(h + 1) * P], p_sb[:, b % 2, h * P:(h + 1) * P],
                                        s.ident[:, :])
                last.then_inc(pT_done, 1)

            def o_proj(u, b, g):
                pe.wait_ge(oT_lo_done, u + 1)
                reached(pe, acc_done, B + u - 1)
                for h in range(HG):
                    if b == 0:
                        pe.wait_ge(wo_lo_done, 4 * g + h + 1)
                    oh, ol = oT_hi[:, h * P:(h + 1) * P], oT_lo[:, h * P:(h + 1) * P]
                    pe.matmul(o_ps[b % 2][:, :], oh, wo_hi[:, h, :], start=(h == 0), stop=False)
                    pe.matmul(o_ps[b % 2][:, :], ol, wo_hi[:, h, :], start=False, stop=False)
                    last = pe.matmul(o_ps[b % 2][:, :], oh, wo_lo[:, h, :], start=False, stop=(h == HG - 1))
                    if b == B - 1 and h < HG - 1:
                        last.then_inc(wo_used, 1)
                last.then_inc(o_done, 1)

            def values(u, b, g):
                pe.wait_ge(pT_lo_done, u + 1)
                pe.wait_ge(v_lo_done, u + 1)
                reached(pe, oT_lo_done, u)
                pe.matmul(oT_ps[:, :], v_hi[:, b, :], pT_hi[:, :], start=True, stop=False)
                pe.matmul(oT_ps[:, :], v_lo[:, b, :], pT_hi[:, :], start=False, stop=False)
                pe.matmul(oT_ps[:, :], v_hi[:, b, :], pT_lo[:, :], start=False, stop=True).then_inc(pv_done, 1)

            run(pe, [(scores, 0), (q_proj, 2), (q_transpose, 1), (p_transpose, -1), (o_proj, -2), (values, -1)])

        stage.close()
        m.clear_sems()


def layernorm_stats(dve, s, b, bn, mv, step, count):
    dve.bn_stats(bn[:, b, :], s.x[:, b, :]).then_inc(step, 1)
    dve.wait_ge(step, count + 1)
    return dve.bn_aggr(mv[:, b, :], bn[:, b, :])


def feed_forward(nc, d, s):
    with ExitStack() as ctx:
        m = Mem(nc, ctx)
        xln = m.sb("xln2", [P, B, D])
        bn = m.sb("bn2", [P, B, 6])
        mv = m.sb("mv2", [P, B, 2])
        xval, xseed = m.sb("xval2", [P, B]), m.sb("xseed2", [P, B])
        xtmp, xrstd = m.sb("xtmp2", [P, B]), m.sb("xrstd2", [P, B])
        perm_rowi, perm_coli = m.sb("perm_rowi", [P, D], I32), m.sb("perm_coli", [P, KT], I32)
        perm_row, perm_col = m.sb("perm_row", [P, D]), m.sb("perm_col", [P, KT])
        iota_row, iota_col = m.sb("iota_row", [P, D]), m.sb("iota_col", [P, KT])
        pick = m.sb("pick", [P, KT, D], F32R)
        pickT = m.sb("pickT", [P, KT, D], F32R)
        up_raw = m.sb("up_raw", [P, KT, P])
        up_hi, up_lo = m.sb("up_hi", [P, KT, P], F32R), m.sb("up_lo", [P, KT, P], F32R)
        down = m.sb("down", [P, D])
        xp_hi, xp_lo = m.sb("xp_hi", [P, KT, T], F32R), m.sb("xp_lo", [P, KT, T], F32R)
        hid = m.sb("hid", [P, 3, HALF])
        yT_hi, yT_lo = m.sb("yT_hi", [P, KT, T], F32R), m.sb("yT_lo", [P, KT, T], F32R)

        perm_ld, up_ld, down_ld = m.sem("perm_ld"), m.sem("up_ld"), m.sem("down_ld")
        ctx_ld = m.sem("ctx_nat_ld")
        x_step, xval_done = m.sem("x2_step"), m.sem("xval2_done")
        xln_ln, xseed_done, xrstd_done = m.sem("xln2_ln"), m.sem("xseed2_done"), m.sem("xrstd2_done")
        newton, xln_done = m.sem("newton2"), m.sem("xln2_done")
        xT_done, xT_hi_done, xT_lo_done = m.sem("xT2_done"), m.sem("xT2_hi_done"), m.sem("xT2_lo_done")
        pick_step, pick_done = m.sem("pick_step"), m.sem("pick_done")
        up_hi_done, up_lo_done = m.sem("up_hi_done"), m.sem("up_lo_done")
        xp_done, xp_copied = m.sem("xp_done"), [m.sem("xp_hi_copied"), m.sem("xp_lo_copied")]
        up_done, gelu_done, down_done = m.sem("up_done"), m.sem("gelu_done"), m.sem("down_done")
        yT_hi_done, yT_lo_done = m.sem("yT_hi_done"), m.sem("yT_lo_done")
        y_done, x_done = m.sem("y_done"), m.sem("x2_done")
        xT_ps, xp_ps, up_ps, yT_ps = s.ps[0:2], s.ps[2:4], s.ps[4:6], s.ps[6:8]
        y_ps = s.ps[0:2]
        HB = B // 2

        stage = ExitStack()
        block = stage.enter_context(nc.Block())

        @block.sync
        def _(sp):
            sp.dma_start(perm_rowi[:, :], d.perm_row).then_inc(perm_ld, 16)
            sp.dma_start(perm_coli[:, :], d.perm_col).then_inc(perm_ld, 16)
            sp.dma_start(iota_row[:, :], d.iota_row).then_inc(perm_ld, 16)
            sp.dma_start(iota_col[:, :], d.iota_col).then_inc(perm_ld, 16)
            sp.dma_start(up_raw[:, :, :], d.up).then_inc(up_ld, 16)
            sp.dma_start(down[:, :], d.down).then_inc(down_ld, 16)
            sp.dma_start(s.ctx_nat[:, :, :], d.ctx).then_inc(ctx_ld, 16)
            sp.wait_ge(ctx_ld, 16)

        @block.scalar
        def _(act):
            act.wait_ge(up_ld, 16)
            act.activation(up_hi[:, :, :], up_raw[:, :, :], ACT.Copy).then_inc(up_hi_done, 1)
            for c in range(2):
                cols = slice(c * HB, (c + 1) * HB)
                act.wait_ge(xval_done, c + 1)
                act.activation(xtmp[:, cols], xval[:, cols], ACT.Ln, scale=2.0).then_inc(xln_ln, 1)
                act.wait_ge(xln_ln, c + 1)
                act.activation(xseed[:, cols], xtmp[:, cols], ACT.Exp, scale=-0.5).then_inc(xseed_done, 1)
            for b in range(B):
                act.wait_ge(xT_done, b + 1)
                act.activation(s.xT_hi[:, :, b * P:(b + 1) * P], blocks(xT_ps[b % 2][:, :]), ACT.Copy)\
                    .then_inc(xT_hi_done, 1)
            for n in range(2 * KT):
                c, jt = divmod(n, KT)
                act.wait_ge(xp_done, 2 * n + 1)
                act.activation(xp_hi[:, jt, c * HALF:(c + 1) * HALF], xp_ps[0][:, :], ACT.Copy)\
                    .then_inc(xp_copied[0], 1)
            for n in range(2 * FH):
                act.wait_ge(up_done, n + 1)
                reached(act, down_done, n - 2)
                act.activation(hid[:, n % 3, :], up_ps[n % 2][:, :], ACT.Gelu).then_inc(gelu_done, 1)
                ready = [n // HG - 1] if n % HG == 0 and n % FH else []
                ready += [n // HG] if n % FH == FH - 1 else []
                for k in ready:
                    c, jt = divmod(k, KT)
                    act.wait_ge(down_done, HG * (k + 1))
                    act.activation(yT_hi[:, jt, c * HALF:(c + 1) * HALF], yT_ps[k % 2][:, :], ACT.Copy)\
                        .then_inc(yT_hi_done, 1)

        @block.gpsimd
        def _(pool):
            pool.wait_ge(perm_ld, 16 * 4)
            pool.tensor_copy(perm_row[:, :], perm_rowi[:, :]).then_inc(pick_step, 1)
            pool.tensor_copy(perm_col[:, :], perm_coli[:, :]).then_inc(pick_step, 1)
            pool.wait_ge(pick_step, 2)
            for kt in range(KT):
                pool.tensor_scalar(pick[:, kt, :], perm_row[:, :], iota_col[:, kt:kt + 1], None, ALU.is_equal)\
                    .then_inc(pick_done, 1)
            for c in range(2):
                cols = slice(c * HB, (c + 1) * HB)
                pool.wait_ge(xseed_done, c + 1)
                newton_rsqrt(pool, newton, 3 * c, xval[:, cols], xseed[:, cols], xtmp[:, cols], xrstd[:, cols],
                             s.c15)\
                    .then_inc(xrstd_done, 1)
            for jt in range(KT):
                pool.tensor_scalar(pickT[:, jt, :], iota_row[:, :], perm_col[:, jt:jt + 1], None, ALU.is_equal)\
                    .then_inc(pick_done, 1)

        @block.vector
        def _(dve):
            for c in range(2):
                for b in range(c * HB, (c + 1) * HB):
                    dve.scalar_tensor_tensor(out=s.x[:, b, :], in0=s.acc[:, b, :], scalar=s.tgates[:, 0:1],
                                             in1=s.x[:, b, :], op0=ALU.mult, op1=ALU.add).then_inc(x_step, 1)
                    dve.wait_ge(x_step, 3 * b + 1)
                    layernorm_stats(dve, s, b, bn, mv, x_step, 3 * b + 1).then_inc(x_step, 1)
                dve.wait_ge(x_step, 3 * HB * (c + 1))
                cols = slice(c * HB, (c + 1) * HB)
                dve.tensor_scalar(xval[:, cols], mv[:, cols, 1], EPS, 0.5, ALU.add, ALU.mult).then_inc(xval_done, 1)
            dve.wait_ge(up_hi_done, 1)
            dve.tensor_tensor(up_lo[:, :, :], up_raw[:, :, :], up_hi[:, :, :].bitcast(F32), ALU.subtract)\
                .then_inc(up_lo_done, 1)
            for b in range(B):
                dve.wait_ge(xrstd_done, b // HB + 1)
                dve.tensor_scalar(xln[:, b, :], s.x[:, b, :], mv[:, b, 0:1], xrstd[:, b:b + 1],
                                  ALU.subtract, ALU.mult).then_inc(xln_done, 1)
            for b in range(B):
                dve.wait_ge(xT_hi_done, b + 1)
                dve.tensor_tensor(s.xT_lo[:, :, b * P:(b + 1) * P], blocks(xT_ps[b % 2][:, :]),
                                  s.xT_hi[:, :, b * P:(b + 1) * P].bitcast(F32), ALU.subtract)\
                    .then_inc(xT_lo_done, 1)
            for n in range(2 * KT):
                c, jt = divmod(n, KT)
                dve.wait_ge(xp_done, 2 * n + 2)
                dve.tensor_copy(xp_lo[:, jt, c * HALF:(c + 1) * HALF], xp_ps[1][:, :]).then_inc(xp_copied[1], 1)
            for c in range(2):
                for jt in range(KT):
                    k = c * KT + jt
                    dve.wait_ge(yT_hi_done, k + 1)
                    dve.tensor_tensor(yT_lo[:, jt, c * HALF:(c + 1) * HALF], yT_ps[k % 2][:, :],
                                      yT_hi[:, jt, c * HALF:(c + 1) * HALF].bitcast(F32), ALU.subtract)\
                        .then_inc(yT_lo_done, 1)
                for b in range(c * HB, (c + 1) * HB):
                    dve.wait_ge(y_done, b + 1)
                    dve.scalar_tensor_tensor(out=s.x[:, b, :], in0=y_ps[b % 2][:, :], scalar=s.tgates[:, 2:3],
                                             in1=s.x[:, b, :], op0=ALU.mult, op1=ALU.add).then_inc(x_done, 1)

        @block.tensor
        def _(pe):
            for b in range(B):
                pe.wait_ge(xln_done, b + 1)
                reached(pe, xT_lo_done, b - 1)
                for kt in range(KT):
                    last = pe.transpose(xT_ps[b % 2][:, kt * P:(kt + 1) * P], xln[:, b, kt * P:(kt + 1) * P],
                                        s.ident[:, :])
                last.then_inc(xT_done, 1)
            pe.wait_ge(pick_done, KT)
            for n in range(2 * KT):
                c, jt = divmod(n, KT)
                pe.wait_ge(xT_lo_done, HB * (c + 1))
                for part, xT in enumerate((s.xT_hi, s.xT_lo)):
                    reached(pe, xp_copied[part], n)
                    for kt in range(KT):
                        last = pe.matmul(xp_ps[part][:, :], pick[:, kt, jt * P:(jt + 1) * P],
                                         xT[:, kt, c * HALF:(c + 1) * HALF], start=(kt == 0), stop=(kt == KT - 1))
                    last.then_inc(xp_done, 1)
            pe.wait_ge(up_lo_done, 1)
            pe.wait_ge(down_ld, 16)
            for c in range(2):
                half = slice(c * HALF, (c + 1) * HALF)
                for h in range(FH + 1):
                    if h < FH:
                        n, jt, rows = c * FH + h, h // HG, slice(FD * (h % HG), FD * (h % HG + 1))
                        pe.wait_ge(xp_copied[0], c * KT + jt + 1)
                        pe.wait_ge(xp_copied[1], c * KT + jt + 1)
                        reached(pe, gelu_done, n - 1)
                        out = up_ps[n % 2][:, :]
                        pe.matmul(out, up_hi[rows, jt, :], xp_hi[rows, jt, half], start=True, stop=False)
                        pe.matmul(out, up_lo[rows, jt, :], xp_hi[rows, jt, half], start=False, stop=False)
                        pe.matmul(out, up_hi[rows, jt, :], xp_lo[rows, jt, half], start=False, stop=True)\
                            .then_inc(up_done, 1)
                    if h >= 1:
                        hh = h - 1
                        n, k, rows = c * FH + hh, c * KT + hh // HG, slice(FD * (hh % HG), FD * (hh % HG + 1))
                        pe.wait_ge(gelu_done, n + 1)
                        if hh % HG == 0:
                            reached(pe, yT_lo_done, k - 1)
                        pe.matmul(yT_ps[k % 2][rows, :], down[:, hh * FD:(hh + 1) * FD], hid[:, n % 3, :],
                                  start=True, stop=True).then_inc(down_done, 1)
                pe.wait_ge(pick_done, 2 * KT)
                pe.wait_ge(yT_lo_done, KT * (c + 1))
                for b in range(c * HB, (c + 1) * HB):
                    reached(pe, x_done, b - 1)
                    for jt in range(KT):
                        pe.matmul(y_ps[b % 2][:, :], yT_hi[:, jt, b * P:(b + 1) * P], pickT[:, jt, :],
                                  start=(jt == 0), stop=False)
                        last = pe.matmul(y_ps[b % 2][:, :], yT_lo[:, jt, b * P:(b + 1) * P], pickT[:, jt, :],
                                         start=False, stop=(jt == KT - 1))
                    last.then_inc(y_done, 1)

        stage.close()


def nonlocal_attention(nc, d, s):
    with ExitStack() as ctx:
        m = Mem(nc, ctx)
        xln = m.sb("xln3", [P, B, D])
        bn, mv = m.sb("bn3", [P, B, 6]), m.sb("mv3", [P, B, 2])
        xval, xseed = m.sb("xval3", [P, B]), m.sb("xseed3", [P, B])
        xtmp, xrstd = m.sb("xtmp3", [P, B]), m.sb("xrstd3", [P, B])
        wt, wzT = m.sb("wt", [P, P]), m.sb("wzT", [P, P])
        wgT, wpT, mT = m.sb("wgT", [P, P]), m.sb("wpT", [P, P]), m.sb("mT", [P, P])
        group_mean = m.sb("group_mean", [P, P])
        gn_w, gn_b = m.sb("gn_w", [P, 1]), m.sb("gn_b", [P, 1])
        z = m.sb("z", [P, B, D])
        y = m.sb("y", [P, B, D])
        g_sb = m.sb("g_sb", [P, 2, D])
        prod = m.sb("prod", [P, 2, D])
        zbn, zmv = m.sb("zbn", [P, B, 6]), m.sb("zmv", [P, B, 2])
        row = m.sb("att_row", [P, B])
        gmean, dev, att = m.sb("gmean", [P, B]), m.sb("dev", [P, B]), m.sb("att", [P, B])
        gvar, yval = m.sb("gvar", [P, B]), m.sb("yval", [P, B])
        yln, yseed, ytmp, yrstd = (m.sb(n, [P, B]) for n in ("yln", "yseed", "ytmp", "yrstd"))
        a_col, b_col, tw, tb = m.sb("a_col", [P, B]), m.sb("b_col", [P, B]), m.sb("tw", [P, 1]), m.sb("tb", [P, 1])

        w_ld = m.sem("l1w_ld")
        x_step, xval_done = m.sem("x3_step"), m.sem("xval3_done")
        xln_ln, xseed_done, xrstd_done = m.sem("xln3_ln"), m.sem("xseed3_done"), m.sem("xrstd3_done")
        newton, xln_done = m.sem("newton3"), m.sem("xln3_done")
        mT_done, mT_copied = m.sem("mT_done"), m.sem("mT_copied")
        z_done, z_copied, g_done, g_copied = m.sem("z_done"), m.sem("z_copied"), m.sem("g_done"), m.sem("g_copied")
        p_done, row_done, zstat_step = m.sem("pp_done"), m.sem("row_done"), m.sem("zstat_step")
        gmean_done, dev_step, gvar_done = m.sem("gmean_done"), m.sem("dev_step"), m.sem("gvar_done")
        att_done, col_step, yval_done = m.sem("att_done"), m.sem("col_step"), m.sem("yval_done")
        yln_done, yseed_done, yrstd_done = m.sem("yln_done"), m.sem("yseed_done"), m.sem("yrstd_done")
        y_done, res_done, x_done = m.sem("yy_done"), m.sem("res_done"), m.sem("x3_done")
        z_ps, g_ps, p_ps, sm_ps, att_ps = s.ps[0:2], s.ps[2:4], s.ps[4:6], s.ps[6], s.ps[7]
        LOADS = 7

        stage = ExitStack()
        block = stage.enter_context(nc.Block())

        @block.sync
        def _(sp):
            for dst, src in ((wt, d.wt), (wzT, d.wzT), (wgT, d.wgT), (wpT, d.wpT), (group_mean, d.group_mean),
                             (gn_w, d.gn_w), (gn_b, d.gn_b)):
                sp.dma_start(dst[:, :], src).then_inc(w_ld, 16)

        @block.scalar
        def _(act):
            act.preload_act_table_set(LN_EXP_SET)
            act.wait_ge(mT_done, 1)
            act.activation(mT[:, :], sm_ps[:, 0:P], ACT.Copy).then_inc(mT_copied, 1)
            for b in range(B):
                act.wait_ge(z_done, b + 1)
                act.activation(z[:, b, :], z_ps[b % 2][:, :], ACT.Copy).then_inc(z_copied, 1)
                if b == 1:
                    act.wait_ge(xval_done, 1)
                    act.activation(xtmp[:, :], xval[:, :], ACT.Ln, scale=2.0).then_inc(xln_ln, 1)
                    act.wait_ge(xln_ln, 1)
                    act.activation(xseed[:, :], xtmp[:, :], ACT.Exp, scale=-0.5).then_inc(xseed_done, 1)
            for b in range(B):
                act.wait_ge(g_done, b + 1)
                reached(act, row_done, b - 1)
                act.activation(g_sb[:, b % 2, :], g_ps[b % 2][:, :], ACT.Copy).then_inc(g_copied, 1)
            act.wait_ge(yval_done, 1)
            act.activation(yln[:, :], yval[:, :], ACT.Ln, scale=2.0).then_inc(yln_done, 1)
            act.wait_ge(yln_done, 1)
            act.activation(yseed[:, :], yln[:, :], ACT.Exp, scale=-0.5).then_inc(yseed_done, 1)
            act.wait_ge(col_step, 4)
            for b in range(B):
                act.activation(y[:, b, :], z[:, b, :], ACT.Identity, bias=b_col[:, b:b + 1],
                               scale=a_col[:, b:b + 1]).then_inc(y_done, 1)

        @block.gpsimd
        def _(pool):
            pool.wait_ge(xseed_done, 1)
            newton_rsqrt(pool, newton, 0, xval[:, :], xseed[:, :], xtmp[:, :], xrstd[:, :], s.c15).then_inc(xrstd_done, 1)
            pool.wait_ge(yseed_done, 1)
            newton_rsqrt(pool, newton, 3, yval[:, :], yseed[:, :], ytmp[:, :], yrstd[:, :], s.c15).then_inc(yrstd_done, 1)

        @block.vector
        def _(dve):
            for b in range(B):
                layernorm_stats(dve, s, b, bn, mv, x_step, 2 * b).then_inc(x_step, 1)
            dve.wait_ge(x_step, 2 * B)
            dve.tensor_scalar(xval[:, :], mv[:, :, 1], EPS, 0.5, ALU.add, ALU.mult).then_inc(xval_done, 1)
            dve.wait_ge(w_ld, 16 * LOADS)
            dve.tensor_tensor(tw[:, :], gn_w[:, :], s.tgates[:, 1:2], ALU.mult).then_inc(col_step, 1)
            dve.tensor_tensor(tb[:, :], gn_b[:, :], s.tgates[:, 1:2], ALU.mult).then_inc(col_step, 1)
            for b in range(B):
                dve.wait_ge(z_copied, b + 1)
                dve.bn_stats(zbn[:, b, :], z[:, b, :]).then_inc(zstat_step, 1)
                dve.wait_ge(zstat_step, 2 * b + 1)
                dve.bn_aggr(zmv[:, b, :], zbn[:, b, :]).then_inc(zstat_step, 1)
            dve.wait_ge(xrstd_done, 1)
            for b in range(B):
                dve.tensor_scalar(xln[:, b, :], s.x[:, b, :], mv[:, b, 0:1], xrstd[:, b:b + 1],
                                  ALU.subtract, ALU.mult).then_inc(xln_done, 1)
            dve.wait_ge(gmean_done, 1)
            dve.tensor_copy(gmean[:, :], sm_ps[:, 128:128 + B]).then_inc(dev_step, 1)
            dve.wait_ge(dev_step, 1)
            dve.tensor_tensor(dev[:, :], zmv[:, :, 0], gmean[:, :], ALU.subtract).then_inc(dev_step, 1)
            dve.wait_ge(dev_step, 2)
            dve.tensor_tensor(dev[:, :], dev[:, :], dev[:, :], ALU.mult).then_inc(dev_step, 1)
            dve.wait_ge(dev_step, 3)
            dve.tensor_tensor(dev[:, :], dev[:, :], zmv[:, :, 1], ALU.add).then_inc(dev_step, 1)
            dve.wait_ge(gvar_done, 1)
            dve.tensor_copy(gvar[:, :], sm_ps[:, 256:256 + B]).then_inc(dev_step, 1)
            for b in range(B):
                dve.wait_ge(g_copied, b + 1)
                dve.wait_ge(p_done, b + 1)
                reached(dve, row_done, b - 1)
                dve.tensor_tensor_reduce(out=prod[:, b % 2, :], in0=p_ps[b % 2][:, :], in1=g_sb[:, b % 2, :],
                                         scale=1.0, scalar=0.0, op0=ALU.mult, op1=ALU.add,
                                         accum_out=row[:, b:b + 1]).then_inc(row_done, 1)
            for b in range(B):
                dve.scalar_tensor_tensor(out=s.x[:, b, :], in0=s.ctx_nat[:, b, :], scalar=s.tgates[:, 1:2],
                                         in1=s.x[:, b, :], op0=ALU.mult, op1=ALU.add).then_inc(res_done, 1)
                if b == 1:
                    dve.wait_ge(att_done, 1)
                    dve.wait_ge(dev_step, 5)
                    dve.tensor_scalar(att[:, :], att_ps[:, 0:B], 16.0, None, ALU.mult).then_inc(dev_step, 1)
                    dve.wait_ge(dev_step, 6)
                    dve.tensor_tensor(yval[:, :], att[:, :], att[:, :], ALU.mult).then_inc(dev_step, 1)
                    dve.wait_ge(dev_step, 7)
                    dve.tensor_tensor(yval[:, :], yval[:, :], gvar[:, :], ALU.mult).then_inc(dev_step, 1)
                    dve.wait_ge(dev_step, 8)
                    dve.tensor_scalar(yval[:, :], yval[:, :], EPS, 0.5, ALU.add, ALU.mult).then_inc(yval_done, 1)
                    dve.wait_ge(col_step, 2)
                    dve.tensor_scalar(att[:, :], att[:, :], tw[:, 0:1], None, ALU.mult).then_inc(dev_step, 1)
            dve.wait_ge(yrstd_done, 1)
            dve.wait_ge(dev_step, 9)
            dve.tensor_tensor(a_col[:, :], att[:, :], yrstd[:, :], ALU.mult).then_inc(col_step, 1)
            dve.wait_ge(col_step, 3)
            dve.tensor_tensor(b_col[:, :], a_col[:, :], gmean[:, :], ALU.mult).then_inc(dev_step, 1)
            dve.wait_ge(dev_step, 10)
            dve.tensor_scalar(b_col[:, :], b_col[:, :], -1.0, tb[:, 0:1], ALU.mult, ALU.add).then_inc(col_step, 1)
            for b in range(B):
                dve.wait_ge(y_done, b + 1)
                dve.wait_ge(res_done, b + 1)
                dve.tensor_tensor(s.x[:, b, :], s.x[:, b, :], y[:, b, :], ALU.add).then_inc(x_done, 1)

        @block.tensor
        def _(pe):
            pe.wait_ge(w_ld, 16 * LOADS)
            pe.matmul(sm_ps[:, 0:P], wt[:, :], wzT[:, :], start=True, stop=True).then_inc(mT_done, 1)
            pe.wait_ge(mT_copied, 1)
            for b in range(B):
                reached(pe, z_copied, b - 1)
                pe.matmul(z_ps[b % 2][:, :], mT[:, :], s.ctx_nat[:, b, :], start=True, stop=True).then_inc(z_done, 1)
            for b in range(B):
                reached(pe, g_copied, b - 1)
                pe.matmul(g_ps[b % 2][:, :], wgT[:, :], s.ctx_nat[:, b, :], start=True, stop=True)\
                    .then_inc(g_done, 1)
                if b == 1:
                    pe.wait_ge(zstat_step, 2 * B)
                    pe.matmul(sm_ps[:, 128:128 + B], group_mean[:, :], zmv[:, :, 0], start=True, stop=True)\
                        .then_inc(gmean_done, 1)
                pe.wait_ge(xln_done, b + 1)
                reached(pe, row_done, b - 1)
                pe.matmul(p_ps[b % 2][:, :], wpT[:, :], xln[:, b, :], start=True, stop=True).then_inc(p_done, 1)
                if b == 1:
                    pe.wait_ge(dev_step, 4)
                    pe.matmul(sm_ps[:, 256:256 + B], group_mean[:, :], dev[:, :], start=True, stop=True)\
                        .then_inc(gvar_done, 1)
            pe.wait_ge(row_done, B)
            pe.matmul(att_ps[:, 0:B], group_mean[:, :], row[:, :], start=True, stop=True).then_inc(att_done, 1)

        stage.close()


def experts(nc, d, s):
    with ExitStack() as ctx:
        m = Mem(nc, ctx)
        xln = m.sb("xln4", [P, B, D])
        bn, mv = m.sb("bn4", [P, B, 6]), m.sb("mv4", [P, B, 2])
        xval, xseed = m.sb("xval4", [P, B]), m.sb("xseed4", [P, B])
        xtmp, xrstd = m.sb("xtmp4", [P, B]), m.sb("xrstd4", [P, B])
        gw_raw = m.sb("gw_raw", [P, KT, E])
        gw_hi, gw_lo = m.sb("gw_hi", [P, KT, E], F32R), m.sb("gw_lo", [P, KT, E], F32R)
        gate_b, eid = m.sb("gate_b", [P, E]), m.sb("eid", [P, E])
        exp_b = m.sb("exp_b", [E, D])
        w_raw = m.sb("ew_raw", [P, 2, KT, D])
        w_hi, w_lo = m.sb("ew_hi", [P, 2, KT, D], F32R), m.sb("ew_lo", [P, 2, KT, D], F32R)
        logit, top = m.sb("logit", [P, B, E]), m.sb("top", [P, B])
        cand, first = m.sb("cand", [P, B, E]), m.sb("first", [P, B])
        hot = m.sb("hot", [P, B, E])
        hotT = m.sb("hotT", [E, B, P])

        small_ld, w_ld = m.sem("gw_ld"), [m.sem(f"ew_ld{i}") for i in range(2)]
        x_step, xval_done = m.sem("x4_step"), m.sem("xval4_done")
        xln_ln, xseed_done, xrstd_done = m.sem("xln4_ln"), m.sem("xseed4_done"), m.sem("xrstd4_done")
        newton, xln_done = m.sem("newton4"), m.sem("xln4_done")
        xT_done, xT_hi_done, xT_lo_done = m.sem("xT4_done"), m.sem("xT4_hi_done"), m.sem("xT4_lo_done")
        gw_hi_done, gw_lo_done = m.sem("gw_hi_done"), m.sem("gw_lo_done")
        w_hi_done, w_lo_done = m.sem("ew_hi_done"), m.sem("ew_lo_done")
        logit_done, gate_step, hot_done = m.sem("logit_done"), m.sem("gate_step"), m.sem("hot_done")
        hotT_done, hotT_copied, bias_done = m.sem("hotT_done"), m.sem("hotT_copied"), m.sem("bias_done")
        y_done, x_done = m.sem("ey_done"), m.sem("x4_done")
        stored = m.sem("stored")
        xT_ps, logit_ps, hotT_ps = s.ps[0:2], s.ps[2], s.ps[3:5]
        y_ps = [s.ps[5], s.ps[6], s.ps[7]]
        LOADS = 4
        HB = B // 2

        stage = ExitStack()
        block = stage.enter_context(nc.Block())

        @block.sync
        def _(sp):
            for dst, src in ((gw_raw[:, :, :], d.gate_w), (gate_b[:, :], d.gate_b), (eid[:, :], d.eid),
                             (exp_b[:, :], d.exp_b)):
                sp.dma_start(dst, src).then_inc(small_ld, 16)
            for e in range(E):
                reached(sp, w_hi_done, KT * (e - 1))
                reached(sp, w_lo_done, KT * (e - 1))
                sp.dma_start(w_raw[:, e % 2, :, :], d.exp_w[e]).then_inc(w_ld[e % 2], 16)
            for b in range(B):
                sp.wait_ge(x_done, B * E + b + 1)
                sp.dma_start(d.out[:, b, :], s.x[:, b, :]).then_inc(stored, 16)
            sp.wait_ge(stored, 16 * B)

        @block.scalar
        def _(act):
            act.wait_ge(small_ld, 16 * LOADS)
            act.activation(gw_hi[:, :, :], gw_raw[:, :, :], ACT.Copy).then_inc(gw_hi_done, 1)
            for c in range(2):
                cols = slice(c * HB, (c + 1) * HB)
                act.wait_ge(xval_done, c + 1)
                act.activation(xtmp[:, cols], xval[:, cols], ACT.Ln, scale=2.0).then_inc(xln_ln, 1)
                act.wait_ge(xln_ln, c + 1)
                act.activation(xseed[:, cols], xtmp[:, cols], ACT.Exp, scale=-0.5).then_inc(xseed_done, 1)
            for b in range(B):
                act.wait_ge(xT_done, b + 1)
                act.activation(s.xT_hi[:, :, b * P:(b + 1) * P], blocks(xT_ps[b % 2][:, :]), ACT.Copy)\
                    .then_inc(xT_hi_done, 1)
            for e in range(E):
                act.wait_ge(w_ld[e % 2], 16 * (e // 2 + 1))
                for kt in range(KT):
                    if e >= 2:
                        act.wait_ge(y_done, B * (e - 1))
                    act.activation(w_hi[:, e % 2, kt, :], w_raw[:, e % 2, kt, :], ACT.Copy).then_inc(w_hi_done, 1)
                if e == 1:
                    for b in range(B):
                        act.wait_ge(hotT_done, b + 1)
                        act.activation(hotT[:, b, :], hotT_ps[b % 2][0:E, 0:P], ACT.Copy).then_inc(hotT_copied, 1)

        @block.gpsimd
        def _(pool):
            for c in range(2):
                cols = slice(c * HB, (c + 1) * HB)
                pool.wait_ge(xseed_done, c + 1)
                newton_rsqrt(pool, newton, 3 * c, xval[:, cols], xseed[:, cols], xtmp[:, cols], xrstd[:, cols],
                             s.c15)\
                    .then_inc(xrstd_done, 1)
            for e in range(E):
                for kt in range(KT):
                    pool.wait_ge(w_hi_done, KT * e + kt + 1)
                    pool.tensor_tensor(w_lo[:, e % 2, kt, :], w_raw[:, e % 2, kt, :],
                                       w_hi[:, e % 2, kt, :].bitcast(F32), ALU.subtract).then_inc(w_lo_done, 1)

        @block.vector
        def _(dve):
            for c in range(2):
                for b in range(c * HB, (c + 1) * HB):
                    layernorm_stats(dve, s, b, bn, mv, x_step, 2 * b).then_inc(x_step, 1)
                dve.wait_ge(x_step, 2 * HB * (c + 1))
                cols = slice(c * HB, (c + 1) * HB)
                dve.tensor_scalar(xval[:, cols], mv[:, cols, 1], EPS, 0.5, ALU.add, ALU.mult).then_inc(xval_done, 1)
            dve.wait_ge(gw_hi_done, 1)
            dve.tensor_tensor(gw_lo[:, :, :], gw_raw[:, :, :], gw_hi[:, :, :].bitcast(F32), ALU.subtract)\
                .then_inc(gw_lo_done, 1)
            for b in range(B):
                dve.wait_ge(xrstd_done, b // HB + 1)
                dve.tensor_scalar(xln[:, b, :], s.x[:, b, :], mv[:, b, 0:1], xrstd[:, b:b + 1],
                                  ALU.subtract, ALU.mult).then_inc(xln_done, 1)
            for b in range(B):
                dve.wait_ge(xT_hi_done, b + 1)
                dve.tensor_tensor(s.xT_lo[:, :, b * P:(b + 1) * P], blocks(xT_ps[b % 2][:, :]),
                                  s.xT_hi[:, :, b * P:(b + 1) * P].bitcast(F32), ALU.subtract)\
                    .then_inc(xT_lo_done, 1)
            dve.wait_ge(logit_done, 1)
            dve.wait_ge(small_ld, 16 * LOADS)
            over_b = lambda ap: ap.unsqueeze(1).to_broadcast([P, B, E])
            dve.tensor_tensor(logit[:, :, :], logit_ps[:, 0:B * E].rearrange("p (b e) -> p b e", b=B),
                              over_b(gate_b[:, :]), ALU.add).then_inc(gate_step, 1)
            dve.wait_ge(gate_step, 1)
            dve.tensor_reduce(top[:, :], logit[:, :, :], axis=AX_X, op=ALU.max).then_inc(gate_step, 1)
            dve.wait_ge(gate_step, 2)
            dve.tensor_tensor(cand[:, :, :], logit[:, :, :], per_block(top[:, :], E), ALU.is_lt)\
                .then_inc(gate_step, 1)
            dve.wait_ge(gate_step, 3)
            dve.scalar_tensor_tensor(out=cand[:, :, :], in0=cand[:, :, :], scalar=float(E), in1=over_b(eid[:, :]),
                                     op0=ALU.mult, op1=ALU.add).then_inc(gate_step, 1)
            dve.wait_ge(gate_step, 4)
            dve.tensor_reduce(first[:, :], cand[:, :, :], axis=AX_X, op=ALU.min).then_inc(gate_step, 1)
            dve.wait_ge(gate_step, 5)
            dve.tensor_tensor(hot[:, :, :], cand[:, :, :], per_block(first[:, :], E), ALU.is_equal)\
                .then_inc(gate_step, 1)
            dve.wait_ge(gate_step, 6)
            dve.tensor_scalar(hot[:, :, :], hot[:, :, :], s.tgates[:, 3:4], None, ALU.mult).then_inc(hot_done, 1)
            dve.wait_ge(hot_done, 1)
            for b in range(B):
                dve.wait_ge(bias_done, b + 1)
                dve.tensor_tensor(s.x[:, b, :], y_ps[b % 3][:, :], s.x[:, b, :], ALU.add).then_inc(x_done, 1)
            for e in range(E):
                for b in range(B):
                    n = e * B + b
                    dve.wait_ge(y_done, n + 1)
                    dve.wait_ge(x_done, n + 1)
                    dve.scalar_tensor_tensor(out=s.x[:, b, :], in0=y_ps[(n + B) % 3][:, :], scalar=hot[:, b, e:e + 1],
                                             in1=s.x[:, b, :], op0=ALU.mult, op1=ALU.add).then_inc(x_done, 1)

        @block.tensor
        def _(pe):
            for b in range(B):
                pe.wait_ge(xln_done, b + 1)
                reached(pe, xT_lo_done, b - 1)
                for kt in range(KT):
                    last = pe.transpose(xT_ps[b % 2][:, kt * P:(kt + 1) * P], xln[:, b, kt * P:(kt + 1) * P],
                                        s.ident[:, :])
                last.then_inc(xT_done, 1)
            pe.wait_ge(gw_lo_done, 1)
            for b in range(B):
                pe.wait_ge(xT_lo_done, b + 1)
                out = logit_ps[:, b * E:(b + 1) * E]
                for kt in range(KT):
                    xh, xl = s.xT_hi[:, kt, b * P:(b + 1) * P], s.xT_lo[:, kt, b * P:(b + 1) * P]
                    pe.matmul(out, xh, gw_hi[:, kt, :], start=(kt == 0), stop=False)
                    pe.matmul(out, xl, gw_hi[:, kt, :], start=False, stop=False)
                    last = pe.matmul(out, xh, gw_lo[:, kt, :], start=False, stop=(kt == KT - 1))
            last.then_inc(logit_done, 1)
            pe.wait_ge(hot_done, 1)
            for b in range(B):
                reached(pe, hotT_copied, b - 1)
                pe.transpose(hotT_ps[b % 2][0:E, 0:P], hot[:, b, :], s.ident[:, :]).then_inc(hotT_done, 1)
            for b in range(B):
                pe.wait_ge(hotT_copied, b + 1)
                reached(pe, x_done, b - 2)
                pe.matmul(y_ps[b % 3][:, :], hotT[:, b, :], exp_b[:, :], start=True, stop=True).then_inc(bias_done, 1)
            for e in range(E):
                for b in range(B):
                    n = e * B + b
                    pe.wait_ge(x_done, n + B - 2)
                    out = y_ps[(n + B) % 3][:, :]
                    for kt in range(KT):
                        if b == 0:
                            pe.wait_ge(w_lo_done, KT * e + kt + 1)
                        xh, xl = s.xT_hi[:, kt, b * P:(b + 1) * P], s.xT_lo[:, kt, b * P:(b + 1) * P]
                        pe.matmul(out, xh, w_hi[:, e % 2, kt, :], start=(kt == 0), stop=False)
                        pe.matmul(out, xl, w_hi[:, e % 2, kt, :], start=False, stop=False)
                        last = pe.matmul(out, xh, w_lo[:, e % 2, kt, :], start=False, stop=(kt == KT - 1))
                    last.then_inc(y_done, 1)

        stage.close()


class Names:
    pass


def flamingo(nc, a, out):
    d = Names()
    d.x = a["x"].rearrange("b t n -> t b n")
    d.ctx = a["ctx"].rearrange("b t n -> t b n")
    d.out = out.rearrange("b t n -> t b n")
    d.ctxT = a["ctxT"]
    d.kv_w = [a["kw_l"][0], a["kw_l"][1], a["vw_l"][0], a["vw_l"][1]]
    d.ident, d.qw, d.kw, d.mask = a["ident"], a["q_norm"], a["k_norm"], a["mask"]
    d.g_xattn, d.g_ffn = a["g_xattn"].to_broadcast([P, 2]), a["g_ffn"].to_broadcast([P, 2])
    d.wq, d.wo = a["wq_l"], a["wo_l"]
    d.perm_row, d.perm_col = a["perm_row"].to_broadcast([P, D]), a["perm_col"]
    d.iota_row, d.iota_col = a["iota_row"].to_broadcast([P, D]), a["iota_col"]
    d.up, d.down = a["up_l"], a["down_l"]
    d.wt, d.wzT, d.wgT, d.wpT = a["wt"], a["wzT"], a["wgT"], a["wpT"]
    d.group_mean, d.gn_w, d.gn_b = a["group_mean"], a["gn_w"], a["gn_b"]
    d.gate_w, d.gate_b = a["gate_w_l"], a["gate_b"].to_broadcast([P, E])
    d.eid = a["iota_row"][:, 0:E].to_broadcast([P, E])
    d.exp_b, d.exp_w = a["exp_b"], a["exp_w_l"]
    d.kT_scr = nc.dram_tensor("kT_scr", (G, P, T), F32, kind="Internal").ap()
    d.v_scr = nc.dram_tensor("v_scr", (G, P, B, P), F32, kind="Internal").ap()

    with ExitStack() as ctx:
        m = Mem(nc, ctx)
        s = Names()
        s.ps = [ctx.enter_context(nc.psum_tensor(f"bank{i}", [P, D], F32)) for i in range(8)]
        s.x = m.sb("x_sb", [P, B, D])
        s.xT_hi, s.xT_lo = m.sb("xT_hi", [P, KT, T], F32R), m.sb("xT_lo", [P, KT, T], F32R)
        s.ident = m.sb("ident_sb", [P, P])
        s.gates, s.tgates = m.sb("gates", [P, 4]), m.sb("tgates", [P, 4])
        s.eps, s.eps_set = m.sb("eps", [P, 1]), m.sem("eps_set")
        s.c15, s.c15_set = m.sb("three_halves", [P, B]), m.sem("three_halves_set")
        s.acc = m.sb("acc", [P, B, D])
        project_kv(nc, d, s)
        attention(nc, d, s)
        s.ctx_nat = m.sb("ctx_nat", [P, B, D])
        feed_forward(nc, d, s)
        nonlocal_attention(nc, d, s)
        experts(nc, d, s)


def kernel(**inputs):
    import numpy as np
    import concourse.bacc as bacc
    from concourse.bass_utils import run_bass_kernel_spmd

    i = {k: np.asarray(v) for k, v in inputs.items()}
    wz = i["L1_xattn_Wz"].reshape(8, 16, 16)
    wzT = np.zeros((P, P), np.float32)
    for g in range(8):
        wzT[16 * g:16 * g + 16, 16 * g:16 * g + 16] = wz[g].T
    arrays = {
        "x": i["x"],
        "ctx": i["ctx_4096"],
        "ctxT": i["ctx_4096"].reshape(T, KT, P).transpose(2, 1, 0),
        "kw_l": i["L0_xattn_k_proj_w"].reshape(2, D, KT, P).transpose(0, 3, 2, 1),
        "vw_l": i["L0_xattn_v_proj_w"].reshape(2, D, KT, P).transpose(0, 3, 2, 1),
        "wq_l": i["L0_xattn_q_proj_w"].reshape(G, D, KT, P).transpose(0, 3, 2, 1),
        "wo_l": i["L0_xattn_o_proj_w"].reshape(D, G, HG, P).transpose(1, 3, 2, 0),
        "q_norm": i["L0_xattn_q_norm_w"].reshape(P, 1),
        "k_norm": i["L0_xattn_k_norm_w"].reshape(P, 1),
        "mask": i["mask_1x1xSxS2_ff0"].reshape(P, P),
        "g_xattn": i["g_xattn"].reshape(1, 2),
        "g_ffn": i["g_ffn"].reshape(1, 2),
        "perm_row": i["L0_ffn_perm"].reshape(1, D),
        "perm_col": i["L0_ffn_perm"].reshape(KT, P).T,
        "up_l": i["L0_ffn_up"].reshape(KT, P, P).transpose(1, 0, 2),
        "down_l": i["L0_ffn_down"].transpose(1, 0, 2).reshape(P, D),
        "wt": i["L1_xattn_Wt"],
        "wzT": wzT,
        "wgT": i["L1_xattn_Wg"].T,
        "wpT": i["L1_xattn_Wp"].T,
        "gn_w": i["L1_xattn_gn_w"].reshape(P, 1),
        "gn_b": i["L1_xattn_gn_b"].reshape(P, 1),
        "gate_w_l": i["L1_ffn_gate_w"].reshape(E, KT, P).transpose(2, 1, 0),
        "gate_b": i["L1_ffn_gate_b"].reshape(1, E),
        "exp_w_l": i["L1_ffn_expert_w"].reshape(E, D, KT, P).transpose(0, 3, 2, 1),
        "exp_b": i["L1_ffn_expert_b"],
        "ident": np.eye(P, dtype=np.float32),
        "iota_row": np.arange(D, dtype=np.float32).reshape(1, D),
        "iota_col": np.arange(D, dtype=np.float32).reshape(KT, P).T,
        "group_mean": np.kron(np.eye(8), np.full((16, 16), 1 / 16)).astype(np.float32),
    }
    arrays = {k: np.ascontiguousarray(v) for k, v in arrays.items()}
    nc = bacc.Bacc("TRN2", target_bir_lowering=False, num_devices=1)
    aps = {k: nc.dram_tensor(f"in_{k}", v.shape, mybir.dt.from_np(v.dtype), kind="ExternalInput").ap()
           for k, v in arrays.items()}
    out = nc.dram_tensor("out", (B, P, D), F32, kind="ExternalOutput").ap()
    flamingo(nc, aps, out)
    r = run_bass_kernel_spmd(nc, [{f"in_{k}": v for k, v in arrays.items()}], core_ids=[0])
    return r.results[0]["out"]
```

```python
from contextlib import ExitStack

import concourse.bass as bass
from concourse.bass import IndirectOffsetOnAxis
from concourse import mybir

F32 = mybir.dt.float32
F32R = mybir.dt.float32r
I32 = mybir.dt.int32
ALU = mybir.AluOpType
ACT = mybir.ActivationFunctionType
LN_EXP_SET = "natural_log_exp_and_others"
AX_X = mybir.AxisListType.X

P = 128
B = 8
D = 512
KT = D // P
T = B * P
HG = 4
G = 8
UNITS = G * B
E = 8
FH = 16
FD = D // FH
HALF = 512
EPS = 1e-5
SORTED = B + E - 1


def reached(eng, sem, value):
    if not (isinstance(value, int) and value <= 0):
        eng.wait_ge(sem, value)


def per_block(col, n):
    return col.unsqueeze(2).to_broadcast([P, col.shape[1], n])


def blocks(ap, k=HG):
    return ap.rearrange("p (k n) -> p k n", k=k)


def newton_rsqrt(eng, sem, count, half, seed, tmp, out, three_halves):
    eng.tensor_tensor(tmp, seed, seed, ALU.mult).then_inc(sem, 1)
    eng.wait_ge(sem, count + 1)
    eng.tensor_tensor(tmp, tmp, half, ALU.mult).then_inc(sem, 1)
    eng.wait_ge(sem, count + 2)
    eng.tensor_tensor(tmp, three_halves[:, 0:tmp.shape[1]], tmp, ALU.subtract).then_inc(sem, 1)
    eng.wait_ge(sem, count + 3)
    return eng.tensor_tensor(out, seed, tmp, ALU.mult)


def layernorm_stats(dve, s, b, step, count):
    dve.bn_stats(s.bn[:, b, :], s.x[:, b, :]).then_inc(step, 1)
    dve.wait_ge(step, count + 1)
    return dve.bn_aggr(s.mv[:, b, :], s.bn[:, b, :])


def layernorm_half_var(dve, s, step, count):
    dve.wait_ge(step, count)
    dve.tensor_scalar(s.xval[:, :], s.mv[:, :, 1], EPS, 0.5, ALU.add, ALU.mult).then_inc(step, 1)


class Mem:

    def __init__(self, nc, ctx):
        self.nc, self.ctx, self.sems = nc, ctx, []

    def sb(self, name, shape, dt=F32):
        return self.ctx.enter_context(self.nc.sbuf_tensor(name, shape, dt))

    def sem(self, name):
        self.sems.append(self.nc.alloc_semaphore(name))
        return self.sems[-1]

    def clear_sems(self):
        self.nc.clear_and_free_semaphores(self.sems)
        self.nc.all_engine_barrier()


def project_kv(nc, d, s):
    with ExitStack() as ctx:
        m = Mem(nc, ctx)
        ctx_raw = m.sb("ctx_raw", [P, KT, HALF])
        ctx_hi = m.sb("ctx_hi", [P, KT, T], F32R)
        ctx_lo = m.sb("ctx_lo", [P, KT, T], F32R)
        w_raw, w_hi, w_lo = s.w_raw, s.w_hi, s.w_lo
        xln = m.sb("xln1", [P, 2, D])
        junk = m.sb("kv_junk", [P, D])
        k_sb = m.sb("k_sb", [P, 2, D])
        kT_st = m.sb("kT_st", [P, 2, D])
        v_st = m.sb("v_st", [P, 2, D])
        qw = m.sb("qw", [P, 1])
        kw = m.sb("kw", [P, 1])
        qkw = m.sb("qkw", [P, 1])
        ss = m.sb("k_ss", [P, 2, HG])
        lnss = m.sb("k_lnss", [P, 2, HG])
        seed = m.sb("k_seed", [P, 2, HG])
        val = m.sb("k_val", [P, 2, HG])
        tmp = m.sb("k_tmp", [P, 2, HG])
        rstd = m.sb("k_rstd", [P, 2, HG])
        bn, mv = s.bn, s.mv
        xval = m.sb("xval1", [P, B])
        xseed = m.sb("xseed1", [P, B])
        xtmp = m.sb("xtmp1", [P, B])
        xrstd = m.sb("xrstd1", [P, B])

        first_ld = [m.sem(f"first_ld{kt}") for kt in range(KT)]
        ctx_ld = m.sem("ctx_ld")
        wo_ld = m.sem("wo0_ld")
        w_ld = [m.sem(f"kvw_ld{i}") for i in range(2)]
        x_ld = m.sem("x_ld")
        small_ld = m.sem("small_ld")
        gates_ready = m.sem("gates_ready")
        ctx_hi_done, ctx_lo_done = m.sem("ctx_hi_done"), m.sem("ctx_lo_done")
        w_hi_done, w_lo_done = m.sem("kvw_hi_done"), m.sem("kvw_lo_done")
        kv_done = m.sem("kv_done")
        kv_free = m.sem("kv_free")
        k_scaled = m.sem("k_scaled")
        v_copied = m.sem("v_copied")
        sumsq_done, ln_done, seed_done = m.sem("k_sumsq"), m.sem("k_ln"), m.sem("k_seeded")
        newton, rstd_done = m.sem("k_newton"), m.sem("k_rstd_done")
        kT_done, kT_copied = m.sem("kT_done"), m.sem("kT_copied")
        kT_stored = [m.sem(f"kT_stored{i}") for i in range(2)]
        v_stored = [m.sem(f"v_stored{i}") for i in range(2)]
        stats_step, qkw_done = m.sem("stats1_step"), m.sem("qkw_done")
        xval_done, xln_ln, xseed_done = m.sem("xval1_done"), m.sem("xln1_ln"), m.sem("xseed1_done")
        xrstd_done, xln_done = m.sem("xrstd1_done"), m.sem("xln1_done")
        xT_done, xT_hi_done, xT_lo_done = m.sem("xT1_done"), m.sem("xT1_hi_done"), m.sem("xT1_lo_done")
        kv_ps = s.ps[0:3]
        kT_ps = s.ps[3:5]
        xT_ps = s.ps[5:7]
        NU = 4 * B
        NK = 2 * B
        XT0 = NK + 2

        stage = ExitStack()
        block = stage.enter_context(nc.Block())

        @block.sync
        def _(sp):
            for kt in range(KT):
                sp.dma_start(ctx_raw[:, kt, :], d.ctxT[:, kt, 0:HALF]).then_inc(first_ld[kt], 16)
                sp.dma_start(w_raw[:, 0, kt, :], d.kv_w[0][:, kt, :]).then_inc(first_ld[kt], 16)
            for dst, src in ((s.ident[:, :], d.ident), (qw[:, :], d.qw), (kw[:, :], d.kw),
                             (s.gates[:, 0:2], d.g_xattn), (s.gates[:, 2:4], d.g_ffn)):
                sp.dma_start(dst, src).then_inc(small_ld, 16)
            sp.dma_start(w_raw[:, 1, :, :], d.kv_w[1]).then_inc(w_ld[1], 16)
            sp.wait_ge(ctx_lo_done, KT)
            sp.dma_start(ctx_raw[:, :, :], d.ctxT[:, :, HALF:T]).then_inc(ctx_ld, 16)
            sp.dma_start(s.x[:, :, :], d.x).then_inc(x_ld, 16)
            for i in range(NU):
                w, b = divmod(i, B)
                n = {0: 2, B - 2: 3, 2 * B - 2: 4, 3 * B - 2: 5}.get(i)
                if n:
                    sp.wait_ge(w_lo_done, KT * (n - 1))
                    src, ld = (d.kv_w[n], w_ld[n % 2]) if n < 5 else (d.wo[0, :, :, :], wo_ld)
                    sp.dma_start(w_raw[:, n % 2, :, :], src).then_inc(ld, 16)
                if i < NK:
                    sp.wait_ge(kT_copied, i + 1)
                    sp.dma_start(d.kT_scr[4 * w:4 * w + 4, :, b * P:(b + 1) * P].rearrange("g d t -> d g t"),
                                 blocks(kT_st[:, i % 2, :])).then_inc(kT_stored[i % 2], 16)
                else:
                    sp.wait_ge(v_copied, i - NK + 1)
                    sp.dma_start(d.v_scr[4 * (w - 2):4 * (w - 2) + 4, :, b, :].rearrange("g t d -> t g d"),
                                 blocks(v_st[:, i % 2, :])).then_inc(v_stored[i % 2], 16)
            for q in range(2):
                sp.wait_ge(kT_stored[q], 16 * (NK // 2))
                sp.wait_ge(v_stored[q], 16 * (NK // 2))
            sp.wait_ge(wo_ld, 16)

        @block.scalar
        def _(act):
            for kt in range(KT):
                act.wait_ge(first_ld[kt], 32)
                act.activation(ctx_hi[:, kt, 0:HALF], ctx_raw[:, kt, :], ACT.Copy).then_inc(ctx_hi_done, 1)
            act.wait_ge(small_ld, 16 * 5)
            act.activation(s.tgates[:, :], s.gates[:, :], ACT.Tanh).then_inc(gates_ready, 1)
            act.preload_act_table_set(LN_EXP_SET)
            act.wait_ge(ctx_ld, 16)
            act.activation(ctx_hi[:, :, HALF:T], ctx_raw[:, :, :], ACT.Copy).then_inc(ctx_hi_done, 1)
            for i in range(NU):
                if i < NK:
                    act.wait_ge(kv_done, i + 1)
                    if i == 0:
                        act.wait_ge(s.eps_set, 1)
                    reached(act, rstd_done, i - 1)
                    reached(act, sumsq_done, i)
                    for h in range(HG):
                        last = act.activation(junk[:, h * P:(h + 1) * P], kv_ps[i % 3][:, h * P:(h + 1) * P],
                                              ACT.Square, accum_out=ss[:, i % 2, h:h + 1])
                    last.then_inc(sumsq_done, 1)
                    act.wait_ge(sumsq_done, i + 1)
                    act.activation(lnss[:, i % 2, :], ss[:, i % 2, :], ACT.Ln, bias=s.eps[:, 0:1], scale=1.0 / P)\
                        .then_inc(ln_done, 1)
                    act.wait_ge(ln_done, i + 1)
                    act.activation(seed[:, i % 2, :], lnss[:, i % 2, :], ACT.Exp, scale=-0.5).then_inc(seed_done, 1)
                else:
                    n = i - NK
                    act.wait_ge(kv_done, i + 1)
                    if n >= 2:
                        act.wait_ge(v_stored[i % 2], 16 * (n // 2))
                    act.activation(v_st[:, i % 2, :], kv_ps[i % 3][:, :], ACT.Copy).then_inc(v_copied, 1)
                if i == NK - 1:
                    act.wait_ge(xval_done, 1)
                    act.activation(xtmp[:, :], xval[:, :], ACT.Ln, scale=2.0).then_inc(xln_ln, 1)
                    act.wait_ge(xln_ln, 1)
                    act.activation(xseed[:, :], xtmp[:, :], ACT.Exp, scale=-0.5).then_inc(xseed_done, 1)
                if XT0 <= i < XT0 + B:
                    b = i - XT0
                    act.wait_ge(xT_done, b + 1)
                    act.activation(s.xT_hi[:, :, b * P:(b + 1) * P], blocks(xT_ps[b % 2][:, :]), ACT.Copy)\
                        .then_inc(xT_hi_done, 1)

        @block.gpsimd
        def _(pool):
            pool.memset(s.c15[:, :], 1.5).then_inc(s.c15_set, 1)
            pool.wait_ge(s.c15_set, 1)
            for i in range(NK):
                pool.wait_ge(sumsq_done, i + 1)
                reached(pool, rstd_done, i)
                pool.tensor_scalar(val[:, i % 2, :], ss[:, i % 2, :], 0.5 / P, 0.5 * EPS, ALU.mult, ALU.add)\
                    .then_inc(newton, 1)
                pool.wait_ge(seed_done, i + 1)
                pool.wait_ge(newton, 4 * i + 1)
                reached(pool, k_scaled, i - 1)
                newton_rsqrt(pool, newton, 4 * i + 1, val[:, i % 2, :], seed[:, i % 2, :], tmp[:, i % 2, :],
                             rstd[:, i % 2, :], s.c15).then_inc(rstd_done, 1)
            pool.wait_ge(xseed_done, 1)
            newton_rsqrt(pool, newton, 4 * NK, xval[:, :], xseed[:, :], xtmp[:, :], xrstd[:, :], s.c15)\
                .then_inc(xrstd_done, 1)

        @block.vector
        def _(dve):
            dve.memset(s.eps[:, :], EPS).then_inc(s.eps_set, 1)

            def split_w(w, kts):
                for kt in kts:
                    if w == 0:
                        dve.wait_ge(first_ld[kt], 32)
                    else:
                        dve.wait_ge(w_ld[w % 2], 16 * ((w + 1) // 2))
                    if w >= 2:
                        dve.wait_ge(kv_done, B * (w - 1))
                    dve.tensor_copy(w_hi[:, w % 2, kt, :], w_raw[:, w % 2, kt, :]).then_inc(w_hi_done, 1)
                    dve.wait_ge(w_hi_done, KT * w + kt + 1)
                    dve.tensor_tensor(w_lo[:, w % 2, kt, :], w_raw[:, w % 2, kt, :],
                                      w_hi[:, w % 2, kt, :].bitcast(F32), ALU.subtract).then_inc(w_lo_done, 1)

            for kt in range(KT):
                split_w(0, [kt])
                dve.wait_ge(ctx_hi_done, kt + 1)
                dve.tensor_tensor(ctx_lo[:, kt, 0:HALF], ctx_raw[:, kt, :], ctx_hi[:, kt, 0:HALF].bitcast(F32),
                                  ALU.subtract).then_inc(ctx_lo_done, 1)
            dve.wait_ge(small_ld, 16 * 5)
            dve.tensor_tensor(qkw[:, :], qw[:, :], kw[:, :], ALU.mult).then_inc(qkw_done, 1)
            dve.wait_ge(ctx_hi_done, KT + 1)
            dve.tensor_tensor(ctx_lo[:, :, HALF:T], ctx_raw[:, :, :], ctx_hi[:, :, HALF:T].bitcast(F32),
                              ALU.subtract).then_inc(ctx_lo_done, 1)
            dve.wait_ge(x_ld, 16)
            dve.wait_ge(qkw_done, 1)
            for i in range(NU):
                w, b = divmod(i, B)
                if i < NK:
                    dve.wait_ge(rstd_done, i + 1)
                    dve.wait_ge(kv_done, i + 1)
                    reached(dve, kT_done, i - 1)
                    dve.tensor_tensor(blocks(k_sb[:, i % 2, :]), blocks(kv_ps[i % 3][:, :]),
                                      per_block(rstd[:, i % 2, :], P), ALU.mult).then_inc(k_scaled, 1)
                if 1 <= b <= KT:
                    split_w(w + 1, [b - 1])
                if 1 <= i <= NK:
                    n = i - 1
                    dve.wait_ge(kT_done, n + 1)
                    if n >= 2:
                        dve.wait_ge(kT_stored[n % 2], 16 * (n // 2))
                    dve.tensor_scalar(kT_st[:, n % 2, :], kT_ps[n % 2][:, :], qkw[:, 0:1], None, ALU.mult)\
                        .then_inc(kT_copied, 1)
                if i < B:
                    dve.bn_stats(bn[:, i, :], s.x[:, i, :]).then_inc(stats_step, 1)
                    dve.wait_ge(stats_step, 2 * i + 1)
                    dve.bn_aggr(mv[:, i, :], bn[:, i, :]).then_inc(stats_step, 1)
                if i == B:
                    dve.wait_ge(stats_step, 2 * B)
                    dve.tensor_scalar(xval[:, :], mv[:, :, 1], EPS, 0.5, ALU.add, ALU.mult).then_inc(xval_done, 1)
                if XT0 - 1 <= i < XT0 - 1 + B:
                    n = i - XT0 + 1
                    dve.wait_ge(xrstd_done, 1)
                    reached(dve, xT_done, n - 1)
                    dve.tensor_scalar(xln[:, n % 2, :], s.x[:, n, :], mv[:, n, 0:1], xrstd[:, n:n + 1],
                                      ALU.subtract, ALU.mult).then_inc(xln_done, 1)
                if XT0 <= i < XT0 + B:
                    n = i - XT0
                    dve.wait_ge(xT_hi_done, n + 1)
                    dve.tensor_tensor(s.xT_lo[:, :, n * P:(n + 1) * P], blocks(xT_ps[n % 2][:, :]),
                                      s.xT_hi[:, :, n * P:(n + 1) * P].bitcast(F32), ALU.subtract)\
                        .then_inc(xT_lo_done, 1)

        @block.tensor
        def _(pe):
            for i in range(NU):
                w, b = divmod(i, B)
                if i == B // 2:
                    pe.wait_ge(ctx_lo_done, KT + 1)
                if i >= 3:
                    if i - 3 < NK:
                        pe.wait_ge(k_scaled, i - 2)
                    else:
                        pe.wait_ge(v_copied, i - 2 - NK)
                tok = slice(b * P, (b + 1) * P)
                for kt in range(KT):
                    if i == 0:
                        pe.wait_ge(ctx_lo_done, kt + 1)
                    if b == 0:
                        pe.wait_ge(w_lo_done, KT * w + kt + 1)
                    hi, lo = w_hi[:, w % 2, kt, :], w_lo[:, w % 2, kt, :]
                    pe.matmul(kv_ps[i % 3][:, :], ctx_hi[:, kt, tok], hi, start=(kt == 0), stop=False)
                    pe.matmul(kv_ps[i % 3][:, :], ctx_lo[:, kt, tok], hi, start=False, stop=False)
                    last = pe.matmul(kv_ps[i % 3][:, :], ctx_hi[:, kt, tok], lo, start=False, stop=(kt == KT - 1))
                last.then_inc(kv_done, 1)
                if 2 <= i < NK + 2:
                    n = i - 2
                    if n == 0:
                        pe.wait_ge(small_ld, 16 * 5)
                    pe.wait_ge(k_scaled, n + 1)
                    reached(pe, kT_copied, n - 1)
                    for h in range(HG):
                        last = pe.transpose(kT_ps[n % 2][:, h * P:(h + 1) * P], k_sb[:, n % 2, h * P:(h + 1) * P],
                                            s.ident[:, :])
                    last.then_inc(kT_done, 1)
                if XT0 <= i < XT0 + B:
                    n = i - XT0
                    pe.wait_ge(xln_done, n + 1)
                    reached(pe, xT_lo_done, n - 1)
                    for kt in range(KT):
                        last = pe.transpose(xT_ps[n % 2][:, kt * P:(kt + 1) * P], xln[:, n % 2, kt * P:(kt + 1) * P],
                                            s.ident[:, :])
                    last.then_inc(xT_done, 1)

        stage.close()
        m.clear_sems()


def attention(nc, d, s):
    with ExitStack() as ctx:
        m = Mem(nc, ctx)
        wq_raw, wq_hi, wq_lo = (t[:, 0, :, :] for t in (s.w_raw, s.w_hi, s.w_lo))
        wo_raw, wo_hi, wo_lo = (t[:, 1, :, :] for t in (s.w_raw, s.w_hi, s.w_lo))
        kT = m.sb("kT", [P, T])
        v_raw = m.sb("v_raw", [P, B, P])
        v_hi = m.sb("v_hi", [P, B, P], F32R)
        v_lo = m.sb("v_lo", [P, B, P], F32R)
        mask = m.sb("mask", [P, P])
        junk = m.sb("q_junk", [P, D])
        q_sb = m.sb("q_sb", [P, 2, D])
        qT_sb = m.sb("qT_sb", [P, 2, D])
        p_sb = m.sb("p_sb", [P, 2, D])
        pT_hi = m.sb("pT_hi", [P, D], F32R)
        pT_lo = m.sb("pT_lo", [P, D], F32R)
        oT_hi = m.sb("oT_hi", [P, D], F32R)
        oT_lo = m.sb("oT_lo", [P, D], F32R)
        ss = m.sb("q_ss", [P, 2, HG])
        lnss = m.sb("q_lnss", [P, 2, HG])
        seed = m.sb("q_seed", [P, 2, HG])
        val = m.sb("q_val", [P, 2, HG])
        tmp = m.sb("q_tmp", [P, 2, HG])
        rstd = m.sb("q_rstd", [P, 2, HG])
        nmax = m.sb("nmax", [P, 2, HG])
        psum_ = m.sb("prob_sum", [P, 2, HG])
        rsum = m.sb("rsum", [P, 2, HG])
        qeps = m.sb("qeps", [P, 1])

        mask_ld, ctx_nat_ld = m.sem("mask_ld"), m.sem("ctx_nat_ld")
        qeps_set = m.sem("qeps_set")
        wq_ld, wo_ld = m.sem("wq_ld"), m.sem("wo_ld")
        kT_ld = [m.sem(f"kT_ld{i}") for i in range(2)]
        v_ld = [m.sem(f"v_ld{i}") for i in range(2)]
        wq_hi_done, wo_hi_done = m.sem("wq_hi_done"), m.sem("wo_hi_done")
        wq_pool_done, wq_dve_done = m.sem("wq_pool_done"), m.sem("wq_dve_done")
        wo_pool_done, wo_dve_done = m.sem("wo_pool_done"), m.sem("wo_dve_done")
        x_step = m.sem("x1_step")
        wq_used, wo_used = m.sem("wq_used"), m.sem("wo_used")
        v_hi_done, v_lo_done = m.sem("v_hi_done"), m.sem("v_lo_done")
        q_done, q_scaled = m.sem("q_done"), m.sem("q_scaled")
        sumsq_done, ln_done, seed_done = m.sem("q_sumsq"), m.sem("q_ln"), m.sem("q_seeded")
        newton, rstd_done = m.sem("q_newton"), m.sem("q_rstd_done")
        half_done = m.sem("q_half_done")
        qT_done, qT_copied = m.sem("qT_done"), m.sem("qT_copied")
        s_done, masked, max_done = m.sem("s_done"), m.sem("masked"), m.sem("max_done")
        exp_done, rsum_done, p_done = m.sem("exp_done"), m.sem("rsum_done"), m.sem("p_done")
        pT_done, pT_hi_done, pT_lo_done = m.sem("pT_done"), m.sem("pT_hi_done"), m.sem("pT_lo_done")
        pv_done, oT_hi_done, oT_lo_done = m.sem("pv_done"), m.sem("oT_hi_done"), m.sem("oT_lo_done")
        o_done, acc_done = m.sem("o_done"), m.sem("acc_done")

        q_ps, o_ps = s.ps[0:2], s.ps[2:4]
        qT_ps, s_ps, pT_ps, oT_ps = s.ps[4], s.ps[5], s.ps[6], s.ps[7]

        def run(eng, stages):

            def step(g, b):
                for stage, ahead in stages:
                    u = 8 * g + b + ahead
                    if not isinstance(u, int) or 0 <= u < UNITS:
                        stage(u, (b + ahead) % B, g + (b + ahead) // B)

            for b in range(2, B):
                step(-1, b)
            for b in range(B):
                step(0, b)
            with eng.Fori(1, G - 1) as g:
                for b in range(B):
                    step(g, b)
            for b in range(B):
                step(G - 1, b)
            for b in range(2):
                step(G, b)

        stage = ExitStack()
        block = stage.enter_context(nc.Block())

        @block.sync
        def _(sp):
            sp.dma_start(mask[:, :], d.mask).then_inc(mask_ld, 16)

            def loads(g):
                def v_half(c):
                    reached(sp, v_hi_done, 8 * g - 4 + 4 * c)
                    reached(sp, v_lo_done, 8 * g - 4 + 4 * c)
                    sp.dma_start(v_raw[:, 4 * c:4 * c + 4, :], d.v_scr[g, :, 4 * c:4 * c + 4, :])\
                        .then_inc(v_ld[c], 16)

                def kT_half(c):
                    reached(sp, s_done, 8 * g - 4 + 4 * c)
                    sp.dma_start(kT[:, c * HALF:(c + 1) * HALF], d.kT_scr[g, :, c * HALF:(c + 1) * HALF])\
                        .then_inc(kT_ld[c], 16)

                v_half(0)
                reached(sp, wq_pool_done, 2 * g - 2)
                reached(sp, wq_dve_done, 2 * g - 2)
                sp.dma_start(wq_raw[:, :, :], d.wq[g, :, :, :]).then_inc(wq_ld, 16)
                v_half(1)
                reached(sp, wo_pool_done, 2 * g)
                reached(sp, wo_dve_done, 2 * g)
                sp.dma_start(wo_raw[:, :, :], d.wo[g, :, :, :]).then_inc(wo_ld, 16)
                kT_half(0)
                kT_half(1)

            sp_first = 0
            for c in range(2):
                sp.dma_start(v_raw[:, 4 * c:4 * c + 4, :], d.v_scr[sp_first, :, 4 * c:4 * c + 4, :])\
                    .then_inc(v_ld[c], 16)
            for c in range(2):
                sp.dma_start(kT[:, c * HALF:(c + 1) * HALF], d.kT_scr[0, :, c * HALF:(c + 1) * HALF])\
                    .then_inc(kT_ld[c], 16)
            sp.dma_start(s.ctx_nat[:, :, :], d.ctx).then_inc(ctx_nat_ld, 16)
            loads(1)
            with sp.Fori(2, G) as g:
                loads(g)
            sp.wait_ge(ctx_nat_ld, 16)

        @block.scalar
        def _(act):
            act.wait_ge(qeps_set, 1)

            def oT_split(u, b, g):
                act.wait_ge(pv_done, u + 1)
                reached(act, o_done, u)
                act.activation(oT_hi[:, :], oT_ps[:, :], ACT.Copy).then_inc(oT_hi_done, 1)

            def exps(u, b, g):
                act.wait_ge(max_done, u + 1)
                for h in range(HG):
                    last = act.activation(p_sb[:, b % 2, h * P:(h + 1) * P], p_sb[:, b % 2, h * P:(h + 1) * P],
                                          ACT.Exp, bias=nmax[:, b % 2, h:h + 1],
                                          accum_out=psum_[:, b % 2, h:h + 1])
                last.then_inc(exp_done, 1)

            def qT_copy(u, b, g):
                act.wait_ge(qT_done, u + 1)
                reached(act, s_done, u - 1)
                act.activation(qT_sb[:, b % 2, :], qT_ps[:, :], ACT.Copy).then_inc(qT_copied, 1)

            def pT_split(u, b, g):
                act.wait_ge(pT_done, u + 1)
                reached(act, pv_done, u)
                act.activation(pT_hi[:, :], pT_ps[:, :], ACT.Copy).then_inc(pT_hi_done, 1)

            def wq_split(kts):
                def stage(u, b, g):
                    if b or (isinstance(g, int) and g == 0):
                        return
                    act.wait_ge(wq_ld, 16 * g)
                    for kt in kts:
                        if kt < KT - 1:
                            act.wait_ge(wq_used, 3 * g - 2 + kt)
                        else:
                            act.wait_ge(q_done, 8 * g)
                        act.activation(wq_hi[:, kt, :], wq_raw[:, kt, :], ACT.Copy).then_inc(wq_hi_done, 1)

                return stage

            def wo_split(hs):
                def stage(u, b, g):
                    if b:
                        return
                    reached(act, wo_ld, 16 * g)
                    for h in hs:
                        if h < HG - 1:
                            reached(act, wo_used, 3 * g - 2 + h)
                        else:
                            reached(act, o_done, 8 * g)
                        act.activation(wo_hi[:, h, :], wo_raw[:, h, :], ACT.Copy).then_inc(wo_hi_done, 1)

                return stage

            def v_split(u, b, g):
                act.wait_ge(v_ld[b // 4], 16 * g + 16)
                reached(act, pv_done, u - 7)
                act.activation(v_hi[:, b, :], v_raw[:, b, :], ACT.Copy).then_inc(v_hi_done, 1)

            def q_stats(u, b, g):
                act.wait_ge(q_done, u + 1)
                reached(act, half_done, u - 1)
                reached(act, sumsq_done, u)
                for h in range(HG):
                    last = act.activation(junk[:, h * P:(h + 1) * P], q_ps[b % 2][:, h * P:(h + 1) * P],
                                          ACT.Square, accum_out=ss[:, b % 2, h:h + 1])
                last.then_inc(sumsq_done, 1)
                act.wait_ge(sumsq_done, u + 1)
                act.activation(lnss[:, b % 2, :], ss[:, b % 2, :], ACT.Ln, bias=qeps[:, 0:1]).then_inc(ln_done, 1)
                act.wait_ge(ln_done, u + 1)
                act.activation(seed[:, b % 2, :], lnss[:, b % 2, :], ACT.Exp, scale=-0.5).then_inc(seed_done, 1)

            run(act, [(oT_split, -2), (wq_split((0, 1)), 3), (exps, 0), (qT_copy, 1), (wq_split((2, )), 3),
                      (pT_split, -1), (wq_split((3, )), 3), (wo_split((0, 1)), -1), (v_split, 6), (q_stats, 2),
                      (wo_split((2, 3)), -1)])

        @block.gpsimd
        def _(pool):
            def v_split(u, b, g):
                pool.wait_ge(v_hi_done, u + 1)
                pool.tensor_tensor(v_lo[:, b, :], v_raw[:, b, :], v_hi[:, b, :].bitcast(F32), ALU.subtract)\
                    .then_inc(v_lo_done, 1)

            def normalize(u, b, g):
                pool.wait_ge(rsum_done, u + 1)
                pool.tensor_tensor(blocks(p_sb[:, b % 2, :]), blocks(p_sb[:, b % 2, :]),
                                   per_block(rsum[:, b % 2, :], P), ALU.mult).then_inc(p_done, 1)

            def wq_split(u, b, g):
                if b or (isinstance(g, int) and g == 0):
                    return
                for kt in (0, 1):
                    pool.wait_ge(wq_hi_done, 4 * g - 3 + kt)
                    pool.tensor_tensor(wq_lo[:, kt, :], wq_raw[:, kt, :], wq_hi[:, kt, :].bitcast(F32),
                                       ALU.subtract).then_inc(wq_pool_done, 1)

            def wo_split(u, b, g):
                if b:
                    return
                for h in (0, 1):
                    pool.wait_ge(wo_hi_done, 4 * g + h + 1)
                    pool.tensor_tensor(wo_lo[:, h, :], wo_raw[:, h, :], wo_hi[:, h, :].bitcast(F32),
                                       ALU.subtract).then_inc(wo_pool_done, 1)

            def q_rstd(u, b, g):
                pool.wait_ge(half_done, u + 1)
                pool.wait_ge(seed_done, u + 1)
                reached(pool, rstd_done, u)
                reached(pool, q_scaled, u - 1)
                newton_rsqrt(pool, newton, 3 * u, val[:, b % 2, :], seed[:, b % 2, :], tmp[:, b % 2, :],
                             rstd[:, b % 2, :], s.c15).then_inc(rstd_done, 1)

            run(pool, [(v_split, 6), (wq_split, 3), (normalize, 0), (wo_split, -1), (q_rstd, 2)])

        @block.vector
        def _(dve):
            dve.memset(qeps[:, :], P * EPS).then_inc(qeps_set, 1)
            for b in range(B):
                dve.memset(s.acc[:, b, :], 0.0).then_inc(acc_done, 1)

            def oT_split(u, b, g):
                dve.wait_ge(oT_hi_done, u + 1)
                dve.tensor_tensor(oT_lo[:, :], oT_ps[:, :], oT_hi[:, :].bitcast(F32), ALU.subtract)\
                    .then_inc(oT_lo_done, 1)

            def mask_max(u, b, g):
                dve.wait_ge(s_done, u + 1)
                if isinstance(u, int) and u == 0:
                    dve.wait_ge(mask_ld, 16)
                reached(dve, pT_done, u - 1)
                dve.tensor_tensor(blocks(p_sb[:, b % 2, :]), blocks(s_ps[:, :]),
                                  mask[:, :].unsqueeze(1).to_broadcast([P, HG, P]), ALU.add).then_inc(masked, 1)
                dve.wait_ge(masked, u + 1)
                dve.tensor_reduce(nmax[:, b % 2, :], blocks(p_sb[:, b % 2, :]), axis=AX_X, op=ALU.max,
                                  negate=True).then_inc(max_done, 1)

            def q_half(u, b, g):
                dve.wait_ge(sumsq_done, u + 1)
                reached(dve, rstd_done, u - 1)
                dve.tensor_scalar(val[:, b % 2, :], ss[:, b % 2, :], 0.5, 0.5 * P * EPS, ALU.mult, ALU.add)\
                    .then_inc(half_done, 1)

            def q_scale(u, b, g):
                dve.wait_ge(rstd_done, u + 1)
                reached(dve, qT_done, u - 1)
                dve.tensor_tensor(blocks(q_sb[:, b % 2, :]), blocks(q_ps[b % 2][:, :]),
                                  per_block(rstd[:, b % 2, :], P), ALU.mult).then_inc(q_scaled, 1)

            def p_recip(u, b, g):
                dve.wait_ge(exp_done, u + 1)
                reached(dve, p_done, u - 1)
                dve.reciprocal(rsum[:, b % 2, :], psum_[:, b % 2, :]).then_inc(rsum_done, 1)

            def pT_split(u, b, g):
                dve.wait_ge(pT_hi_done, u + 1)
                dve.tensor_tensor(pT_lo[:, :], pT_ps[:, :], pT_hi[:, :].bitcast(F32), ALU.subtract)\
                    .then_inc(pT_lo_done, 1)

            def wq_split(u, b, g):
                if b or (isinstance(g, int) and g == 0):
                    return
                for kt in (2, 3):
                    dve.wait_ge(wq_hi_done, 4 * g - 3 + kt)
                    dve.tensor_tensor(wq_lo[:, kt, :], wq_raw[:, kt, :], wq_hi[:, kt, :].bitcast(F32),
                                      ALU.subtract).then_inc(wq_dve_done, 1)

            def wo_split(u, b, g):
                if b:
                    return
                for h in (2, 3):
                    dve.wait_ge(wo_hi_done, 4 * g + h + 1)
                    dve.tensor_tensor(wo_lo[:, h, :], wo_raw[:, h, :], wo_hi[:, h, :].bitcast(F32),
                                      ALU.subtract).then_inc(wo_dve_done, 1)

            def accumulate(u, b, g):
                dve.wait_ge(o_done, u + 1)
                dve.wait_ge(acc_done, u + 1)
                dve.tensor_tensor(s.acc[:, b, :], o_ps[b % 2][:, :], s.acc[:, b, :], ALU.add)\
                    .then_inc(acc_done, 1)
                if isinstance(g, int) and g == G - 1:
                    dve.wait_ge(acc_done, B + u + 1)
                    dve.scalar_tensor_tensor(out=s.x[:, b, :], in0=s.acc[:, b, :], scalar=s.tgates[:, 0:1],
                                             in1=s.x[:, b, :], op0=ALU.mult, op1=ALU.add).then_inc(x_step, 1)
                    dve.wait_ge(x_step, 3 * b + 1)
                    layernorm_stats(dve, s, b, x_step, 3 * b + 1).then_inc(x_step, 1)

            run(dve, [(oT_split, -2), (mask_max, 0), (q_scale, 1), (p_recip, 0), (pT_split, -1), (wq_split, 3),
                      (q_half, 2), (accumulate, -2), (wo_split, -1)])
            layernorm_half_var(dve, s, x_step, 3 * B)

        @block.tensor
        def _(pe):
            def scores(u, b, g):
                pe.wait_ge(qT_copied, u + 1)
                if b % 4 == 0:
                    pe.wait_ge(kT_ld[b // 4], 16 * g + 16)
                reached(pe, masked, u)
                for h in range(HG):
                    last = pe.matmul(s_ps[:, h * P:(h + 1) * P], qT_sb[:, b % 2, h * P:(h + 1) * P],
                                     kT[:, b * P:(b + 1) * P], start=True, stop=True)
                last.then_inc(s_done, 1)

            def q_proj(u, b, g):
                reached(pe, q_scaled, u - 1)
                for kt in range(KT):
                    if b == 0:
                        if kt < 2:
                            reached(pe, wq_pool_done, 2 * g - 1 + kt if not isinstance(g, int) or g else 0)
                        else:
                            reached(pe, wq_dve_done, 2 * g - 3 + kt if not isinstance(g, int) or g else 0)
                    xh, xl = s.xT_hi[:, kt, b * P:(b + 1) * P], s.xT_lo[:, kt, b * P:(b + 1) * P]
                    pe.matmul(q_ps[b % 2][:, :], xh, wq_hi[:, kt, :], start=(kt == 0), stop=False)
                    pe.matmul(q_ps[b % 2][:, :], xl, wq_hi[:, kt, :], start=False, stop=False)
                    last = pe.matmul(q_ps[b % 2][:, :], xh, wq_lo[:, kt, :], start=False, stop=(kt == KT - 1))
                    if b == B - 1 and kt < KT - 1:
                        last.then_inc(wq_used, 1)
                last.then_inc(q_done, 1)

            def q_transpose(u, b, g):
                pe.wait_ge(q_scaled, u + 1)
                reached(pe, qT_copied, u)
                for h in range(HG):
                    last = pe.transpose(qT_ps[:, h * P:(h + 1) * P], q_sb[:, b % 2, h * P:(h + 1) * P],
                                        s.ident[:, :])
                last.then_inc(qT_done, 1)

            def p_transpose(u, b, g):
                pe.wait_ge(p_done, u + 1)
                reached(pe, pT_lo_done, u)
                for h in range(HG):
                    last = pe.transpose(pT_ps[:, h * P:(h + 1) * P], p_sb[:, b % 2, h * P:(h + 1) * P],
                                        s.ident[:, :])
                last.then_inc(pT_done, 1)

            def o_proj(u, b, g):
                pe.wait_ge(oT_lo_done, u + 1)
                reached(pe, acc_done, B + u - 1)
                for h in range(HG):
                    if b == 0:
                        pe.wait_ge(wo_pool_done if h < 2 else wo_dve_done, 2 * g + h % 2 + 1)
                    oh, ol = oT_hi[:, h * P:(h + 1) * P], oT_lo[:, h * P:(h + 1) * P]
                    pe.matmul(o_ps[b % 2][:, :], oh, wo_hi[:, h, :], start=(h == 0), stop=False)
                    pe.matmul(o_ps[b % 2][:, :], ol, wo_hi[:, h, :], start=False, stop=False)
                    last = pe.matmul(o_ps[b % 2][:, :], oh, wo_lo[:, h, :], start=False, stop=(h == HG - 1))
                    if b == B - 1 and h < HG - 1:
                        last.then_inc(wo_used, 1)
                last.then_inc(o_done, 1)

            def values(u, b, g):
                pe.wait_ge(pT_lo_done, u + 1)
                pe.wait_ge(v_lo_done, u + 1)
                reached(pe, oT_lo_done, u)
                pe.matmul(oT_ps[:, :], v_hi[:, b, :], pT_hi[:, :], start=True, stop=False)
                pe.matmul(oT_ps[:, :], v_lo[:, b, :], pT_hi[:, :], start=False, stop=False)
                pe.matmul(oT_ps[:, :], v_hi[:, b, :], pT_lo[:, :], start=False, stop=True).then_inc(pv_done, 1)

            run(pe, [(scores, 0), (q_proj, 2), (q_transpose, 1), (p_transpose, -1), (o_proj, -2), (values, -1)])

        stage.close()
        m.clear_sems()


def feed_forward(nc, d, s):
    with ExitStack() as ctx:
        m = Mem(nc, ctx)
        xln = m.sb("xln2", [P, B, D])
        mv, xval, xseed = s.mv, s.xval, m.sb("xseed2", [P, B])
        xtmp, xrstd = m.sb("xtmp2", [P, B]), m.sb("xrstd2", [P, B])
        perm_rowi, perm_coli = m.sb("perm_rowi", [P, D], I32), m.sb("perm_coli", [P, KT], I32)
        perm_row, perm_col = m.sb("perm_row", [P, D]), m.sb("perm_col", [P, KT])
        iota_row, iota_col = m.sb("iota_row", [P, D]), m.sb("iota_col", [P, KT])
        pick = m.sb("pick", [P, KT, D], F32R)
        pickT = m.sb("pickT", [P, KT, D], F32R)
        up_raw = m.sb("up_raw", [P, KT, P])
        up_hi, up_lo = m.sb("up_hi", [P, KT, P], F32R), m.sb("up_lo", [P, KT, P], F32R)
        down = m.sb("down", [P, D])
        xp_hi, xp_lo = m.sb("xp_hi", [P, KT, T], F32R), m.sb("xp_lo", [P, KT, T], F32R)
        hid = m.sb("hid", [P, 3, HALF])
        yT_hi, yT_lo = m.sb("yT_hi", [P, KT, T], F32R), m.sb("yT_lo", [P, KT, T], F32R)

        perm_ld, up_ld, down_ld = m.sem("perm_ld"), m.sem("up_ld"), m.sem("down_ld")
        xln_ln, xseed_done, xrstd_done = m.sem("xln2_ln"), m.sem("xseed2_done"), m.sem("xrstd2_done")
        newton, xln_done = m.sem("newton2"), m.sem("xln2_done")
        xT_done, xT_hi_done, xT_lo_done = m.sem("xT2_done"), m.sem("xT2_hi_done"), m.sem("xT2_lo_done")
        pick_step, pick_done = m.sem("pick_step"), m.sem("pick_done")
        up_hi_done, up_lo_done = m.sem("up_hi_done"), m.sem("up_lo_done")
        xp_done, xp_copied = m.sem("xp_done"), [m.sem("xp_hi_copied"), m.sem("xp_lo_copied")]
        up_done, gelu_done, down_done = m.sem("up_done"), m.sem("gelu_done"), m.sem("down_done")
        yT_hi_done, yT_lo_done = m.sem("yT_hi_done"), m.sem("yT_lo_done")
        y_done, x_done = m.sem("y_done"), m.sem("x2_done")
        xT_ps, xp_ps, up_ps, yT_ps = s.ps[0:2], s.ps[2:4], s.ps[4:6], s.ps[6:8]
        y_ps = s.ps[0:2]
        HB = B // 2

        stage = ExitStack()
        block = stage.enter_context(nc.Block())

        @block.sync
        def _(sp):
            sp.dma_start(perm_rowi[:, :], d.perm_row).then_inc(perm_ld, 16)
            sp.dma_start(perm_coli[:, :], d.perm_col).then_inc(perm_ld, 16)
            sp.dma_start(iota_row[:, :], d.iota_row).then_inc(perm_ld, 16)
            sp.dma_start(iota_col[:, :], d.iota_col).then_inc(perm_ld, 16)
            sp.dma_start(up_raw[:, :, :], d.up).then_inc(up_ld, 16)
            sp.dma_start(down[:, :], d.down).then_inc(down_ld, 16)

        @block.scalar
        def _(act):
            act.wait_ge(up_ld, 16)
            act.activation(up_hi[:, :, :], up_raw[:, :, :], ACT.Copy).then_inc(up_hi_done, 1)
            for c in range(2):
                cols = slice(c * HB, (c + 1) * HB)
                act.activation(xtmp[:, cols], xval[:, cols], ACT.Ln, scale=2.0).then_inc(xln_ln, 1)
                act.wait_ge(xln_ln, c + 1)
                act.activation(xseed[:, cols], xtmp[:, cols], ACT.Exp, scale=-0.5).then_inc(xseed_done, 1)
            for b in range(B):
                act.wait_ge(xT_done, b + 1)
                act.activation(s.xT_hi[:, :, b * P:(b + 1) * P], blocks(xT_ps[b % 2][:, :]), ACT.Copy)\
                    .then_inc(xT_hi_done, 1)
            for n in range(2 * KT):
                c, jt = divmod(n, KT)
                act.wait_ge(xp_done, 2 * n + 1)
                act.activation(xp_hi[:, jt, c * HALF:(c + 1) * HALF], xp_ps[0][:, :], ACT.Copy)\
                    .then_inc(xp_copied[0], 1)
            for n in range(2 * FH):
                act.wait_ge(up_done, n + 1)
                reached(act, down_done, n - 2)
                act.activation(hid[:, n % 3, :], up_ps[n % 2][:, :], ACT.Gelu).then_inc(gelu_done, 1)
                ready = [n // HG - 1] if n % HG == 0 and n % FH else []
                ready += [n // HG] if n % FH == FH - 1 else []
                for k in ready:
                    c, jt = divmod(k, KT)
                    act.wait_ge(down_done, HG * (k + 1))
                    act.activation(yT_hi[:, jt, c * HALF:(c + 1) * HALF], yT_ps[k % 2][:, :], ACT.Copy)\
                        .then_inc(yT_hi_done, 1)

        @block.gpsimd
        def _(pool):
            pool.wait_ge(perm_ld, 16 * 4)
            pool.tensor_copy(perm_row[:, :], perm_rowi[:, :]).then_inc(pick_step, 1)
            pool.tensor_copy(perm_col[:, :], perm_coli[:, :]).then_inc(pick_step, 1)
            pool.wait_ge(pick_step, 2)
            for kt in range(KT):
                pool.tensor_scalar(pick[:, kt, :], perm_row[:, :], iota_col[:, kt:kt + 1], None, ALU.is_equal)\
                    .then_inc(pick_done, 1)
            for c in range(2):
                cols = slice(c * HB, (c + 1) * HB)
                pool.wait_ge(xseed_done, c + 1)
                newton_rsqrt(pool, newton, 3 * c, xval[:, cols], xseed[:, cols], xtmp[:, cols], xrstd[:, cols],
                             s.c15)\
                    .then_inc(xrstd_done, 1)
            for jt in range(KT):
                pool.tensor_scalar(pickT[:, jt, :], iota_row[:, :], perm_col[:, jt:jt + 1], None, ALU.is_equal)\
                    .then_inc(pick_done, 1)

        @block.vector
        def _(dve):
            dve.wait_ge(up_hi_done, 1)
            dve.tensor_tensor(up_lo[:, :, :], up_raw[:, :, :], up_hi[:, :, :].bitcast(F32), ALU.subtract)\
                .then_inc(up_lo_done, 1)
            for b in range(B):
                dve.wait_ge(xrstd_done, b // HB + 1)
                dve.tensor_scalar(xln[:, b, :], s.x[:, b, :], mv[:, b, 0:1], xrstd[:, b:b + 1],
                                  ALU.subtract, ALU.mult).then_inc(xln_done, 1)
            for b in range(B):
                dve.wait_ge(xT_hi_done, b + 1)
                dve.tensor_tensor(s.xT_lo[:, :, b * P:(b + 1) * P], blocks(xT_ps[b % 2][:, :]),
                                  s.xT_hi[:, :, b * P:(b + 1) * P].bitcast(F32), ALU.subtract)\
                    .then_inc(xT_lo_done, 1)
            for n in range(2 * KT):
                c, jt = divmod(n, KT)
                dve.wait_ge(xp_done, 2 * n + 2)
                dve.tensor_copy(xp_lo[:, jt, c * HALF:(c + 1) * HALF], xp_ps[1][:, :]).then_inc(xp_copied[1], 1)
            for c in range(2):
                for jt in range(KT):
                    k = c * KT + jt
                    dve.wait_ge(yT_hi_done, k + 1)
                    dve.tensor_tensor(yT_lo[:, jt, c * HALF:(c + 1) * HALF], yT_ps[k % 2][:, :],
                                      yT_hi[:, jt, c * HALF:(c + 1) * HALF].bitcast(F32), ALU.subtract)\
                        .then_inc(yT_lo_done, 1)
                for b in range(c * HB, (c + 1) * HB):
                    dve.wait_ge(y_done, b + 1)
                    dve.scalar_tensor_tensor(out=s.x[:, b, :], in0=y_ps[b % 2][:, :], scalar=s.tgates[:, 2:3],
                                             in1=s.x[:, b, :], op0=ALU.mult, op1=ALU.add).then_inc(x_done, 1)

        @block.tensor
        def _(pe):
            for b in range(B):
                pe.wait_ge(xln_done, b + 1)
                reached(pe, xT_lo_done, b - 1)
                for kt in range(KT):
                    last = pe.transpose(xT_ps[b % 2][:, kt * P:(kt + 1) * P], xln[:, b, kt * P:(kt + 1) * P],
                                        s.ident[:, :])
                last.then_inc(xT_done, 1)
            pe.wait_ge(pick_done, KT)
            for n in range(2 * KT):
                c, jt = divmod(n, KT)
                pe.wait_ge(xT_lo_done, HB * (c + 1))
                for part, xT in enumerate((s.xT_hi, s.xT_lo)):
                    reached(pe, xp_copied[part], n)
                    for kt in range(KT):
                        last = pe.matmul(xp_ps[part][:, :], pick[:, kt, jt * P:(jt + 1) * P],
                                         xT[:, kt, c * HALF:(c + 1) * HALF], start=(kt == 0), stop=(kt == KT - 1))
                    last.then_inc(xp_done, 1)
            pe.wait_ge(up_lo_done, 1)
            pe.wait_ge(down_ld, 16)
            for c in range(2):
                half = slice(c * HALF, (c + 1) * HALF)
                for h in range(FH + 1):
                    if h < FH:
                        n, jt, rows = c * FH + h, h // HG, slice(FD * (h % HG), FD * (h % HG + 1))
                        pe.wait_ge(xp_copied[0], c * KT + jt + 1)
                        pe.wait_ge(xp_copied[1], c * KT + jt + 1)
                        reached(pe, gelu_done, n - 1)
                        out = up_ps[n % 2][:, :]
                        pe.matmul(out, up_hi[rows, jt, :], xp_hi[rows, jt, half], start=True, stop=False)
                        pe.matmul(out, up_lo[rows, jt, :], xp_hi[rows, jt, half], start=False, stop=False)
                        pe.matmul(out, up_hi[rows, jt, :], xp_lo[rows, jt, half], start=False, stop=True)\
                            .then_inc(up_done, 1)
                    if h >= 1:
                        hh = h - 1
                        n, k, rows = c * FH + hh, c * KT + hh // HG, slice(FD * (hh % HG), FD * (hh % HG + 1))
                        pe.wait_ge(gelu_done, n + 1)
                        if hh % HG == 0:
                            reached(pe, yT_lo_done, k - 1)
                        pe.matmul(yT_ps[k % 2][rows, :], down[:, hh * FD:(hh + 1) * FD], hid[:, n % 3, :],
                                  start=True, stop=True).then_inc(down_done, 1)
                pe.wait_ge(pick_done, 2 * KT)
                pe.wait_ge(yT_lo_done, KT * (c + 1))
                for b in range(c * HB, (c + 1) * HB):
                    reached(pe, x_done, b - 1)
                    for jt in range(KT):
                        pe.matmul(y_ps[b % 2][:, :], yT_hi[:, jt, b * P:(b + 1) * P], pickT[:, jt, :],
                                  start=(jt == 0), stop=False)
                        last = pe.matmul(y_ps[b % 2][:, :], yT_lo[:, jt, b * P:(b + 1) * P], pickT[:, jt, :],
                                         start=False, stop=(jt == KT - 1))
                    last.then_inc(y_done, 1)

        stage.close()


def nonlocal_attention(nc, d, s):
    with ExitStack() as ctx:
        m = Mem(nc, ctx)
        xln = m.sb("xln3", [P, B, D])
        mv, xval, xseed = s.mv, s.xval, m.sb("xseed3", [P, B])
        xtmp, xrstd = m.sb("xtmp3", [P, B]), m.sb("xrstd3", [P, B])
        wt, wzT = m.sb("wt", [P, P]), m.sb("wzT", [P, P])
        wgT, wpT, mT = m.sb("wgT", [P, P]), m.sb("wpT", [P, P]), m.sb("mT", [P, P])
        group_mean = m.sb("group_mean", [P, P])
        gn_w, gn_b = m.sb("gn_w", [P, 1]), m.sb("gn_b", [P, 1])
        z = m.sb("z", [P, B, D])
        y = m.sb("y", [P, B, D])
        g_sb = m.sb("g_sb", [P, 2, D])
        prod = m.sb("prod", [P, 2, D])
        zbn, zmv = m.sb("zbn", [P, B, 6]), m.sb("zmv", [P, B, 2])
        row = m.sb("att_row", [P, B])
        gmean, dev, att = m.sb("gmean", [P, B]), m.sb("dev", [P, B]), m.sb("att", [P, B])
        gvar, yval = m.sb("gvar", [P, B]), m.sb("yval", [P, B])
        yln, yseed, ytmp, yrstd = (m.sb(n, [P, B]) for n in ("yln", "yseed", "ytmp", "yrstd"))
        a_col, b_col, tw, tb = m.sb("a_col", [P, B]), m.sb("b_col", [P, B]), m.sb("tw", [P, 1]), m.sb("tb", [P, 1])

        zero, zero_set, zero_stored = m.sb("zero", [P, D]), m.sem("zero_set"), m.sem("zero_stored")
        w_ld = m.sem("l1w_ld")
        x_step, xval_done = m.sem("x3_step"), m.sem("xval3_done")
        xln_ln, xseed_done, xrstd_done = m.sem("xln3_ln"), m.sem("xseed3_done"), m.sem("xrstd3_done")
        newton, xln_done = m.sem("newton3"), m.sem("xln3_done")
        mT_done, mT_copied = m.sem("mT_done"), m.sem("mT_copied")
        z_done, z_copied, g_done, g_copied = m.sem("z_done"), m.sem("z_copied"), m.sem("g_done"), m.sem("g_copied")
        p_done, row_done, zstat_step = m.sem("pp_done"), m.sem("row_done"), m.sem("zstat_step")
        gmean_done, dev_step, gvar_done = m.sem("gmean_done"), m.sem("dev_step"), m.sem("gvar_done")
        att_done, col_step, yval_done = m.sem("att_done"), m.sem("col_step"), m.sem("yval_done")
        yln_done, yseed_done, yrstd_done = m.sem("yln_done"), m.sem("yseed_done"), m.sem("yrstd_done")
        y_done, res_done, x_done = m.sem("yy_done"), m.sem("res_done"), m.sem("x3_done")
        z_ps, g_ps, p_ps, sm_ps, att_ps = s.ps[0:2], s.ps[2:4], s.ps[4:6], s.ps[6], s.ps[7]
        LOADS = 7

        stage = ExitStack()
        block = stage.enter_context(nc.Block())

        @block.sync
        def _(sp):
            for dst, src in ((wt, d.wt), (wzT, d.wzT), (wgT, d.wgT), (wpT, d.wpT), (group_mean, d.group_mean),
                             (gn_w, d.gn_w), (gn_b, d.gn_b)):
                sp.dma_start(dst[:, :], src).then_inc(w_ld, 16)
            sp.wait_ge(zero_set, 1)
            sp.dma_start(d.sorted_x.rearrange("t p n -> p t n"),
                         zero[:, :].unsqueeze(1).to_broadcast([P, SORTED, D])).then_inc(zero_stored, 16)
            for e in range(E):
                sp.dma_start(s.exp_w[:, e, :, :], d.exp_w[e]).then_inc(s.exp_ld, 16)
            sp.wait_ge(zero_stored, 16)

        @block.scalar
        def _(act):
            act.preload_act_table_set(LN_EXP_SET)
            act.wait_ge(mT_done, 1)
            act.activation(mT[:, :], sm_ps[:, 0:P], ACT.Copy).then_inc(mT_copied, 1)
            for b in range(B):
                act.wait_ge(z_done, b + 1)
                act.activation(z[:, b, :], z_ps[b % 2][:, :], ACT.Copy).then_inc(z_copied, 1)
                if b == 1:
                    act.wait_ge(xval_done, 1)
                    act.activation(xtmp[:, :], xval[:, :], ACT.Ln, scale=2.0).then_inc(xln_ln, 1)
                    act.wait_ge(xln_ln, 1)
                    act.activation(xseed[:, :], xtmp[:, :], ACT.Exp, scale=-0.5).then_inc(xseed_done, 1)
            for b in range(B):
                act.wait_ge(g_done, b + 1)
                reached(act, row_done, b - 1)
                act.activation(g_sb[:, b % 2, :], g_ps[b % 2][:, :], ACT.Copy).then_inc(g_copied, 1)
            act.wait_ge(yval_done, 1)
            act.activation(yln[:, :], yval[:, :], ACT.Ln, scale=2.0).then_inc(yln_done, 1)
            act.wait_ge(yln_done, 1)
            act.activation(yseed[:, :], yln[:, :], ACT.Exp, scale=-0.5).then_inc(yseed_done, 1)
            act.wait_ge(col_step, 4)
            for b in range(B):
                act.activation(y[:, b, :], z[:, b, :], ACT.Identity, bias=b_col[:, b:b + 1],
                               scale=a_col[:, b:b + 1]).then_inc(y_done, 1)

        @block.gpsimd
        def _(pool):
            pool.memset(zero[:, :], 0.0).then_inc(zero_set, 1)
            pool.wait_ge(xseed_done, 1)
            newton_rsqrt(pool, newton, 0, xval[:, :], xseed[:, :], xtmp[:, :], xrstd[:, :], s.c15).then_inc(xrstd_done, 1)
            pool.wait_ge(yseed_done, 1)
            newton_rsqrt(pool, newton, 3, yval[:, :], yseed[:, :], ytmp[:, :], yrstd[:, :], s.c15).then_inc(yrstd_done, 1)

        @block.vector
        def _(dve):
            for b in range(B):
                layernorm_stats(dve, s, b, x_step, 2 * b).then_inc(x_step, 1)
            dve.wait_ge(x_step, 2 * B)
            dve.tensor_scalar(xval[:, :], mv[:, :, 1], EPS, 0.5, ALU.add, ALU.mult).then_inc(xval_done, 1)
            dve.wait_ge(w_ld, 16 * LOADS)
            dve.tensor_tensor(tw[:, :], gn_w[:, :], s.tgates[:, 1:2], ALU.mult).then_inc(col_step, 1)
            dve.tensor_tensor(tb[:, :], gn_b[:, :], s.tgates[:, 1:2], ALU.mult).then_inc(col_step, 1)
            for b in range(B):
                dve.wait_ge(z_copied, b + 1)
                dve.bn_stats(zbn[:, b, :], z[:, b, :]).then_inc(zstat_step, 1)
                dve.wait_ge(zstat_step, 2 * b + 1)
                dve.bn_aggr(zmv[:, b, :], zbn[:, b, :]).then_inc(zstat_step, 1)
            dve.wait_ge(xrstd_done, 1)
            for b in range(B):
                dve.tensor_scalar(xln[:, b, :], s.x[:, b, :], mv[:, b, 0:1], xrstd[:, b:b + 1],
                                  ALU.subtract, ALU.mult).then_inc(xln_done, 1)
            dve.wait_ge(gmean_done, 1)
            dve.tensor_copy(gmean[:, :], sm_ps[:, 128:128 + B]).then_inc(dev_step, 1)
            dve.wait_ge(dev_step, 1)
            dve.tensor_tensor(dev[:, :], zmv[:, :, 0], gmean[:, :], ALU.subtract).then_inc(dev_step, 1)
            dve.wait_ge(dev_step, 2)
            dve.tensor_tensor(dev[:, :], dev[:, :], dev[:, :], ALU.mult).then_inc(dev_step, 1)
            dve.wait_ge(dev_step, 3)
            dve.tensor_tensor(dev[:, :], dev[:, :], zmv[:, :, 1], ALU.add).then_inc(dev_step, 1)
            dve.wait_ge(gvar_done, 1)
            dve.tensor_copy(gvar[:, :], sm_ps[:, 256:256 + B]).then_inc(dev_step, 1)
            for b in range(B):
                dve.wait_ge(g_copied, b + 1)
                dve.wait_ge(p_done, b + 1)
                reached(dve, row_done, b - 1)
                dve.tensor_tensor_reduce(out=prod[:, b % 2, :], in0=p_ps[b % 2][:, :], in1=g_sb[:, b % 2, :],
                                         scale=1.0, scalar=0.0, op0=ALU.mult, op1=ALU.add,
                                         accum_out=row[:, b:b + 1]).then_inc(row_done, 1)
            for b in range(B):
                dve.scalar_tensor_tensor(out=s.x[:, b, :], in0=s.ctx_nat[:, b, :], scalar=s.tgates[:, 1:2],
                                         in1=s.x[:, b, :], op0=ALU.mult, op1=ALU.add).then_inc(res_done, 1)
                if b == 1:
                    dve.wait_ge(att_done, 1)
                    dve.wait_ge(dev_step, 5)
                    dve.tensor_scalar(att[:, :], att_ps[:, 0:B], 16.0, None, ALU.mult).then_inc(dev_step, 1)
                    dve.wait_ge(dev_step, 6)
                    dve.tensor_tensor(yval[:, :], att[:, :], att[:, :], ALU.mult).then_inc(dev_step, 1)
                    dve.wait_ge(dev_step, 7)
                    dve.tensor_tensor(yval[:, :], yval[:, :], gvar[:, :], ALU.mult).then_inc(dev_step, 1)
                    dve.wait_ge(dev_step, 8)
                    dve.tensor_scalar(yval[:, :], yval[:, :], EPS, 0.5, ALU.add, ALU.mult).then_inc(yval_done, 1)
                    dve.wait_ge(col_step, 2)
                    dve.tensor_scalar(att[:, :], att[:, :], tw[:, 0:1], None, ALU.mult).then_inc(dev_step, 1)
            dve.wait_ge(yrstd_done, 1)
            dve.wait_ge(dev_step, 9)
            dve.tensor_tensor(a_col[:, :], att[:, :], yrstd[:, :], ALU.mult).then_inc(col_step, 1)
            dve.wait_ge(col_step, 3)
            dve.tensor_tensor(b_col[:, :], a_col[:, :], gmean[:, :], ALU.mult).then_inc(dev_step, 1)
            dve.wait_ge(dev_step, 10)
            dve.tensor_scalar(b_col[:, :], b_col[:, :], -1.0, tb[:, 0:1], ALU.mult, ALU.add).then_inc(col_step, 1)
            for b in range(B):
                dve.wait_ge(y_done, b + 1)
                dve.wait_ge(res_done, b + 1)
                dve.tensor_tensor(s.x[:, b, :], s.x[:, b, :], y[:, b, :], ALU.add).then_inc(x_done, 1)

        @block.tensor
        def _(pe):
            pe.wait_ge(w_ld, 16 * LOADS)
            pe.matmul(sm_ps[:, 0:P], wt[:, :], wzT[:, :], start=True, stop=True).then_inc(mT_done, 1)
            pe.wait_ge(mT_copied, 1)
            for b in range(B):
                reached(pe, z_copied, b - 1)
                pe.matmul(z_ps[b % 2][:, :], mT[:, :], s.ctx_nat[:, b, :], start=True, stop=True).then_inc(z_done, 1)
            for b in range(B):
                reached(pe, g_copied, b - 1)
                pe.matmul(g_ps[b % 2][:, :], wgT[:, :], s.ctx_nat[:, b, :], start=True, stop=True)\
                    .then_inc(g_done, 1)
                if b == 1:
                    pe.wait_ge(zstat_step, 2 * B)
                    pe.matmul(sm_ps[:, 128:128 + B], group_mean[:, :], zmv[:, :, 0], start=True, stop=True)\
                        .then_inc(gmean_done, 1)
                pe.wait_ge(xln_done, b + 1)
                reached(pe, row_done, b - 1)
                pe.matmul(p_ps[b % 2][:, :], wpT[:, :], xln[:, b, :], start=True, stop=True).then_inc(p_done, 1)
                if b == 1:
                    pe.wait_ge(dev_step, 4)
                    pe.matmul(sm_ps[:, 256:256 + B], group_mean[:, :], dev[:, :], start=True, stop=True)\
                        .then_inc(gvar_done, 1)
            pe.wait_ge(row_done, B)
            pe.matmul(att_ps[:, 0:B], group_mean[:, :], row[:, :], start=True, stop=True).then_inc(att_done, 1)

        stage.close()


def experts(nc, d, s):
    with ExitStack() as ctx:
        m = Mem(nc, ctx)
        xln = m.sb("xln4", [P, B, D])
        mv, xval, xseed = s.mv, s.xval, m.sb("xseed4", [P, B])
        xtmp, xrstd = m.sb("xtmp4", [P, B]), m.sb("xrstd4", [P, B])
        xT = m.sb("xT4", [P, 2, D])
        gate_w = m.sb("gate_w", [P, KT, E])
        gate_b, eid = m.sb("gate_b", [P, E]), m.sb("eid", [P, SORTED])
        rows_before, upto = m.sb("rows_before", [P, P]), m.sb("upto", [P, E, E])
        ones, steps = m.sb("ones", [P, P]), m.sb("steps", [P, B])
        exp_b = m.sb("exp_b", [E, D])
        logit, top = m.sb("logit", [P, B, E]), m.sb("top", [P, B])
        cand, first = m.sb("cand", [P, B, E]), m.sb("first", [P, B])
        hot, hot_sum = m.sb("hot", [P, B, E]), m.sb("hot_sum", [P, E])
        hotT = m.sb("hotT", [E, B, P])
        fuller, tiles = m.sb("fuller", [P, E, B]), m.sb("tiles", [P, E])
        below, end, begin = m.sb("below", [P, E, E]), m.sb("end", [P, E]), m.sb("begin", [P, E])
        place, pos = m.sb("place", [P, B, E]), m.sb("pos", [P, B])
        pos_i = m.sb("pos_i", [P, B], I32)
        past, tile_e = m.sb("past", [P, SORTED, E]), m.sb("tile_e", [P, SORTED])
        tile_i = m.sb("tile_i", [P, SORTED], I32)
        xs, xsT = m.sb("xs", [P, 3, D]), m.sb("xsT", [P, 3, D])
        ys, y_tok = m.sb("ys", [P, 3, D]), s.acc

        small_ld = m.sem("gate_ld")
        ones_set = m.sem("ones_set")
        x_step, xval_done = m.sem("x4_step"), m.sem("xval4_done")
        xln_ln, xseed_done, xrstd_done = m.sem("xln4_ln"), m.sem("xseed4_done"), m.sem("xrstd4_done")
        newton, xln_done = m.sem("newton4"), m.sem("xln4_done")
        xT_done, xT_copied = m.sem("xT4_done"), m.sem("xT4_copied")
        logit_done, gate_step, hot_done = m.sem("logit_done"), m.sem("gate_step"), m.sem("hot_done")
        hot_summed, rank_done, count_done = m.sem("hot_summed"), m.sem("rank_done"), m.sem("count_done")
        pos_done, tile_done, scattered = m.sem("pos_done"), m.sem("tile_done"), m.sem("scattered")
        hotT_done, hotT_copied, bias_done = m.sem("hotT_done"), m.sem("hotT_copied"), m.sem("bias_done")
        bias_added = m.sem("bias_added")
        xs_ld = [m.sem(f"xs_ld{i}") for i in range(3)]
        xsT_done, xsT_copied = m.sem("xsT_done"), m.sem("xsT_copied")
        y_done, y_copied = m.sem("ey_done"), m.sem("ey_copied")
        y_stored = [m.sem(f"y_stored{i}") for i in range(3)]
        gathered, x_done, stored = [m.sem(f"gathered{b}") for b in range(B)], m.sem("x4_done"), m.sem("stored")
        xT_ps, logit_ps, rank_ps, hotT_ps = s.ps[0:2], s.ps[2], s.ps[3], s.ps[4:6]
        bias_ps = s.ps[6:8]
        xsT_ps, y_ps = s.ps[0:3], s.ps[3:6]
        LOADS = 6
        HB = B // 2

        def run(eng, stages):

            def step(r, j):
                for stage, ahead in stages:
                    t = 3 * r + j + ahead
                    if not isinstance(t, int) or 0 <= t < SORTED:
                        stage(t, (j + ahead) % 3, r + (j + ahead) // 3)

            for j in range(3):
                step(-1, j)
            for j in range(3):
                step(0, j)
            with eng.Fori(1, SORTED // 3 - 1) as r:
                for j in range(3):
                    step(r, j)
            for j in range(3):
                step(SORTED // 3 - 1, j)
            for j in range(3):
                step(SORTED // 3, j)

        stage = ExitStack()
        block = stage.enter_context(nc.Block())

        @block.sync
        def _(sp):
            for dst, src in ((gate_w[:, :, :], d.gate_w), (gate_b[:, :], d.gate_b), (eid[:, :], d.eid),
                             (rows_before[:, :], d.rows_before), (upto[:, :, :], d.upto), (exp_b[:, :], d.exp_b)):
                sp.dma_start(dst, src).then_inc(small_ld, 16)
            sp.wait_ge(scattered, 16 * B)

            def load(t, slot, r):
                reached(sp, xsT_done, t - 2)
                sp.dma_start(xs[:, slot, :], d.sorted_x[t, :, :]).then_inc(xs_ld[slot], 16)

            def store(t, slot, r):
                sp.wait_ge(y_copied, t + 1)
                sp.dma_start(d.sorted_y[t, :, :], ys[:, slot, :]).then_inc(y_stored[slot], 16)

            run(sp, [(load, 2), (store, -1)])
            for b in range(B):
                sp.wait_ge(x_done, b + 1)
                sp.dma_start(d.out[:, b, :], s.x[:, b, :]).then_inc(stored, 16)
            sp.wait_ge(stored, 16 * B)

        @block.scalar
        def _(act):
            for c in range(2):
                cols = slice(c * HB, (c + 1) * HB)
                act.wait_ge(xval_done, c + 1)
                act.activation(xtmp[:, cols], xval[:, cols], ACT.Ln, scale=2.0).then_inc(xln_ln, 1)
                act.wait_ge(xln_ln, c + 1)
                act.activation(xseed[:, cols], xtmp[:, cols], ACT.Exp, scale=-0.5).then_inc(xseed_done, 1)
            for b in range(B):
                act.wait_ge(xT_done, b + 1)
                act.activation(xT[:, b % 2, :], xT_ps[b % 2][:, :], ACT.Copy).then_inc(xT_copied, 1)
            for k in range(2):
                act.wait_ge(hotT_done, k + 1)
                act.activation(hotT[:, k * HB:(k + 1) * HB, :], blocks(hotT_ps[k][0:E, :]), ACT.Copy,
                               scale=s.tgates[0:E, 3:4]).then_inc(hotT_copied, 1)

            def copy_xsT(t, slot, r):
                act.wait_ge(xsT_done, t + 1)
                reached(act, y_done, t - 2)
                act.activation(xsT[:, slot, :], xsT_ps[slot][:, :], ACT.Copy).then_inc(xsT_copied, 1)

            run(act, [(copy_xsT, 1)])

        @block.gpsimd
        def _(pool):
            for c in range(2):
                cols = slice(c * HB, (c + 1) * HB)
                pool.wait_ge(xseed_done, c + 1)
                newton_rsqrt(pool, newton, 3 * c, xval[:, cols], xseed[:, cols], xtmp[:, cols], xrstd[:, cols],
                             s.c15)\
                    .then_inc(xrstd_done, 1)
            pool.wait_ge(pos_done, 1)
            for b in range(B):
                pool.indirect_dma_start(out=d.sorted_x_rows, out_offset=IndirectOffsetOnAxis(ap=pos_i[:, b:b + 1], axis=0),
                                        in_=xln[:, b, :], in_offset=None).then_inc(scattered, 16)
            for i in range(3):
                pool.wait_ge(y_stored[i], 16 * (SORTED // 3))
            for b in range(B):
                pool.indirect_dma_start(out=y_tok[:, b, :], out_offset=None, in_=d.sorted_y_rows,
                                        in_offset=IndirectOffsetOnAxis(ap=pos_i[:, b:b + 1], axis=0))\
                    .then_inc(gathered[b], 16)

        @block.vector
        def _(dve):
            dve.memset(ones[:, :], 1.0).then_inc(ones_set, 1)
            for k in range(B):
                dve.memset(steps[:, k:k + 1], float(P * k)).then_inc(ones_set, 1)
            for c in range(2):
                for b in range(c * HB, (c + 1) * HB):
                    layernorm_stats(dve, s, b, x_step, 2 * b).then_inc(x_step, 1)
                dve.wait_ge(x_step, 2 * HB * (c + 1))
                cols = slice(c * HB, (c + 1) * HB)
                dve.tensor_scalar(xval[:, cols], mv[:, cols, 1], EPS, 0.5, ALU.add, ALU.mult).then_inc(xval_done, 1)
            for b in range(B):
                dve.wait_ge(xrstd_done, b // HB + 1)
                dve.tensor_scalar(xln[:, b, :], s.x[:, b, :], mv[:, b, 0:1], xrstd[:, b:b + 1],
                                  ALU.subtract, ALU.mult).then_inc(xln_done, 1)
            dve.wait_ge(logit_done, 1)
            dve.wait_ge(small_ld, 16 * LOADS)
            over_b = lambda ap: ap.unsqueeze(1).to_broadcast([P, B, E])
            dve.tensor_tensor(logit[:, :, :], logit_ps[:, 0:B * E].rearrange("p (b e) -> p b e", b=B),
                              over_b(gate_b[:, :]), ALU.add).then_inc(gate_step, 1)
            dve.wait_ge(gate_step, 1)
            dve.tensor_reduce(top[:, :], logit[:, :, :], axis=AX_X, op=ALU.max).then_inc(gate_step, 1)
            dve.wait_ge(gate_step, 2)
            dve.tensor_tensor(cand[:, :, :], logit[:, :, :], per_block(top[:, :], E), ALU.is_lt)\
                .then_inc(gate_step, 1)
            dve.wait_ge(gate_step, 3)
            dve.scalar_tensor_tensor(out=cand[:, :, :], in0=cand[:, :, :], scalar=float(E),
                                     in1=over_b(eid[:, 0:E]), op0=ALU.mult, op1=ALU.add).then_inc(gate_step, 1)
            dve.wait_ge(gate_step, 4)
            dve.tensor_reduce(first[:, :], cand[:, :, :], axis=AX_X, op=ALU.min).then_inc(gate_step, 1)
            dve.wait_ge(gate_step, 5)
            dve.tensor_tensor(hot[:, :, :], cand[:, :, :], per_block(first[:, :], E), ALU.is_equal)\
                .then_inc(hot_done, 1)
            dve.wait_ge(hot_done, 1)
            dve.tensor_reduce(hot_sum[:, :], hot[:, :, :].rearrange("p b e -> p e b"), axis=AX_X, op=ALU.add)\
                .then_inc(hot_summed, 1)
            dve.wait_ge(count_done, 1)
            dve.tensor_tensor(fuller[:, :, :], per_block(rank_ps[:, 128:128 + E], B),
                              steps[:, :].unsqueeze(1).to_broadcast([P, E, B]), ALU.is_gt).then_inc(gate_step, 1)
            dve.wait_ge(gate_step, 6)
            dve.tensor_reduce(tiles[:, :], fuller[:, :, :], axis=AX_X, op=ALU.add).then_inc(gate_step, 1)
            dve.wait_ge(gate_step, 7)
            dve.tensor_tensor(below[:, :, :], upto[:, :, :], tiles[:, :].unsqueeze(1).to_broadcast([P, E, E]),
                              ALU.mult).then_inc(gate_step, 1)
            dve.wait_ge(gate_step, 8)
            dve.tensor_reduce(end[:, :], below[:, :, :], axis=AX_X, op=ALU.add).then_inc(gate_step, 1)
            dve.wait_ge(gate_step, 9)
            dve.tensor_tensor(begin[:, :], end[:, :], tiles[:, :], ALU.subtract).then_inc(gate_step, 1)
            dve.wait_ge(gate_step, 10)
            dve.scalar_tensor_tensor(out=place[:, :, :], in0=over_b(begin[:, :]), scalar=float(P),
                                     in1=rank_ps[:, 0:B * E].rearrange("p (b e) -> p b e", b=B),
                                     op0=ALU.mult, op1=ALU.add).then_inc(gate_step, 1)
            dve.wait_ge(gate_step, 11)
            dve.tensor_tensor(place[:, :, :], place[:, :, :], hot[:, :, :], ALU.mult).then_inc(gate_step, 1)
            dve.wait_ge(gate_step, 12)
            dve.tensor_reduce(pos[:, :], place[:, :, :], axis=AX_X, op=ALU.add).then_inc(gate_step, 1)
            dve.wait_ge(gate_step, 13)
            dve.tensor_copy(pos_i[:, :], pos[:, :]).then_inc(pos_done, 1)
            dve.tensor_tensor(past[:, :, :], per_block(eid[:, 0:SORTED], E),
                              end[:, :].unsqueeze(1).to_broadcast([P, SORTED, E]), ALU.is_ge).then_inc(gate_step, 1)
            dve.wait_ge(gate_step, 14)
            dve.tensor_reduce(tile_e[:, :], past[:, :, :], axis=AX_X, op=ALU.add).then_inc(gate_step, 1)
            dve.wait_ge(gate_step, 15)
            dve.tensor_scalar(tile_e[:, :], tile_e[:, :], float(E - 1), None, ALU.min).then_inc(gate_step, 1)
            dve.wait_ge(gate_step, 16)
            dve.tensor_copy(tile_i[:, :], tile_e[:, :]).then_inc(tile_done, 1)
            for b in range(B):
                dve.wait_ge(bias_done, b + 1)
                dve.tensor_tensor(s.x[:, b, :], bias_ps[b % 2][:, :], s.x[:, b, :], ALU.add).then_inc(bias_added, 1)

            def copy_y(t, slot, r):
                dve.wait_ge(y_done, t + 1)
                if not isinstance(r, int) or r >= 1:
                    dve.wait_ge(y_stored[slot], 16 * r)
                dve.tensor_copy(ys[:, slot, :], y_ps[slot][:, :]).then_inc(y_copied, 1)

            run(dve, [(copy_y, 0)])
            for b in range(B):
                dve.wait_ge(gathered[b], 16)
                dve.wait_ge(bias_added, b + 1)
                dve.scalar_tensor_tensor(out=s.x[:, b, :], in0=y_tok[:, b, :], scalar=s.tgates[:, 3:4],
                                         in1=s.x[:, b, :], op0=ALU.mult, op1=ALU.add).then_inc(x_done, 1)

        @block.tensor
        def _(pe):
            def transpose_x(b):
                pe.wait_ge(xln_done, b + 1)
                reached(pe, xT_copied, b - 1)
                for kt in range(KT):
                    last = pe.transpose(xT_ps[b % 2][:, kt * P:(kt + 1) * P], xln[:, b, kt * P:(kt + 1) * P],
                                        s.ident[:, :])
                last.then_inc(xT_done, 1)

            transpose_x(0)
            pe.wait_ge(small_ld, 16 * LOADS)
            for b in range(B):
                if b + 1 < B:
                    transpose_x(b + 1)
                pe.wait_ge(xT_copied, b + 1)
                for kt in range(KT):
                    last = pe.matmul(logit_ps[:, b * E:(b + 1) * E], xT[:, b % 2, kt * P:(kt + 1) * P],
                                     gate_w[:, kt, :], start=(kt == 0), stop=(kt == KT - 1))
            last.then_inc(logit_done, 1)
            pe.wait_ge(hot_done, 1)
            pe.wait_ge(ones_set, 1 + B)
            flat = hot[:, :, :].rearrange("p b e -> p (b e)")
            pe.matmul(rank_ps[:, 0:B * E], rows_before[:, :], flat, start=True, stop=False)
            for k in range(1, B):
                last = pe.matmul(rank_ps[:, k * E:B * E], ones[:, :], flat[:, 0:(B - k) * E], start=False,
                                 stop=(k == B - 1))
            last.then_inc(rank_done, 1)
            pe.wait_ge(hot_summed, 1)
            pe.matmul(rank_ps[:, 128:128 + E], ones[:, :], hot_sum[:, :], start=True, stop=True).then_inc(count_done, 1)
            for k in range(2):
                for i in range(HB):
                    last = pe.transpose(hotT_ps[k][0:E, i * P:(i + 1) * P], hot[:, k * HB + i, :], s.ident[:, :])
                last.then_inc(hotT_done, 1)
            for b in range(B):
                pe.wait_ge(hotT_copied, b // HB + 1)
                reached(pe, bias_added, b - 1)
                pe.matmul(bias_ps[b % 2][:, :], hotT[:, b, :], exp_b[:, :], start=True, stop=True).then_inc(bias_done, 1)
            pe.wait_ge(tile_done, 1)
            pe.wait_ge(s.exp_ld, 16 * E)

            def transpose_tile(t, slot, r):
                pe.wait_ge(xs_ld[slot], 16 * r + 16)
                reached(pe, xsT_copied, t - 2)
                for kt in range(KT):
                    last = pe.transpose(xsT_ps[slot][:, kt * P:(kt + 1) * P], xs[:, slot, kt * P:(kt + 1) * P],
                                        s.ident[:, :])
                last.then_inc(xsT_done, 1)

            def multiply(t, slot, r):
                pe.wait_ge(xsT_copied, t + 1)
                reached(pe, y_copied, t - 2)
                e = pe.value_load(tile_i[0:1, bass.ds(t, 1)], min_val=0, max_val=E - 1)
                for kt in range(KT):
                    last = pe.matmul(y_ps[slot][:, :], xsT[:, slot, kt * P:(kt + 1) * P], s.exp_w[:, e, kt, :],
                                     start=(kt == 0), stop=(kt == KT - 1))
                last.then_inc(y_done, 1)

            run(pe, [(transpose_tile, 1), (multiply, 0)])

        stage.close()


class Names:
    pass


def flamingo(nc, a, out):
    d = Names()
    d.x = a["x"].rearrange("b t n -> t b n")
    d.ctx = a["ctx"].rearrange("b t n -> t b n")
    d.out = out.rearrange("b t n -> t b n")
    d.ctxT = a["ctxT"]
    d.kv_w = [a["kw_l"][0], a["kw_l"][1], a["vw_l"][0], a["vw_l"][1], a["wq_l"][0]]
    d.ident, d.qw, d.kw, d.mask = a["ident"], a["q_norm"], a["k_norm"], a["mask"]
    d.g_xattn, d.g_ffn = a["g_xattn"].to_broadcast([P, 2]), a["g_ffn"].to_broadcast([P, 2])
    d.wq, d.wo = a["wq_l"], a["wo_l"]
    d.perm_row, d.perm_col = a["perm_row"].to_broadcast([P, D]), a["perm_col"]
    d.iota_row, d.iota_col = a["iota_row"].to_broadcast([P, D]), a["iota_col"]
    d.up, d.down = a["up_l"], a["down_l"]
    d.wt, d.wzT, d.wgT, d.wpT = a["wt"], a["wzT"], a["wgT"], a["wpT"]
    d.group_mean, d.gn_w, d.gn_b = a["group_mean"], a["gn_w"], a["gn_b"]
    d.gate_w, d.gate_b = a["gate_w_l"], a["gate_b"].to_broadcast([P, E])
    d.eid = a["iota_row"][:, 0:SORTED].to_broadcast([P, SORTED])
    d.rows_before, d.upto = a["rows_before"], a["upto"].to_broadcast([P, E, E])
    d.exp_b, d.exp_w = a["exp_b"], a["exp_w_l"]
    d.kT_scr = nc.dram_tensor("kT_scr", (G, P, T), F32, kind="Internal").ap()
    d.sorted_x = nc.dram_tensor("sorted_x", (SORTED, P, D), F32, kind="Internal").ap()
    d.sorted_y = nc.dram_tensor("sorted_y", (SORTED, P, D), F32, kind="Internal").ap()
    d.sorted_x_rows = d.sorted_x.rearrange("t p n -> (t p) n")
    d.sorted_y_rows = d.sorted_y.rearrange("t p n -> (t p) n")
    d.v_scr = nc.dram_tensor("v_scr", (G, P, B, P), F32, kind="Internal").ap()

    with ExitStack() as ctx:
        m = Mem(nc, ctx)
        s = Names()
        s.ps = [ctx.enter_context(nc.psum_tensor(f"bank{i}", [P, D], F32)) for i in range(8)]
        s.x = m.sb("x_sb", [P, B, D])
        s.xT_hi, s.xT_lo = m.sb("xT_hi", [P, KT, T], F32R), m.sb("xT_lo", [P, KT, T], F32R)
        s.ident = m.sb("ident_sb", [P, P])
        s.gates, s.tgates = m.sb("gates", [P, 4]), m.sb("tgates", [P, 4])
        s.eps, s.eps_set = m.sb("eps", [P, 1]), m.sem("eps_set")
        s.c15, s.c15_set = m.sb("three_halves", [P, B]), m.sem("three_halves_set")
        s.acc = m.sb("acc", [P, B, D])
        s.ctx_nat = m.sb("ctx_nat", [P, B, D])
        s.bn, s.mv, s.xval = m.sb("bn", [P, B, 6]), m.sb("mv", [P, B, 2]), m.sb("xval", [P, B])
        with ExitStack() as weights:
            w = Mem(nc, weights)
            s.w_raw = w.sb("w_raw", [P, 2, KT, D])
            s.w_hi, s.w_lo = w.sb("w_hi", [P, 2, KT, D], F32R), w.sb("w_lo", [P, 2, KT, D], F32R)
            project_kv(nc, d, s)
            attention(nc, d, s)
        feed_forward(nc, d, s)
        s.exp_w, s.exp_ld = m.sb("exp_w", [P, E, KT, D]), m.sem("exp_ld")
        nonlocal_attention(nc, d, s)
        experts(nc, d, s)


def kernel(**inputs):
    import numpy as np
    import concourse.bacc as bacc
    from concourse.bass_utils import run_bass_kernel_spmd

    i = {k: np.asarray(v) for k, v in inputs.items()}
    wz = i["L1_xattn_Wz"].reshape(8, 16, 16)
    wzT = np.zeros((P, P), np.float32)
    for g in range(8):
        wzT[16 * g:16 * g + 16, 16 * g:16 * g + 16] = wz[g].T
    arrays = {
        "x": i["x"],
        "ctx": i["ctx_4096"],
        "ctxT": i["ctx_4096"].reshape(T, KT, P).transpose(2, 1, 0),
        "kw_l": i["L0_xattn_k_proj_w"].reshape(2, D, KT, P).transpose(0, 3, 2, 1),
        "vw_l": i["L0_xattn_v_proj_w"].reshape(2, D, KT, P).transpose(0, 3, 2, 1),
        "wq_l": i["L0_xattn_q_proj_w"].reshape(G, D, KT, P).transpose(0, 3, 2, 1),
        "wo_l": i["L0_xattn_o_proj_w"].reshape(D, G, HG, P).transpose(1, 3, 2, 0),
        "q_norm": i["L0_xattn_q_norm_w"].reshape(P, 1),
        "k_norm": i["L0_xattn_k_norm_w"].reshape(P, 1),
        "mask": i["mask_1x1xSxS2_ff0"].reshape(P, P),
        "g_xattn": i["g_xattn"].reshape(1, 2),
        "g_ffn": i["g_ffn"].reshape(1, 2),
        "perm_row": i["L0_ffn_perm"].reshape(1, D),
        "perm_col": i["L0_ffn_perm"].reshape(KT, P).T,
        "up_l": i["L0_ffn_up"].reshape(KT, P, P).transpose(1, 0, 2),
        "down_l": i["L0_ffn_down"].transpose(1, 0, 2).reshape(P, D),
        "wt": i["L1_xattn_Wt"],
        "wzT": wzT,
        "wgT": i["L1_xattn_Wg"].T,
        "wpT": i["L1_xattn_Wp"].T,
        "gn_w": i["L1_xattn_gn_w"].reshape(P, 1),
        "gn_b": i["L1_xattn_gn_b"].reshape(P, 1),
        "gate_w_l": i["L1_ffn_gate_w"].reshape(E, KT, P).transpose(2, 1, 0),
        "gate_b": i["L1_ffn_gate_b"].reshape(1, E),
        "exp_w_l": i["L1_ffn_expert_w"].reshape(E, D, KT, P).transpose(0, 3, 2, 1),
        "exp_b": i["L1_ffn_expert_b"],
        "ident": np.eye(P, dtype=np.float32),
        "iota_row": np.arange(D, dtype=np.float32).reshape(1, D),
        "iota_col": np.arange(D, dtype=np.float32).reshape(KT, P).T,
        "rows_before": np.triu(np.ones((P, P), np.float32), 1),
        "upto": np.tril(np.ones((E, E), np.float32)).reshape(1, E, E),
        "group_mean": np.kron(np.eye(8), np.full((16, 16), 1 / 16)).astype(np.float32),
    }
    arrays = {k: np.ascontiguousarray(v) for k, v in arrays.items()}
    nc = bacc.Bacc("TRN2", target_bir_lowering=False, num_devices=1)
    aps = {k: nc.dram_tensor(f"in_{k}", v.shape, mybir.dt.from_np(v.dtype), kind="ExternalInput").ap()
           for k, v in arrays.items()}
    out = nc.dram_tensor("out", (B, P, D), F32, kind="ExternalOutput").ap()
    flamingo(nc, aps, out)
    r = run_bass_kernel_spmd(nc, [{f"in_{k}": v for k, v in arrays.items()}], core_ids=[0])
    return r.results[0]["out"]
```

```python
from contextlib import ExitStack

import concourse.bass as bass
from concourse.bass import IndirectOffsetOnAxis
from concourse import mybir

F32 = mybir.dt.float32
F32R = mybir.dt.float32r
I32 = mybir.dt.int32
ALU = mybir.AluOpType
ACT = mybir.ActivationFunctionType
LN_EXP_SET = "natural_log_exp_and_others"
AX_X = mybir.AxisListType.X

P = 128
B = 8
HB = B // 2
D = 512
KT = D // P
T = B * P
HG = 4
G = 8
UNITS = G * B
E = 8
FH = 16
FD = D // FH
P3 = 3 * FD
HALF = 512
EPS = 1e-5
WARM = 10
WARM2 = 2
SORTED = B + E - 1


def reached(eng, sem, value):
    if not (isinstance(value, int) and value <= 0):
        eng.wait_ge(sem, value)


def per_block(col, n):
    return col.unsqueeze(2).to_broadcast([P, col.shape[1], n])


def blocks(ap, k=HG):
    return ap.rearrange("p (k n) -> p k n", k=k)


def newton_rsqrt(eng, sem, count, half, seed, tmp, out, three_halves):
    eng.tensor_tensor(tmp, seed, seed, ALU.mult).then_inc(sem, 1)
    eng.wait_ge(sem, count + 1)
    eng.tensor_tensor(tmp, tmp, half, ALU.mult).then_inc(sem, 1)
    eng.wait_ge(sem, count + 2)
    eng.tensor_tensor(tmp, three_halves[:, 0:tmp.shape[1]], tmp, ALU.subtract).then_inc(sem, 1)
    eng.wait_ge(sem, count + 3)
    return eng.tensor_tensor(out, seed, tmp, ALU.mult)


def layernorm_stats(dve, s, b, step, count):
    dve.bn_stats(s.bn[:, b, :], s.x[:, b, :]).then_inc(step, 1)
    dve.wait_ge(step, count + 1)
    return dve.bn_aggr(s.mv[:, b, :], s.bn[:, b, :])


def updates_with_stats(dve, s, update, updated, bn_done, mv_done, xval_done):
    for i in range(B + 2):
        if i < B:
            update(i).then_inc(updated, 1)
        if 1 <= i <= B:
            dve.wait_ge(updated, i)
            dve.bn_stats(s.bn[:, i - 1, :], s.x[:, i - 1, :]).then_inc(bn_done, 1)
        if i >= 2:
            dve.wait_ge(bn_done, i - 1)
            dve.bn_aggr(s.mv[:, i - 2, :], s.bn[:, i - 2, :]).then_inc(mv_done, 1)
        if i in (HB + 1, B + 1):
            layernorm_half_var(dve, s, mv_done, i - 1, i // B).then_inc(xval_done, 1)


def negated_shift(dve, s, cols, rstd, shift):
    return dve.scalar_tensor_tensor(out=shift[:, cols], in0=s.mv[:, cols, 0], scalar=-1.0, in1=rstd[:, cols],
                                    op0=ALU.mult, op1=ALU.mult)


def layernorm_half_var(dve, s, step, count, c=None):
    cols = slice(0, B) if c is None else slice(c * HB, (c + 1) * HB)
    dve.wait_ge(step, count)
    return dve.tensor_scalar(s.xval[:, cols], s.mv[:, cols, 1], EPS, 0.5, ALU.add, ALU.mult)


class Mem:

    def __init__(self, nc, ctx):
        self.nc, self.ctx, self.sems = nc, ctx, []

    def sb(self, name, shape, dt=F32):
        return self.ctx.enter_context(self.nc.sbuf_tensor(name, shape, dt))

    def sem(self, name):
        self.sems.append(self.nc.alloc_semaphore(name))
        return self.sems[-1]

    def clear_sems(self):
        self.nc.clear_and_free_semaphores(self.sems)
        self.nc.all_engine_barrier()


def project_kv(nc, d, s):
    with ExitStack() as ctx:
        m = Mem(nc, ctx)
        ctx_raw = m.sb("ctx_raw", [P, KT, T])
        ctx_hi = m.sb("ctx_hi", [P, KT, T], F32R)
        ctx_lo = m.sb("ctx_lo", [P, KT, T], F32R)
        w_raw, w_hi, w_lo = s.w_raw, s.w_hi, s.w_lo
        xln = m.sb("xln1", [P, 2, D])
        junk = m.sb("kv_junk", [P, D])
        k_sb = m.sb("k_sb", [P, 2, D])
        kT_st = m.sb("kT_st", [P, 2, D])
        v_st = s.v_st
        qw = m.sb("qw", [P, 1])
        kw = m.sb("kw", [P, 1])
        qkw = m.sb("qkw", [P, 1])
        ss = m.sb("k_ss", [P, 2, HG])
        lnss = m.sb("k_lnss", [P, 2, HG])
        seed = m.sb("k_seed", [P, 2, HG])
        val = m.sb("k_val", [P, 2, HG])
        tmp = m.sb("k_tmp", [P, 2, HG])
        rstd = m.sb("k_rstd", [P, 2, HG])
        bn, mv = s.bn, s.mv
        xval = m.sb("xval1", [P, B])
        xseed = m.sb("xseed1", [P, B])
        xtmp = m.sb("xtmp1", [P, B])
        xrstd = m.sb("xrstd1", [P, B])

        first_ld = [m.sem(f"first_ld{kt}") for kt in range(KT)]
        ctx_ld = m.sem("ctx_ld")
        wo_ld = m.sem("wo0_ld")
        w_ld = [m.sem(f"kvw_ld{i}") for i in range(2)]
        x_ld = m.sem("x_ld")
        small_ld = m.sem("small_ld")
        gates_ready = m.sem("gates_ready")
        ctx_hi_done, ctx_lo_done = m.sem("ctx_hi_done"), m.sem("ctx_lo_done")
        w_hi_done, w_lo_done = m.sem("kvw_hi_done"), m.sem("kvw_lo_done")
        kv_done = m.sem("kv_done")
        k_scaled = m.sem("k_scaled")
        v_copied = m.sem("v_copied")
        sumsq_done, ln_done, seed_done = m.sem("k_sumsq"), m.sem("k_ln"), m.sem("k_seeded")
        newton, rstd_done = m.sem("k_newton"), m.sem("k_rstd_done")
        kT_done, kT_copied = m.sem("kT_done"), m.sem("kT_copied")
        kT_stored = [m.sem(f"kT_stored{i}") for i in range(2)]
        v_stored = s.v_stored
        stats_step, qkw_done = m.sem("stats1_step"), m.sem("qkw_done")
        xval_done, xln_ln, xseed_done = m.sem("xval1_done"), m.sem("xln1_ln"), m.sem("xseed1_done")
        xrstd_done, xln_done = m.sem("xrstd1_done"), m.sem("xln1_done")
        xT_done, xT_hi_done, xT_lo_done = m.sem("xT1_done"), m.sem("xT1_hi_done"), m.sem("xT1_lo_done")
        kv_ps = s.ps[0:3]
        kT_ps = s.ps[3:5]
        xT_ps = s.ps[5:7]
        NU = 4 * B
        NK = 2 * B
        XT0 = NK + 2

        stage = ExitStack()
        block = stage.enter_context(nc.Block())

        @block.sync
        def _(sp):
            for kt in range(KT):
                sp.dma_start(ctx_raw[:, kt, 0:HALF], d.ctxT[:, kt, 0:HALF]).then_inc(first_ld[kt], 16)
                sp.dma_start(w_raw[:, 0, kt, :], d.kv_w[0][:, kt, :]).then_inc(first_ld[kt], 16)
            sp.dma_start(ctx_raw[:, :, HALF:T], d.ctxT[:, :, HALF:T]).then_inc(ctx_ld, 16)
            for dst, src in ((s.ident[:, :], d.ident), (qw[:, :], d.qw), (kw[:, :], d.kw),
                             (s.gates[:, 0:2], d.g_xattn), (s.gates[:, 2:4], d.g_ffn)):
                sp.dma_start(dst, src).then_inc(small_ld, 16)
            sp.dma_start(w_raw[:, 1, :, :], d.kv_w[1]).then_inc(w_ld[1], 16)
            sp.dma_start(s.x[:, :, :], d.x).then_inc(x_ld, 16)
            for i in range(NU):
                w, b = divmod(i, B)
                n = {0: 2, B - 2: 3, 2 * B - 2: 4, 3 * B - 2: 5}.get(i)
                if n:
                    sp.wait_ge(w_lo_done, KT * (n - 1))
                    src, ld = (d.kv_w[n], w_ld[n % 2]) if n < 5 else (d.wo[0, :, :, :], wo_ld)
                    sp.dma_start(w_raw[:, n % 2, :, :], src).then_inc(ld, 16)
                if i < NK:
                    sp.wait_ge(kT_copied, i + 1)
                    sp.dma_start(d.kT_scr[4 * w:4 * w + 4, :, b * P:(b + 1) * P].rearrange("g d t -> d g t"),
                                 blocks(kT_st[:, i % 2, :])).then_inc(kT_stored[i % 2], 16)
                else:
                    sp.wait_ge(v_copied, i - NK + 1)
                    sp.dma_start(d.v_scr[4 * (w - 2):4 * (w - 2) + 4, :, b, :].rearrange("g t d -> t g d"),
                                 blocks(v_st[:, i % 2, :])).then_inc(v_stored[i % 2], 16)
                if i == 3 * B + 2:
                    for q in range(2):
                        sp.wait_ge(kT_stored[q], 16 * (NK // 2))
                        sp.wait_ge(v_stored[q], 16 * (B // 2))
                    sp.dma_start(s.v_raw[:, :, :], d.v_scr[0]).then_inc(first_ld[0], 16)
                    sp.dma_start(s.kT[:, :], d.kT_scr[0]).then_inc(first_ld[1], 16)
                    sp.dma_start(s.mask[:, :], d.mask).then_inc(first_ld[2], 16)
            for i in range(3):
                sp.wait_ge(first_ld[i], 48)
            sp.wait_ge(wo_ld, 16)

        @block.scalar
        def _(act):
            for kt in range(KT):
                act.wait_ge(first_ld[kt], 32)
                act.activation(ctx_hi[:, kt, 0:HALF], ctx_raw[:, kt, 0:HALF], ACT.Copy).then_inc(ctx_hi_done, 1)
            act.wait_ge(ctx_ld, 16)
            for kt in range(KT):
                act.activation(ctx_hi[:, kt, HALF:T], ctx_raw[:, kt, HALF:T], ACT.Copy).then_inc(ctx_hi_done, 1)
            act.wait_ge(small_ld, 16 * 5)
            act.activation(s.tgates[:, :], s.gates[:, :], ACT.Tanh).then_inc(gates_ready, 1)
            act.preload_act_table_set(LN_EXP_SET)
            for i in range(NU):
                if i < NK:
                    act.wait_ge(kv_done, i + 1)
                    if i == 0:
                        act.wait_ge(s.eps_set, 1)
                    reached(act, rstd_done, i - 1)
                    reached(act, sumsq_done, i)
                    for h in range(HG):
                        last = act.activation(junk[:, h * P:(h + 1) * P], kv_ps[i % 3][:, h * P:(h + 1) * P],
                                              ACT.Square, accum_out=ss[:, i % 2, h:h + 1])
                    last.then_inc(sumsq_done, 1)
                    act.wait_ge(sumsq_done, i + 1)
                    act.activation(lnss[:, i % 2, :], ss[:, i % 2, :], ACT.Ln, bias=s.eps[:, 0:1], scale=1.0 / P)\
                        .then_inc(ln_done, 1)
                    act.wait_ge(ln_done, i + 1)
                    act.activation(seed[:, i % 2, :], lnss[:, i % 2, :], ACT.Exp, scale=-0.5).then_inc(seed_done, 1)
                else:
                    n = i - NK
                    act.wait_ge(kv_done, i + 1)
                    if n >= 2:
                        act.wait_ge(v_stored[i % 2], 16 * (n // 2))
                    act.activation(v_st[:, i % 2, :], kv_ps[i % 3][:, :], ACT.Copy).then_inc(v_copied, 1)
                if i == NK - 1:
                    act.wait_ge(xval_done, 1)
                    act.activation(xtmp[:, :], xval[:, :], ACT.Ln, scale=2.0).then_inc(xln_ln, 1)
                    act.wait_ge(xln_ln, 1)
                    act.activation(xseed[:, :], xtmp[:, :], ACT.Exp, scale=-0.5).then_inc(xseed_done, 1)
                if XT0 <= i < XT0 + B:
                    b = i - XT0
                    act.wait_ge(xT_done, b + 1)
                    act.activation(s.xT_hi[:, :, b * P:(b + 1) * P], blocks(xT_ps[b % 2][:, :]), ACT.Copy)\
                        .then_inc(xT_hi_done, 1)

        @block.gpsimd
        def _(pool):
            pool.memset(s.c15[:, :], 1.5).then_inc(s.c15_set, 1)
            pool.wait_ge(s.c15_set, 1)
            for i in range(NK):
                pool.wait_ge(sumsq_done, i + 1)
                reached(pool, rstd_done, i)
                pool.tensor_scalar(val[:, i % 2, :], ss[:, i % 2, :], 0.5 / P, 0.5 * EPS, ALU.mult, ALU.add)\
                    .then_inc(newton, 1)
                pool.wait_ge(seed_done, i + 1)
                pool.wait_ge(newton, 4 * i + 1)
                reached(pool, k_scaled, i - 1)
                newton_rsqrt(pool, newton, 4 * i + 1, val[:, i % 2, :], seed[:, i % 2, :], tmp[:, i % 2, :],
                             rstd[:, i % 2, :], s.c15).then_inc(rstd_done, 1)
            pool.wait_ge(xseed_done, 1)
            newton_rsqrt(pool, newton, 4 * NK, xval[:, :], xseed[:, :], xtmp[:, :], xrstd[:, :], s.c15)\
                .then_inc(xrstd_done, 1)

        @block.vector
        def _(dve):
            dve.memset(s.eps[:, :], EPS).then_inc(s.eps_set, 1)

            def split_w(w, kts):
                for kt in kts:
                    if w == 0:
                        dve.wait_ge(first_ld[kt], 32)
                    else:
                        dve.wait_ge(w_ld[w % 2], 16 * ((w + 1) // 2))
                    if w >= 2:
                        dve.wait_ge(kv_done, B * (w - 1))
                    dve.tensor_copy(w_hi[:, w % 2, kt, :], w_raw[:, w % 2, kt, :]).then_inc(w_hi_done, 1)
                    dve.wait_ge(w_hi_done, KT * w + kt + 1)
                    dve.tensor_tensor(w_lo[:, w % 2, kt, :], w_raw[:, w % 2, kt, :],
                                      w_hi[:, w % 2, kt, :].bitcast(F32), ALU.subtract).then_inc(w_lo_done, 1)

            for kt in range(KT):
                split_w(0, [kt])
                dve.wait_ge(ctx_hi_done, kt + 1)
                dve.tensor_tensor(ctx_lo[:, kt, 0:HALF], ctx_raw[:, kt, 0:HALF], ctx_hi[:, kt, 0:HALF].bitcast(F32),
                                  ALU.subtract).then_inc(ctx_lo_done, 1)
            dve.wait_ge(small_ld, 16 * 5)
            dve.tensor_tensor(qkw[:, :], qw[:, :], kw[:, :], ALU.mult).then_inc(qkw_done, 1)
            for kt in range(KT):
                dve.wait_ge(ctx_hi_done, KT + kt + 1)
                dve.tensor_tensor(ctx_lo[:, kt, HALF:T], ctx_raw[:, kt, HALF:T], ctx_hi[:, kt, HALF:T].bitcast(F32),
                                  ALU.subtract).then_inc(ctx_lo_done, 1)
            dve.wait_ge(qkw_done, 1)
            for i in range(NU):
                w, b = divmod(i, B)
                if i < NK:
                    dve.wait_ge(rstd_done, i + 1)
                    dve.wait_ge(kv_done, i + 1)
                    reached(dve, kT_done, i - 1)
                    dve.tensor_tensor(blocks(k_sb[:, i % 2, :]), blocks(kv_ps[i % 3][:, :]),
                                      per_block(rstd[:, i % 2, :], P), ALU.mult).then_inc(k_scaled, 1)
                if 1 <= b <= KT:
                    split_w(w + 1, [b - 1])
                if 1 <= i <= NK:
                    n = i - 1
                    dve.wait_ge(kT_done, n + 1)
                    if n >= 2:
                        dve.wait_ge(kT_stored[n % 2], 16 * (n // 2))
                    dve.tensor_scalar(kT_st[:, n % 2, :], kT_ps[n % 2][:, :], qkw[:, 0:1], None, ALU.mult)\
                        .then_inc(kT_copied, 1)
                if HB <= i < HB + B:
                    n = i - HB
                    if n == 0:
                        dve.wait_ge(x_ld, 16)
                    dve.bn_stats(bn[:, n, :], s.x[:, n, :]).then_inc(stats_step, 1)
                    dve.wait_ge(stats_step, 2 * n + 1)
                    dve.bn_aggr(mv[:, n, :], bn[:, n, :]).then_inc(stats_step, 1)
                if i == HB + B:
                    dve.wait_ge(stats_step, 2 * B)
                    dve.tensor_scalar(xval[:, :], mv[:, :, 1], EPS, 0.5, ALU.add, ALU.mult).then_inc(xval_done, 1)
                if XT0 - 1 <= i < XT0 - 1 + B:
                    n = i - XT0 + 1
                    dve.wait_ge(xrstd_done, 1)
                    reached(dve, xT_done, n - 1)
                    dve.tensor_scalar(xln[:, n % 2, :], s.x[:, n, :], mv[:, n, 0:1], xrstd[:, n:n + 1],
                                      ALU.subtract, ALU.mult).then_inc(xln_done, 1)
                if XT0 <= i < XT0 + B:
                    n = i - XT0
                    dve.wait_ge(xT_hi_done, n + 1)
                    dve.tensor_tensor(s.xT_lo[:, :, n * P:(n + 1) * P], blocks(xT_ps[n % 2][:, :]),
                                      s.xT_hi[:, :, n * P:(n + 1) * P].bitcast(F32), ALU.subtract)\
                        .then_inc(xT_lo_done, 1)

        @block.tensor
        def _(pe):
            for i in range(NU):
                w, b = divmod(i, B)
                if i >= 3:
                    if i - 3 < NK:
                        pe.wait_ge(k_scaled, i - 2)
                    else:
                        pe.wait_ge(v_copied, i - 2 - NK)
                tok = slice(b * P, (b + 1) * P)
                for kt in range(KT):
                    if i in (0, B // 2):
                        pe.wait_ge(ctx_lo_done, (KT if i else 0) + kt + 1)
                    if b == 0:
                        pe.wait_ge(w_lo_done, KT * w + kt + 1)
                    hi, lo = w_hi[:, w % 2, kt, :], w_lo[:, w % 2, kt, :]
                    pe.matmul(kv_ps[i % 3][:, :], ctx_hi[:, kt, tok], hi, start=(kt == 0), stop=False)
                    pe.matmul(kv_ps[i % 3][:, :], ctx_lo[:, kt, tok], hi, start=False, stop=False)
                    last = pe.matmul(kv_ps[i % 3][:, :], ctx_hi[:, kt, tok], lo, start=False, stop=(kt == KT - 1))
                last.then_inc(kv_done, 1)
                if 2 <= i < NK + 2:
                    n = i - 2
                    if n == 0:
                        pe.wait_ge(small_ld, 16 * 5)
                    pe.wait_ge(k_scaled, n + 1)
                    reached(pe, kT_copied, n - 1)
                    for h in range(HG):
                        last = pe.transpose(kT_ps[n % 2][:, h * P:(h + 1) * P], k_sb[:, n % 2, h * P:(h + 1) * P],
                                            s.ident[:, :])
                    last.then_inc(kT_done, 1)
                if XT0 <= i < XT0 + B:
                    n = i - XT0
                    pe.wait_ge(xln_done, n + 1)
                    reached(pe, xT_lo_done, n - 1)
                    for kt in range(KT):
                        last = pe.transpose(xT_ps[n % 2][:, kt * P:(kt + 1) * P], xln[:, n % 2, kt * P:(kt + 1) * P],
                                            s.ident[:, :])
                    last.then_inc(xT_done, 1)

        stage.close()
        m.clear_sems()


def attention(nc, d, s):
    with ExitStack() as ctx:
        m = Mem(nc, ctx)
        wq_raw, wo_raw = s.w_raw[:, 0, :, :], s.w_raw[:, 1, :, :]
        odd_hi, odd_lo = m.sb("odd_hi", [P, 2, KT, D], F32R), m.sb("odd_lo", [P, 2, KT, D], F32R)
        wq_hi, wo_hi = [[w[:, i, :, :] for w in (s.w_hi, odd_hi)] for i in range(2)]
        wq_lo, wo_lo = [[w[:, i, :, :] for w in (s.w_lo, odd_lo)] for i in range(2)]
        kT, v_raw, mask = s.kT, s.v_raw, s.mask
        v_hi = m.sb("v_hi", [P, B, P], F32R)
        v_lo = m.sb("v_lo", [P, B, P], F32R)
        junk = m.sb("q_junk", [P, D])
        q_sb = m.sb("q_sb", [P, 2, D])
        qT_sb = m.sb("qT_sb", [P, 2, D])
        p_sb = m.sb("p_sb", [P, 2, D])
        pT_hi = m.sb("pT_hi", [P, D], F32R)
        pT_lo = m.sb("pT_lo", [P, D], F32R)
        oT_hi = m.sb("oT_hi", [P, D], F32R)
        oT_lo = m.sb("oT_lo", [P, D], F32R)
        ss = m.sb("q_ss", [P, 2, HG])
        lnss = m.sb("q_lnss", [P, 2, HG])
        seed = m.sb("q_seed", [P, 2, HG])
        val = m.sb("q_val", [P, 2, HG])
        tmp = m.sb("q_tmp", [P, 2, HG])
        rstd = m.sb("q_rstd", [P, 2, HG])
        nmax = m.sb("nmax", [P, 2, HG])
        psum_ = m.sb("prob_sum", [P, 2, HG])
        rsum = m.sb("rsum", [P, 2, HG])
        qeps = m.sb("qeps", [P, 1])

        ctx_nat_ld = m.sem("ctx_nat_ld")
        qeps_set = m.sem("qeps_set")
        wq_ld, wo_ld = m.sem("wq_ld"), m.sem("wo_ld")
        kT_ld = [m.sem(f"kT_ld{i}") for i in range(2)]
        v_ld = [m.sem(f"v_ld{i}") for i in range(2)]
        wq_hi_done, wo_hi_done = m.sem("wq_hi_done"), m.sem("wo_hi_done")
        wq_lo_done, wo_lo_done = m.sem("wq_lo_done"), m.sem("wo_lo_done")
        sum_scaled, x_done, x_step = m.sem("sum_scaled"), m.sem("x1_done"), m.sem("x1_step")
        v_hi_done, v_lo_done = m.sem("v_hi_done"), m.sem("v_lo_done")
        q_done, q_scaled = m.sem("q_done"), m.sem("q_scaled")
        sumsq_done, ln_done, seed_done = m.sem("q_sumsq"), m.sem("q_ln"), m.sem("q_seeded")
        newton, rstd_done = m.sem("q_newton"), m.sem("q_rstd_done")
        half_done = m.sem("q_half_done")
        qT_done, qT_copied = m.sem("qT_done"), m.sem("qT_copied")
        s_done, masked, max_done = m.sem("s_done"), m.sem("masked"), m.sem("max_done")
        exp_done, rsum_done, p_done = m.sem("exp_done"), m.sem("rsum_done"), m.sem("p_done")
        pT_done, pT_hi_done, pT_lo_done = m.sem("pT_done"), m.sem("pT_hi_done"), m.sem("pT_lo_done")
        pv_done, oT_hi_done, oT_lo_done = m.sem("pv_done"), m.sem("oT_hi_done"), m.sem("oT_lo_done")
        o_done, acc_done = m.sem("o_done"), m.sem("acc_done")

        q_ps, o_ps = s.ps[0:2], s.ps[2:4]
        qT_ps, s_ps, pT_ps, oT_ps = s.ps[4], s.ps[5], s.ps[6], s.ps[7]

        def run(eng, stages):

            def step(g, odd, b):
                for stage, ahead in stages:
                    u = 8 * g + b + ahead
                    if not isinstance(u, int) or 0 <= u < UNITS:
                        stage(u, (b + ahead) % B, g + (b + ahead) // B, (odd + (b + ahead) // B) % 2)

            for b in range(2, B):
                step(-1, 1, b)
            for b in range(B):
                step(0, 0, b)
            with eng.Fori(0, (G - 2) // 2) as r:
                for b in range(B):
                    step(2 * r + 1, 1, b)
                for b in range(B):
                    step(2 * r + 2, 0, b)
            for b in range(B):
                step(G - 1, 1, b)
            for b in range(4):
                step(G, 0, b)

        stage = ExitStack()
        block = stage.enter_context(nc.Block())

        @block.sync
        def _(sp):
            def loads(g):
                def v_half(c):
                    reached(sp, v_hi_done, 8 * g - 4 + 4 * c)
                    reached(sp, v_lo_done, 8 * g - 4 + 4 * c)
                    sp.dma_start(v_raw[:, 4 * c:4 * c + 4, :], d.v_scr[g, :, 4 * c:4 * c + 4, :])\
                        .then_inc(v_ld[c], 16)

                def kT_half(c):
                    reached(sp, s_done, 8 * g - 4 + 4 * c)
                    sp.dma_start(kT[:, c * HALF:(c + 1) * HALF], d.kT_scr[g, :, c * HALF:(c + 1) * HALF])\
                        .then_inc(kT_ld[c], 16)

                v_half(0)
                reached(sp, wq_lo_done, 4 * g - 4)
                sp.dma_start(wq_raw[:, :, :], d.wq[g, :, :, :]).then_inc(wq_ld, 16)
                v_half(1)
                reached(sp, wo_lo_done, 4 * g)
                sp.dma_start(wo_raw[:, :, :], d.wo[g, :, :, :]).then_inc(wo_ld, 16)
                kT_half(0)
                kT_half(1)

            sp.dma_start(s.ctx_nat[:, :, :], d.ctx).then_inc(ctx_nat_ld, 16)
            for q in range(2):
                sp.wait_ge(s.v_stored[q], 16 * B)
            loads(1)
            with sp.Fori(2, G) as g:
                loads(g)
            sp.wait_ge(ctx_nat_ld, 16)

        @block.scalar
        def _(act):
            act.wait_ge(qeps_set, 1)

            def oT_split(u, b, g, odd):
                act.wait_ge(pv_done, u + 1)
                reached(act, o_done, u)
                act.activation(oT_hi[:, :], oT_ps[:, :], ACT.Copy).then_inc(oT_hi_done, 1)

            def exps(u, b, g, odd):
                act.wait_ge(max_done, u + 1)
                for h in range(HG):
                    last = act.activation(p_sb[:, b % 2, h * P:(h + 1) * P], p_sb[:, b % 2, h * P:(h + 1) * P],
                                          ACT.Exp, bias=nmax[:, b % 2, h:h + 1],
                                          accum_out=psum_[:, b % 2, h:h + 1])
                last.then_inc(exp_done, 1)

            def qT_copy(u, b, g, odd):
                act.wait_ge(qT_done, u + 1)
                reached(act, s_done, u - 1)
                act.activation(qT_sb[:, b % 2, :], qT_ps[:, :], ACT.Copy).then_inc(qT_copied, 1)

            def pT_split(u, b, g, odd):
                act.wait_ge(pT_done, u + 1)
                reached(act, pv_done, u)
                act.activation(pT_hi[:, :], pT_ps[:, :], ACT.Copy).then_inc(pT_hi_done, 1)

            def wq_split(kt):
                def stage(u, b, g, odd):
                    if b or (isinstance(g, int) and g == 0):
                        return
                    act.wait_ge(wq_ld, 16 * g)
                    reached(act, q_done, 8 * g - 8)
                    act.activation(wq_hi[odd][:, kt, :], wq_raw[:, kt, :], ACT.Copy).then_inc(wq_hi_done, 1)

                return stage

            def wo_split(h):
                def stage(u, b, g, odd):
                    if b:
                        return
                    reached(act, wo_ld, 16 * g)
                    reached(act, o_done, 8 * g - 8)
                    act.activation(wo_hi[odd][:, h, :], wo_raw[:, h, :], ACT.Copy).then_inc(wo_hi_done, 1)

                return stage

            def v_split(u, b, g, odd):
                reached(act, v_ld[b // 4], 16 * g)
                reached(act, pv_done, u - 7)
                act.activation(v_hi[:, b, :], v_raw[:, b, :], ACT.Copy).then_inc(v_hi_done, 1)

            def q_stats(u, b, g, odd):
                act.wait_ge(q_done, u + 1)
                reached(act, half_done, u - 1)
                reached(act, sumsq_done, u)
                for h in range(HG):
                    last = act.activation(junk[:, h * P:(h + 1) * P], q_ps[b % 2][:, h * P:(h + 1) * P],
                                          ACT.Square, accum_out=ss[:, b % 2, h:h + 1])
                last.then_inc(sumsq_done, 1)
                act.wait_ge(sumsq_done, u + 1)
                act.activation(lnss[:, b % 2, :], ss[:, b % 2, :], ACT.Ln, bias=qeps[:, 0:1]).then_inc(ln_done, 1)
                act.wait_ge(ln_done, u + 1)
                act.activation(seed[:, b % 2, :], lnss[:, b % 2, :], ACT.Exp, scale=-0.5).then_inc(seed_done, 1)

            def scale_sum(u, b, g, odd):
                if isinstance(g, int) and g == G - 1:
                    act.wait_ge(acc_done, B + u + 1)
                    act.activation(s.acc[:, b, :], s.acc[:, b, :], ACT.Copy, scale=s.tgates[:, 0:1]).then_inc(sum_scaled, 1)

            run(act, [(oT_split, -2), (exps, 0), (qT_copy, 1), (pT_split, -1), (v_split, 6), (q_stats, 2), (scale_sum, -3)]
                + [(wq_split(kt), 7 - kt) for kt in range(KT)] + [(wo_split(h), 4 - h) for h in range(HG)])

        @block.gpsimd
        def _(pool):
            def v_split(u, b, g, odd):
                pool.wait_ge(v_hi_done, u + 1)
                pool.tensor_tensor(v_lo[:, b, :], v_raw[:, b, :], v_hi[:, b, :].bitcast(F32), ALU.subtract)\
                    .then_inc(v_lo_done, 1)

            def normalize(u, b, g, odd):
                pool.wait_ge(rsum_done, u + 1)
                pool.tensor_tensor(blocks(p_sb[:, b % 2, :]), blocks(p_sb[:, b % 2, :]),
                                   per_block(rsum[:, b % 2, :], P), ALU.mult).then_inc(p_done, 1)

            def wq_split(kt):
                def stage(u, b, g, odd):
                    if b or (isinstance(g, int) and g == 0):
                        return
                    pool.wait_ge(wq_hi_done, 4 * g - 3 + kt)
                    pool.tensor_tensor(wq_lo[odd][:, kt, :], wq_raw[:, kt, :], wq_hi[odd][:, kt, :].bitcast(F32),
                                       ALU.subtract).then_inc(wq_lo_done, 1)

                return stage

            def wo_split(h):
                def stage(u, b, g, odd):
                    if b:
                        return
                    pool.wait_ge(wo_hi_done, 4 * g + h + 1)
                    pool.tensor_tensor(wo_lo[odd][:, h, :], wo_raw[:, h, :], wo_hi[odd][:, h, :].bitcast(F32),
                                       ALU.subtract).then_inc(wo_lo_done, 1)

                return stage

            def q_rstd(u, b, g, odd):
                pool.wait_ge(half_done, u + 1)
                pool.wait_ge(seed_done, u + 1)
                reached(pool, rstd_done, u)
                reached(pool, q_scaled, u - 1)
                newton_rsqrt(pool, newton, 3 * u, val[:, b % 2, :], seed[:, b % 2, :], tmp[:, b % 2, :],
                             rstd[:, b % 2, :], s.c15).then_inc(rstd_done, 1)

            def x_update(u, b, g, odd):
                if isinstance(g, int) and g == G - 1:
                    pool.wait_ge(sum_scaled, b + 1)
                    pool.tensor_tensor(s.x[:, b, :], s.x[:, b, :], s.acc[:, b, :], ALU.add).then_inc(x_done, 1)

            run(pool, [(v_split, 6), (normalize, 0), (q_rstd, 2), (x_update, -3)]
                + [(wq_split(kt), 7 - kt) for kt in range(KT)] + [(wo_split(h), 4 - h) for h in range(HG)])

        @block.vector
        def _(dve):
            dve.memset(qeps[:, :], P * EPS).then_inc(qeps_set, 1)
            for b in range(B):
                dve.memset(s.acc[:, b, :], 0.0).then_inc(acc_done, 1)

            def oT_split(u, b, g, odd):
                dve.wait_ge(oT_hi_done, u + 1)
                dve.tensor_tensor(oT_lo[:, :], oT_ps[:, :], oT_hi[:, :].bitcast(F32), ALU.subtract)\
                    .then_inc(oT_lo_done, 1)

            def mask_max(u, b, g, odd):
                dve.wait_ge(s_done, u + 1)
                reached(dve, pT_done, u - 1)
                dve.tensor_tensor(blocks(p_sb[:, b % 2, :]), blocks(s_ps[:, :]),
                                  mask[:, :].unsqueeze(1).to_broadcast([P, HG, P]), ALU.add).then_inc(masked, 1)
                dve.wait_ge(masked, u + 1)
                dve.tensor_reduce(nmax[:, b % 2, :], blocks(p_sb[:, b % 2, :]), axis=AX_X, op=ALU.max,
                                  negate=True).then_inc(max_done, 1)

            def q_half(u, b, g, odd):
                dve.wait_ge(sumsq_done, u + 1)
                reached(dve, rstd_done, u - 1)
                dve.tensor_scalar(val[:, b % 2, :], ss[:, b % 2, :], 0.5, 0.5 * P * EPS, ALU.mult, ALU.add)\
                    .then_inc(half_done, 1)

            def q_scale(u, b, g, odd):
                dve.wait_ge(rstd_done, u + 1)
                reached(dve, qT_done, u - 1)
                dve.tensor_tensor(blocks(q_sb[:, b % 2, :]), blocks(q_ps[b % 2][:, :]),
                                  per_block(rstd[:, b % 2, :], P), ALU.mult).then_inc(q_scaled, 1)

            def p_recip(u, b, g, odd):
                dve.wait_ge(exp_done, u + 1)
                reached(dve, p_done, u - 1)
                dve.reciprocal(rsum[:, b % 2, :], psum_[:, b % 2, :]).then_inc(rsum_done, 1)

            def pT_split(u, b, g, odd):
                dve.wait_ge(pT_hi_done, u + 1)
                dve.tensor_tensor(pT_lo[:, :], pT_ps[:, :], pT_hi[:, :].bitcast(F32), ALU.subtract)\
                    .then_inc(pT_lo_done, 1)

            def accumulate(u, b, g, odd):
                dve.wait_ge(o_done, u + 1)
                dve.wait_ge(acc_done, u + 1)
                dve.tensor_tensor(s.acc[:, b, :], o_ps[b % 2][:, :], s.acc[:, b, :], ALU.add)\
                    .then_inc(acc_done, 1)

            def x_stats(u, b, g, odd):
                if isinstance(g, int) and g == G - 1:
                    dve.wait_ge(x_done, b + 1)
                    layernorm_stats(dve, s, b, x_step, 2 * b).then_inc(x_step, 1)

            run(dve, [(oT_split, -2), (mask_max, 0), (q_scale, 1), (p_recip, 0), (pT_split, -1), (q_half, 2),
                      (accumulate, -2), (x_stats, -4)])
            layernorm_half_var(dve, s, x_step, 2 * B).then_inc(x_step, 1)

        @block.tensor
        def _(pe):
            def scores(u, b, g, odd):
                pe.wait_ge(qT_copied, u + 1)
                if b % 4 == 0:
                    reached(pe, kT_ld[b // 4], 16 * g)
                reached(pe, masked, u)
                for h in range(HG):
                    last = pe.matmul(s_ps[:, h * P:(h + 1) * P], qT_sb[:, b % 2, h * P:(h + 1) * P],
                                     kT[:, b * P:(b + 1) * P], start=True, stop=True)
                last.then_inc(s_done, 1)

            def q_proj(u, b, g, odd):
                reached(pe, q_scaled, u - 1)
                for kt in range(KT):
                    if b == 0 and not (isinstance(g, int) and g == 0):
                        pe.wait_ge(wq_lo_done, 4 * g - 3 + kt)
                    xh, xl = s.xT_hi[:, kt, b * P:(b + 1) * P], s.xT_lo[:, kt, b * P:(b + 1) * P]
                    pe.matmul(q_ps[b % 2][:, :], xh, wq_hi[odd][:, kt, :], start=(kt == 0), stop=False)
                    pe.matmul(q_ps[b % 2][:, :], xl, wq_hi[odd][:, kt, :], start=False, stop=False)
                    last = pe.matmul(q_ps[b % 2][:, :], xh, wq_lo[odd][:, kt, :], start=False, stop=(kt == KT - 1))
                last.then_inc(q_done, 1)

            def q_transpose(u, b, g, odd):
                pe.wait_ge(q_scaled, u + 1)
                reached(pe, qT_copied, u)
                for h in range(HG):
                    last = pe.transpose(qT_ps[:, h * P:(h + 1) * P], q_sb[:, b % 2, h * P:(h + 1) * P],
                                        s.ident[:, :])
                last.then_inc(qT_done, 1)

            def p_transpose(u, b, g, odd):
                pe.wait_ge(p_done, u + 1)
                reached(pe, pT_lo_done, u)
                for h in range(HG):
                    last = pe.transpose(pT_ps[:, h * P:(h + 1) * P], p_sb[:, b % 2, h * P:(h + 1) * P],
                                        s.ident[:, :])
                last.then_inc(pT_done, 1)

            def o_proj(u, b, g, odd):
                pe.wait_ge(oT_lo_done, u + 1)
                reached(pe, acc_done, B + u - 1)
                for h in range(HG):
                    if b == 0:
                        pe.wait_ge(wo_lo_done, 4 * g + h + 1)
                    oh, ol = oT_hi[:, h * P:(h + 1) * P], oT_lo[:, h * P:(h + 1) * P]
                    pe.matmul(o_ps[b % 2][:, :], oh, wo_hi[odd][:, h, :], start=(h == 0), stop=False)
                    pe.matmul(o_ps[b % 2][:, :], ol, wo_hi[odd][:, h, :], start=False, stop=False)
                    last = pe.matmul(o_ps[b % 2][:, :], oh, wo_lo[odd][:, h, :], start=False, stop=(h == HG - 1))
                last.then_inc(o_done, 1)

            def values(u, b, g, odd):
                pe.wait_ge(pT_lo_done, u + 1)
                pe.wait_ge(v_lo_done, u + 1)
                reached(pe, oT_lo_done, u)
                pe.matmul(oT_ps[:, :], v_hi[:, b, :], pT_hi[:, :], start=True, stop=False)
                pe.matmul(oT_ps[:, :], v_lo[:, b, :], pT_hi[:, :], start=False, stop=False)
                pe.matmul(oT_ps[:, :], v_hi[:, b, :], pT_lo[:, :], start=False, stop=True).then_inc(pv_done, 1)

            run(pe, [(scores, 0), (q_proj, 2), (q_transpose, 1), (p_transpose, -1), (o_proj, -2), (values, -1)])

        stage.close()
        m.clear_sems()


def feed_forward(nc, d, s):
    with ExitStack() as ctx:
        m = Mem(nc, ctx)
        xln = m.sb("xln2", [P, 2, D])
        mv, xval, xseed = s.mv, s.xval, m.sb("xseed2", [P, B])
        xtmp, xrstd, xshift = m.sb("xtmp2", [P, B]), m.sb("xrstd2", [P, B]), m.sb("xshift2", [P, B])
        rows_i, rows_f = m.sb("rows_i", [P3, FH], I32), m.sb("rows_f", [P3, FH])
        lo_rows, rows = m.sb("lo_rows", [P3, FH]), m.sb("rows", [P3, FH], I32)
        perm_col = m.sb("perm_col", [P, KT], I32)
        up_space, up = m.sb("up_raw", [P, FH, P]), m.sb("up", [P3, FH, P], F32R)
        up_raw = up_space[0:P3, :, :]
        down = m.sb("down", [P, D])
        xg = m.sb("xg", [P3, FH, T])
        hid = s.hid
        yT, yU = up_space[:, :, :].rearrange("p h m -> p (h m)").rearrange("p (i t) -> p i t", i=2), s.yU
        wt, wzT, wgT, mT = m.sb("wt", [P, P]), m.sb("wzT", [P, P]), m.sb("wgT", [P, P]), m.sb("mT", [P, P])
        zbn = m.sb("zbn", [P, B, 6])
        dev = m.sb("dev", [P, B])
        gn_w, gn_b = m.sb("gn_w", [P, 1]), m.sb("gn_b", [P, 1])
        col_ld, col_step = m.sem("col_ld"), m.sem("col_step")

        rows_ld, up_ld, down_ld, w_ld = m.sem("rows_ld"), m.sem("up_ld"), m.sem("down_ld"), m.sem("l1w_ld")
        rows_step, rows_done = m.sem("rows_step"), m.sem("rows_done")
        xln_ln, xseed_done, xrstd_done = m.sem("xln2_ln"), m.sem("xseed2_done"), m.sem("xrstd2_done")
        newton, xshift_done = m.sem("newton2"), m.sem("xshift2_done")
        xln_done = [m.sem(f"xln2_done{i}") for i in range(2)]
        xT_done, xT_hi_done, xT_lo_done = m.sem("xT2_done"), m.sem("xT2_hi_done"), m.sem("xT2_lo_done")
        xT_stored = m.sem("xT2_stored")
        gathered = [m.sem(f"head_gathered{h}") for h in range(FH)]
        up_hi_done, up_lo_done = m.sem("up_hi_done"), m.sem("up_lo_done")
        up_done, gelu_done, down_done = m.sem("up_done"), m.sem("gelu_done"), m.sem("down_done")
        yT_copied = m.sem("yT_copied")
        scattered = [m.sem(f"yT_scattered{jt}") for jt in range(KT)]
        mT_done, mT_copied = m.sem("mT_done"), m.sem("mT_copied")
        z_done, z_copied, g_done, g_copied = m.sem("z_done"), m.sem("z_copied"), m.sem("g_done"), m.sem("g_copied")
        zstat_step, gmean_done = m.sem("zstat_step"), m.sem("gmean_done")
        dev_step, gvar_done = m.sem("dev_step"), m.sem("gvar_done")
        xT_ps, z_ps, up_ps, yT_ps = [s.ps[i] for i in (0, 1, 4, 5)], s.ps[6:8], s.ps[2:6], s.ps[6:8]
        g_ps = s.ps[4:6]
        mT_ps, sm_ps = s.ps[2], s.ps[0]
        PACKS = 2 * KT

        stage = ExitStack()
        block = stage.enter_context(nc.Block())

        @block.sync
        def _(sp):
            for dst, src in ((wt, d.wt), (wzT, d.wzT), (wgT, d.wgT), (s.group_mean, d.group_mean)):
                sp.dma_start(dst[:, :], src).then_inc(w_ld, 16)
            for dst, src in ((gn_w, d.gn_w), (gn_b, d.gn_b), (s.wpT, d.wpT)):
                sp.dma_start(dst[:, :], src).then_inc(col_ld if dst is not s.wpT else s.wp_ld, 16)
            for part in range(3):
                sp.dma_start(rows_i[part * FD:(part + 1) * FD, :], d.perm_heads).then_inc(rows_ld, 16)
            sp.dma_start(perm_col[:, :], d.perm_col).then_inc(rows_ld, 16)
            for part in range(3):
                sp.dma_start(up_raw[part * FD:(part + 1) * FD, :, :], d.up).then_inc(up_ld, 16)
            sp.dma_start(down[:, :], d.down).then_inc(down_ld, 16)
            for b in range(0, B, 2):
                tok = slice(b * P, (b + 2) * P)
                for part, (xT, done) in enumerate(((s.xT_hi, xT_hi_done), (s.xT_lo, xT_lo_done))):
                    sp.wait_ge(done, b + 2)
                    sp.dma_start(d.xT_scr[part, :, :, tok].rearrange("k p n -> p k n"),
                                 xT[:, :, tok].bitcast(F32)).then_inc(xT_stored, 16)
            for jt in range(KT):
                sp.wait_ge(scattered[jt], 16)
            for c in range(2):
                half = slice(c * HALF, (c + 1) * HALF)
                sp.dma_start(yU[:, :, half], d.yT_scr[:, half].rearrange("(k p) n -> p k n", p=P))\
                    .then_inc(s.yU_ld[c], 16)

        @block.scalar
        def _(act):
            act.activation(xtmp[:, :], xval[:, :], ACT.Ln, scale=2.0).then_inc(xln_ln, 1)
            act.wait_ge(xln_ln, 1)
            act.activation(xseed[:, :], xtmp[:, :], ACT.Exp, scale=-0.5).then_inc(xseed_done, 1)

            def normalise(b):
                act.wait_ge(xshift_done, 1)
                reached(act, xT_done, b - 1)
                act.activation(xln[:, b % 2, :], s.x[:, b, :], ACT.Identity, bias=xshift[:, b:b + 1],
                               scale=xrstd[:, b:b + 1]).then_inc(xln_done[1], 1)

            def copy_z(b):
                act.wait_ge(z_done, b + 1)
                act.activation(s.z[:, b, :], z_ps[b % 2][:, :], ACT.Copy).then_inc(z_copied, 1)

            normalise(1)
            for b in range(B):
                if b % 2 and b + 2 < B:
                    normalise(b + 2)
                act.wait_ge(xT_done, b + 1)
                act.activation(s.xT_hi[:, :, b * P:(b + 1) * P], blocks(xT_ps[b % 4][:, :]), ACT.Copy)\
                    .then_inc(xT_hi_done, 1)
                if b == HB:
                    act.wait_ge(mT_done, 1)
                    act.activation(mT[:, :], mT_ps[:, 0:P], ACT.Copy).then_inc(mT_copied, 1)
            act.wait_ge(up_ld, 16 * 3)
            act.activation(up[:, :, :], up_raw[:, :, :], ACT.Copy).then_inc(up_hi_done, 1)
            for b in range(B):
                copy_z(b)
            act.preload_act_table(ACT.Gelu)
            for n in range(PACKS):
                reached(act, down_done, n - 1)
                for i in range(HG):
                    act.wait_ge(up_done, HG * n + i + 1)
                    act.activation(hid[:, HG * (n % 2) + i, :], up_ps[i][:, :], ACT.Gelu).then_inc(gelu_done, 1)
            act.preload_act_table_set(LN_EXP_SET)
            for b in range(B):
                act.wait_ge(g_done, b + 1)
                act.activation(s.g[:, b, :], g_ps[b % 2][:, :], ACT.Copy).then_inc(g_copied, 1)

        @block.gpsimd
        def _(pool):
            pool.wait_ge(xseed_done, 1)
            newton_rsqrt(pool, newton, 0, xval[:, :], xseed[:, :], xtmp[:, :], xrstd[:, :], s.c15)\
                .then_inc(xrstd_done, 1)
            pool.wait_ge(rows_done, 1)
            pool.wait_ge(xT_stored, 16 * B)
            for h in range(FH):
                pool.indirect_dma_start(out=xg[:, h, :], out_offset=None, in_=d.xT_scr_rows,
                                        in_offset=IndirectOffsetOnAxis(ap=rows[:, h:h + 1], axis=0))\
                    .then_inc(gathered[h], 16)
            for jt in range(KT):
                pool.wait_ge(yT_copied, 2 * jt + 2)
                pool.indirect_dma_start(out=d.yT_scr,
                                        out_offset=IndirectOffsetOnAxis(ap=perm_col[:, jt:jt + 1], axis=0),
                                        in_=yT[:, jt % 2, :], in_offset=None).then_inc(scattered[jt], 16)

        @block.vector
        def _(dve):
            def gather_rows():
                dve.memset(lo_rows[:, :], 0.0).then_inc(rows_step, 1)
                dve.wait_ge(rows_step, 1)
                dve.memset(lo_rows[2 * FD:P3, :], float(D)).then_inc(rows_step, 1)
                dve.wait_ge(rows_ld, 16 * 4)
                dve.tensor_copy(rows_f[:, :], rows_i[:, :]).then_inc(rows_step, 1)
                dve.wait_ge(rows_step, 3)
                dve.tensor_tensor(rows_f[:, :], rows_f[:, :], lo_rows[:, :], ALU.add).then_inc(rows_step, 1)
                dve.wait_ge(rows_step, 4)
                dve.tensor_copy(rows[:, :], rows_f[:, :]).then_inc(rows_done, 1)

            def normalise(b):
                dve.wait_ge(xrstd_done, 1)
                reached(dve, xT_done, b - 1)
                dve.tensor_scalar(xln[:, b % 2, :], s.x[:, b, :], mv[:, b, 0:1], xrstd[:, b:b + 1],
                                  ALU.subtract, ALU.mult).then_inc(xln_done[0], 1)

            dve.wait_ge(xrstd_done, 1)
            negated_shift(dve, s, slice(0, B), xrstd, xshift).then_inc(xshift_done, 1)
            normalise(0)
            for b in range(B):
                if b == HB:
                    gather_rows()
                if b % 2 == 0 and b + 2 < B:
                    normalise(b + 2)
                dve.wait_ge(xT_hi_done, b + 1)
                dve.tensor_tensor(s.xT_lo[:, :, b * P:(b + 1) * P], blocks(xT_ps[b % 4][:, :]),
                                  s.xT_hi[:, :, b * P:(b + 1) * P].bitcast(F32), ALU.subtract)\
                    .then_inc(xT_lo_done, 1)
            dve.wait_ge(up_hi_done, 1)
            dve.tensor_tensor(up[FD:2 * FD, :, :], up_raw[FD:2 * FD, :, :], up[FD:2 * FD, :, :].bitcast(F32),
                              ALU.subtract).then_inc(up_lo_done, 1)
            for b in range(B):
                dve.wait_ge(z_copied, b + 1)
                dve.bn_stats(zbn[:, b, :], s.z[:, b, :]).then_inc(zstat_step, 1)
                dve.wait_ge(zstat_step, 2 * b + 1)
                dve.bn_aggr(s.zmv[:, b, :], zbn[:, b, :]).then_inc(zstat_step, 1)
            dve.wait_ge(gmean_done, 1)
            dve.tensor_copy(s.gmean[:, :], sm_ps[:, 0:B]).then_inc(dev_step, 1)
            dve.wait_ge(dev_step, 1)
            dve.tensor_tensor(dev[:, :], s.zmv[:, :, 0], s.gmean[:, :], ALU.subtract).then_inc(dev_step, 1)
            dve.wait_ge(dev_step, 2)
            dve.tensor_tensor(dev[:, :], dev[:, :], dev[:, :], ALU.mult).then_inc(dev_step, 1)
            dve.wait_ge(dev_step, 3)
            dve.tensor_tensor(dev[:, :], dev[:, :], s.zmv[:, :, 1], ALU.add).then_inc(dev_step, 1)

            for n in range(PACKS):
                jt, c = divmod(n, 2)
                dve.wait_ge(down_done, n + 1)
                if jt >= 2:
                    dve.wait_ge(scattered[jt - 2], 16)
                dve.tensor_copy(yT[:, jt % 2, c * HALF:(c + 1) * HALF], yT_ps[n % 2][:, :])\
                    .then_inc(yT_copied, 1)
                if n == PACKS // 2:
                    dve.wait_ge(gvar_done, 1)
                    dve.tensor_copy(s.gvar[:, :], sm_ps[:, 256:256 + B]).then_inc(dev_step, 1)
            dve.wait_ge(col_ld, 32)
            dve.tensor_tensor(s.tw[:, :], gn_w[:, :], s.tgates[:, 1:2], ALU.mult).then_inc(col_step, 1)
            dve.tensor_tensor(s.tb[:, :], gn_b[:, :], s.tgates[:, 1:2], ALU.mult).then_inc(col_step, 1)
            dve.tensor_scalar(s.nmean[:, :], s.gmean[:, :], -1.0, None, ALU.mult).then_inc(col_step, 1)

        @block.tensor
        def _(pe):
            def z_product(b):
                reached(pe, z_copied, b - 1)
                pe.matmul(z_ps[b % 2][:, :], mT[:, :], s.ctx_nat[:, b, :], start=True, stop=True).then_inc(z_done, 1)

            for b in range(B):
                pe.wait_ge(xln_done[b % 2], b // 2 + 1)
                reached(pe, xT_lo_done, b - 3)
                for kt in range(KT):
                    last = pe.transpose(xT_ps[b % 4][:, kt * P:(kt + 1) * P], xln[:, b % 2, kt * P:(kt + 1) * P],
                                        s.ident[:, :])
                last.then_inc(xT_done, 1)
                if b == HB:
                    pe.wait_ge(w_ld, 16 * 4)
                    pe.matmul(mT_ps[:, 0:P], wt[:, :], wzT[:, :], start=True, stop=True).then_inc(mT_done, 1)
            pe.wait_ge(mT_copied, 1)
            for b in range(B):
                z_product(b)
            pe.wait_ge(up_lo_done, 1)
            pe.wait_ge(down_ld, 16)
            for n in range(PACKS + 1):
                if n < PACKS:
                    jt, c = divmod(n, 2)
                    for i in range(HG):
                        pe.wait_ge(gathered[HG * jt + i], 16)
                        reached(pe, gelu_done, HG * (n - 1) + i + 1)
                        pe.matmul(up_ps[i][:, :], up[:, HG * jt + i, :],
                                  xg[:, HG * jt + i, c * HALF:(c + 1) * HALF].bitcast(F32R), start=True, stop=True)\
                            .then_inc(up_done, 1)
                if n == 1:
                    pe.wait_ge(z_copied, B)
                if n >= 1:
                    k = n - 1
                    pe.wait_ge(gelu_done, HG * (k + 1))
                    reached(pe, yT_copied, k - 1)
                    for i in range(HG):
                        hh = HG * (k // 2) + i
                        last = pe.matmul(yT_ps[k % 2][FD * i:FD * (i + 1), :], down[:, hh * FD:(hh + 1) * FD],
                                         hid[:, HG * (k % 2) + i, :], start=True, stop=True)
                    last.then_inc(down_done, 1)
                if n == 2:
                    pe.wait_ge(zstat_step, 2 * B)
                    pe.wait_ge(xT_lo_done, B)
                    pe.matmul(sm_ps[:, 0:B], s.group_mean[:, :], s.zmv[:, :, 0], start=True, stop=True)\
                        .then_inc(gmean_done, 1)
                if n == 3:
                    pe.wait_ge(dev_step, 4)
                    pe.matmul(sm_ps[:, 256:256 + B], s.group_mean[:, :], dev[:, :], start=True, stop=True)\
                        .then_inc(gvar_done, 1)
            for b in range(B):
                reached(pe, g_copied, b - 1)
                pe.matmul(g_ps[b % 2][:, :], wgT[:, :], s.ctx_nat[:, b, :], start=True, stop=True).then_inc(g_done, 1)

        stage.close()


def nonlocal_attention(nc, d, s):
    with ExitStack() as ctx:
        m = Mem(nc, ctx)
        xln = m.sb("xln3", [P, HB, D])
        mv, xval, xseed = s.mv, s.xval, m.sb("xseed3", [P, B])
        xtmp, xrstd, xshift = m.sb("xtmp3", [P, B]), m.sb("xrstd3", [P, B]), m.sb("xshift3", [P, B])
        prod = m.sb("prod", [P, 2, D])
        row, att, yval = m.sb("att_row", [P, B]), m.sb("att", [P, B]), m.sb("yval", [P, B])
        yln, yseed, ytmp, yrstd = (m.sb(n, [P, B]) for n in ("yln", "yseed", "ytmp", "yrstd"))

        y_done, x_done, xval_done = m.sem("y_done"), m.sem("x2_done"), m.sem("xval3_done")
        bn_done, mv_done = m.sem("bn3_done"), m.sem("mv3_done")
        xln_ln, xseed_done, xrstd_done = m.sem("xln3_ln"), m.sem("xseed3_done"), m.sem("xrstd3_done")
        newton, xshift_done, xln_done = m.sem("newton3"), m.sem("xshift3_done"), m.sem("xln3_done")
        p_done, row_done, att_done = m.sem("pp_done"), m.sem("row_done"), m.sem("att_done")
        att_step, yval_done = m.sem("att_step"), m.sem("yval_done")
        yln_done, yseed_done, yrstd_done = m.sem("yln_done"), m.sem("yseed_done"), m.sem("yrstd_done")
        res_done, ctx_scaled, centred = m.sem("res_done"), m.sem("ctx_scaled"), m.sem("centred")
        y_ps, p_ps, att_ps = s.ps[0:3], s.ps[3:7], s.ps[7]

        stage = ExitStack()
        block = stage.enter_context(nc.Block())

        @block.sync
        def _(sp):
            for e in range(E):
                sp.dma_start(s.exp_w[:, e, :, :], d.exp_w[e]).then_inc(s.exp_ld, 16)

        @block.scalar
        def _(act):
            for b in range(B):
                act.activation(s.ctx_nat[:, b, :], s.ctx_nat[:, b, :], ACT.Identity, bias=s.tb[:, 0:1],
                               scale=s.tgates[:, 1:2]).then_inc(ctx_scaled, 1)
            for c in range(2):
                cols = slice(c * HB, (c + 1) * HB)
                act.wait_ge(xval_done, c + 1)
                act.activation(xtmp[:, cols], xval[:, cols], ACT.Ln, scale=2.0).then_inc(xln_ln, 1)
                act.wait_ge(xln_ln, c + 1)
                act.activation(xseed[:, cols], xtmp[:, cols], ACT.Exp, scale=-0.5).then_inc(xseed_done, 1)
                act.wait_ge(xshift_done, c + 1)
                for b in range(c * HB, (c + 1) * HB):
                    reached(act, p_done, b - HB + 1)
                    act.activation(xln[:, b % HB, :], s.x[:, b, :], ACT.Identity, bias=xshift[:, b:b + 1],
                                   scale=xrstd[:, b:b + 1]).then_inc(xln_done, 1)
            for b in range(B):
                act.activation(s.z[:, b, :], s.z[:, b, :], ACT.Identity, bias=s.nmean[:, b:b + 1]).then_inc(centred, 1)
            act.wait_ge(yval_done, 1)
            act.activation(yln[:, :], yval[:, :], ACT.Ln, scale=2.0).then_inc(yln_done, 1)
            act.wait_ge(yln_done, 1)
            act.activation(yseed[:, :], yln[:, :], ACT.Exp, scale=-0.5).then_inc(yseed_done, 1)

        @block.gpsimd
        def _(pool):
            for c in range(2):
                cols = slice(c * HB, (c + 1) * HB)
                pool.wait_ge(xseed_done, c + 1)
                newton_rsqrt(pool, newton, 3 * c, xval[:, cols], xseed[:, cols], xtmp[:, cols], xrstd[:, cols],
                             s.c15).then_inc(xrstd_done, 1)
                if c == 0:
                    pool.wait_ge(ctx_scaled, B)
                for b in (range(2), range(2, B))[c]:
                    pool.wait_ge(xln_done, b + 1)
                    pool.tensor_tensor(s.x[:, b, :], s.x[:, b, :], s.ctx_nat[:, b, :], ALU.add).then_inc(res_done, 1)
            pool.wait_ge(yseed_done, 1)
            newton_rsqrt(pool, newton, 6, yval[:, :], yseed[:, :], ytmp[:, :], yrstd[:, :], s.c15).then_inc(yrstd_done, 1)

        @block.vector
        def _(dve):
            def update_x(b):
                if b == HB + 3:
                    shift(0)
                dve.wait_ge(y_done, b + 1)
                return dve.scalar_tensor_tensor(out=s.x[:, b, :], in0=y_ps[b % 3][:, :], scalar=s.tgates[:, 2:3],
                                                in1=s.x[:, b, :], op0=ALU.mult, op1=ALU.add)

            def shift(c):
                dve.wait_ge(xrstd_done, c + 1)
                negated_shift(dve, s, slice(c * HB, (c + 1) * HB), xrstd, xshift).then_inc(xshift_done, 1)

            updates_with_stats(dve, s, update_x, x_done, bn_done, mv_done, xval_done)
            for b in range(B):
                if b == 1:
                    shift(1)
                dve.wait_ge(p_done, b + 1)
                reached(dve, row_done, b - 1)
                dve.tensor_tensor_reduce(out=prod[:, b % 2, :], in0=p_ps[b % 4][:, :], in1=s.g[:, b, :],
                                         scale=1.0, scalar=0.0, op0=ALU.mult, op1=ALU.add,
                                         accum_out=row[:, b:b + 1]).then_inc(row_done, 1)
            dve.wait_ge(att_done, 1)
            dve.tensor_scalar(att[:, :], att_ps[:, 0:B], 16.0, None, ALU.mult).then_inc(att_step, 1)
            dve.wait_ge(att_step, 1)
            dve.tensor_tensor(yval[:, :], att[:, :], att[:, :], ALU.mult).then_inc(att_step, 1)
            dve.wait_ge(att_step, 2)
            dve.tensor_tensor(yval[:, :], yval[:, :], s.gvar[:, :], ALU.mult).then_inc(att_step, 1)
            dve.wait_ge(att_step, 3)
            dve.tensor_scalar(yval[:, :], yval[:, :], EPS, 0.5, ALU.add, ALU.mult).then_inc(yval_done, 1)
            dve.tensor_scalar(att[:, :], att[:, :], s.tw[:, 0:1], None, ALU.mult).then_inc(att_step, 1)
            dve.wait_ge(yrstd_done, 1)
            dve.wait_ge(att_step, 4)
            dve.tensor_tensor(s.a_col[:, :], att[:, :], yrstd[:, :], ALU.mult).then_inc(att_step, 1)

        @block.tensor
        def _(pe):
            for b in range(B):
                pe.wait_ge(s.yU_ld[b // HB], 16)
                reached(pe, x_done, b - 2)
                for kt in range(KT):
                    last = pe.transpose(y_ps[b % 3][:, kt * P:(kt + 1) * P],
                                        s.yU[:, kt, b * P:(b + 1) * P], s.ident[:, :])
                last.then_inc(y_done, 1)
            pe.wait_ge(s.wp_ld, 16)
            for b in range(B):
                pe.wait_ge(xln_done, b + 1)
                reached(pe, row_done, b - 3)
                pe.matmul(p_ps[b % 4][:, :], s.wpT[:, :], xln[:, b % HB, :], start=True, stop=True)\
                    .then_inc(p_done, 1)
            pe.wait_ge(row_done, B)
            pe.matmul(att_ps[:, 0:B], s.group_mean[:, :], row[:, :], start=True, stop=True).then_inc(att_done, 1)

        stage.close()


def experts(nc, d, s):
    with ExitStack() as ctx:
        m = Mem(nc, ctx)
        xln = s.g
        mv, xval, xseed = s.mv, s.xval, m.sb("xseed4", [P, B])
        xtmp, xrstd, xshift = m.sb("xtmp4", [P, B]), m.sb("xrstd4", [P, B]), m.sb("xshift4", [P, B])
        zero = m.sb("zero", [P, D])
        gate_w, fold = m.sb("gate_w", [P, KT, P // KT]), m.sb("fold", [P, E])
        gateT = s.ctx_nat[:, 4:6, :]
        gate_b, eid = m.sb("gate_b", [P, E]), m.sb("eid", [P, SORTED])
        rows_before, upto = m.sb("rows_before", [P, P]), m.sb("upto", [P, E, E])
        ones, steps = m.sb("ones", [P, P]), m.sb("steps", [P, B])
        exp_b = m.sb("exp_b", [E, D])
        exp_b_hi, exp_b_lo = m.sb("exp_b_hi", [E, D], F32R), m.sb("exp_b_lo", [E, D], F32R)
        logit, top = m.sb("logit", [P, B, E]), m.sb("top", [P, B])
        cand, first = m.sb("cand", [P, B, E]), m.sb("first", [P, B])
        hot, hot_sum = m.sb("hot", [P, B, E]), m.sb("hot_sum", [P, E])
        hotT = m.sb("hotT", [E, B, P], F32R)
        fuller, tiles = m.sb("fuller", [P, E, B]), m.sb("tiles", [P, E])
        below, end, begin = m.sb("below", [P, E, E]), m.sb("end", [P, E]), m.sb("begin", [P, E])
        place, pos = m.sb("place", [P, B, E]), m.sb("pos", [P, B])
        pos_i = m.sb("pos_i", [P, B], I32)
        past, tile_e = m.sb("past", [P, SORTED, E]), m.sb("tile_e", [P, SORTED])
        tile_i = m.sb("tile_i", [P, SORTED], I32)
        xT = [s.hid[:, c * KT:(c + 1) * KT, :] for c in range(2)]
        xs = s.hid[:, 0:2, :]
        xsT_hi, xsT_lo = m.sb("xsT_hi", [P, 2, D], F32R), m.sb("xsT_lo", [P, 2, D], F32R)
        w_hi, w_lo = ([x[:, :, i * D:(i + 1) * D] for i in range(2)] for x in (s.xT_hi, s.xT_lo))
        ys, y_tok = s.ctx_nat[:, 1:3, :], s.acc

        small_ld, gate_w_set = m.sem("gate_ld"), m.sem("gate_w_set")
        exp_b_hi_done, exp_b_lo_done = m.sem("exp_b_hi_done"), m.sem("exp_b_lo_done")
        gateT_done, gateT_copied = m.sem("gateT_done"), m.sem("gateT_copied")
        zero_set, zero_stored = m.sem("zero_set"), m.sem("zero_stored")
        bn_done, mv_done = m.sem("bn4_done"), m.sem("mv4_done")
        x3_done, xval_done, xshift_done = m.sem("x3_done"), m.sem("xval4_done"), m.sem("xshift4_done")
        ones_set = m.sem("ones_set")
        xln_ln, xseed_done, xrstd_done = m.sem("xln4_ln"), m.sem("xseed4_done"), m.sem("xrstd4_done")
        newton, xln_done = m.sem("newton4"), [m.sem(f"xln4_done{c}") for c in range(2)]
        xT_done, xT_copied = m.sem("xT4_done"), m.sem("xT4_copied")
        logit_done, gate_step, hot_done = m.sem("logit_done"), m.sem("gate_step"), m.sem("hot_done")
        hot_summed, rank_done, count_done = m.sem("hot_summed"), m.sem("rank_done"), m.sem("count_done")
        pos_done, tile_done, scattered = m.sem("pos_done"), m.sem("tile_done"), m.sem("scattered")
        hotT_done, hotT_copied, bias_done = m.sem("hotT_done"), m.sem("hotT_copied"), m.sem("bias_done")
        bias_added = m.sem("bias_added")
        xs_ld = [m.sem(f"xs_ld{i}") for i in range(2)]
        xsT_done, xsT_hi_done, xsT_lo_done = m.sem("xsT_done"), m.sem("xsT_hi_done"), m.sem("xsT_lo_done")
        w_hi_done, w_lo_done = m.sem("ew_hi_done"), [m.sem("ew_lo_dve_done"), m.sem("ew_lo_pool_done")]
        y_done, y_copied = m.sem("ey_done"), m.sem("ey_copied")
        y_stored = [m.sem(f"y_stored{i}") for i in range(2)]
        gathered, x_done, stored = [m.sem(f"gathered{b}") for b in range(B)], m.sem("x4_done"), m.sem("stored")
        xT_ps, logit_ps, rank_ps, hotT_ps = [s.ps[i] for i in (0, 1, 4, 5)], s.ps[2], s.ps[3], s.ps[4:6]
        gateT_ps, count_ps = s.ps[6:8], s.ps[0]
        bias_ps = s.ps[6:8]
        xsT_ps, y_ps = s.ps[0:2], s.ps[3:5]
        LOADS = 7

        def run(eng, stages):

            def step(r, j):
                for stage, ahead in stages:
                    t = 2 * r + j + ahead
                    if not isinstance(t, int) or 0 <= t < SORTED:
                        stage(t, (j + ahead) % 2, r + (j + ahead) // 2)

            rounds = SORTED // 2
            for j in range(2):
                step(-1, j)
            for j in range(2):
                step(0, j)
            with eng.Fori(1, rounds - 1) as r:
                for j in range(2):
                    step(r, j)
            for k in range(5):
                step(rounds - 1 + k // 2, k % 2)

        stage = ExitStack()
        block = stage.enter_context(nc.Block())

        @block.sync
        def _(sp):
            sp.wait_ge(gate_w_set, 1)
            for dst, src in ((gate_w[:, :, 0:E], d.gate_w), (fold[:, :], d.fold), (gate_b[:, :], d.gate_b), (eid[:, :], d.eid),
                             (rows_before[:, :], d.rows_before), (upto[:, :, :], d.upto), (exp_b[:, :], d.exp_b)):
                sp.dma_start(dst, src).then_inc(small_ld, 16)
            sp.wait_ge(zero_set, 1)
            sp.dma_start(d.sorted_x.rearrange("t p n -> p t n"),
                         zero[:, :].unsqueeze(1).to_broadcast([P, SORTED, D])).then_inc(zero_stored, 16)
            sp.wait_ge(scattered, 16 * B)

            def load(t, slot, r):
                reached(sp, xsT_done, t - 1)
                sp.dma_start(xs[:, slot, :], d.sorted_x[t, :, :]).then_inc(xs_ld[slot], 16)

            def store(t, slot, r):
                sp.wait_ge(y_copied, t + 1)
                sp.dma_start(d.sorted_y[t, :, :], ys[:, slot, :]).then_inc(y_stored[slot], 16)

            run(sp, [(load, 2), (store, -1)])
            for b in range(B):
                sp.wait_ge(x_done, b + 1)
                sp.dma_start(d.out[:, b, :], s.x[:, b, :]).then_inc(stored, 16)
            sp.wait_ge(stored, 16 * B)

        @block.scalar
        def _(act):
            def seed(c):
                cols = slice(c * HB, (c + 1) * HB)
                act.wait_ge(xval_done, c + 1)
                act.activation(xtmp[:, cols], xval[:, cols], ACT.Ln, scale=2.0).then_inc(xln_ln, 1)
                act.wait_ge(xln_ln, c + 1)
                act.activation(xseed[:, cols], xtmp[:, cols], ACT.Exp, scale=-0.5).then_inc(xseed_done, 1)

            def normalise(b):
                act.activation(xln[:, b, :], s.x[:, b, :], ACT.Identity, bias=xshift[:, b:b + 1],
                               scale=xrstd[:, b:b + 1]).then_inc(xln_done[0], 1)

            def copy_xT(b):
                act.wait_ge(xT_done, b + 1)
                act.activation(xT[b // HB][:, :, (b % HB) * P:(b % HB + 1) * P], blocks(xT_ps[b % 4][:, :]), ACT.Copy)\
                    .then_inc(xT_copied, 1)

            def copy_gateT(c):
                act.wait_ge(gateT_done, c + 1)
                act.activation(gateT[:, c, :], gateT_ps[c][:, :], ACT.Copy).then_inc(gateT_copied, 1)

            seed(0)
            act.wait_ge(xshift_done, 1)
            normalise(0)
            normalise(1)
            copy_xT(0)
            normalise(2)
            copy_xT(1)
            normalise(3)
            seed(1)
            copy_xT(2)
            copy_xT(3)
            copy_gateT(0)
            for b in range(HB, B):
                copy_xT(b)
            copy_gateT(1)
            act.wait_ge(small_ld, 16 * LOADS)
            act.activation(exp_b_hi[:, :], exp_b[:, :], ACT.Copy).then_inc(exp_b_hi_done, 1)
            for k in range(2):
                act.wait_ge(hotT_done, k + 1)
                act.activation(hotT[:, k * HB:(k + 1) * HB, :], blocks(hotT_ps[k][0:E, :]), ACT.Copy)\
                    .then_inc(hotT_copied, 1)

            def split_x(t, slot, r):
                act.wait_ge(xsT_done, t + 1)
                reached(act, y_done, t - 1)
                act.activation(xsT_hi[:, slot, :], xsT_ps[slot][:, :], ACT.Copy).then_inc(xsT_hi_done, 1)

            def split_w(t, slot, r):
                reached(act, y_done, t - 1)
                e = act.value_load(tile_i[0:1, bass.ds(t, 1)], min_val=0, max_val=E - 1)
                for kt in range(KT):
                    act.activation(w_hi[slot][:, kt, :], s.exp_w[:, e, kt, :], ACT.Copy).then_inc(w_hi_done, 1)

            act.wait_ge(tile_done, 1)
            act.wait_ge(s.exp_ld, 16 * E)
            def split_next_w(t, slot, r):
                if not (isinstance(t, int) and t == 0):
                    split_w(t, slot, r)

            split_w(0, 0, 0)
            run(act, [(split_x, 1), (split_next_w, 1)])

        @block.gpsimd
        def _(pool):
            pool.memset(zero[:, :], 0.0).then_inc(zero_set, 1)
            for c in range(2):
                cols = slice(c * HB, (c + 1) * HB)
                pool.wait_ge(xseed_done, c + 1)
                newton_rsqrt(pool, newton, 3 * c, xval[:, cols], xseed[:, cols], xtmp[:, cols], xrstd[:, cols],
                             s.c15).then_inc(xrstd_done, 1)
            pool.wait_ge(zero_stored, 16)
            pool.wait_ge(pos_done, 1)
            for b in range(B):
                pool.indirect_dma_start(out=d.sorted_x_rows, out_offset=IndirectOffsetOnAxis(ap=pos_i[:, b:b + 1], axis=0),
                                        in_=xln[:, b, :], in_offset=None).then_inc(scattered, 16)

            def split_w(t, slot, r):
                e = pool.value_load(tile_i[0:1, bass.ds(t, 1)], min_val=0, max_val=E - 1)
                for kt in (2, 3):
                    pool.wait_ge(w_hi_done, KT * t + kt + 1)
                    pool.tensor_tensor(w_lo[slot][:, kt, :], s.exp_w[:, e, kt, :],
                                       w_hi[slot][:, kt, :].bitcast(F32), ALU.subtract).then_inc(w_lo_done[1], 1)

            pool.wait_ge(tile_done, 1)
            run(pool, [(split_w, 1)])
            for i in range(2):
                pool.wait_ge(y_stored[i], 16 * ((SORTED + 1 - i) // 2))
            for b in range(B):
                pool.indirect_dma_start(out=y_tok[:, b, :], out_offset=None, in_=d.sorted_y_rows,
                                        in_offset=IndirectOffsetOnAxis(ap=pos_i[:, b:b + 1], axis=0))\
                    .then_inc(gathered[b], 16)

        @block.vector
        def _(dve):
            dve.memset(gate_w[:, :, :], 0.0).then_inc(gate_w_set, 1)
            dve.memset(ones[:, :], 1.0).then_inc(ones_set, 1)
            for k in range(B):
                dve.memset(steps[:, k:k + 1], float(P * k)).then_inc(ones_set, 1)
            def update_x(b):
                if b == HB + 3:
                    dve.wait_ge(xrstd_done, 1)
                    negated_shift(dve, s, slice(0, HB), xrstd, xshift).then_inc(xshift_done, 1)
                return dve.scalar_tensor_tensor(out=s.x[:, b, :], in0=s.z[:, b, :], scalar=s.a_col[:, b:b + 1],
                                                in1=s.x[:, b, :], op0=ALU.mult, op1=ALU.add)

            updates_with_stats(dve, s, update_x, x3_done, bn_done, mv_done, xval_done)
            dve.wait_ge(xrstd_done, 2)
            for b in range(HB, B):
                dve.tensor_scalar(xln[:, b, :], s.x[:, b, :], mv[:, b, 0:1], xrstd[:, b:b + 1],
                                  ALU.subtract, ALU.mult).then_inc(xln_done[1], 1)
            dve.wait_ge(logit_done, 2)
            dve.wait_ge(small_ld, 16 * LOADS)
            over_b = lambda ap: ap.unsqueeze(1).to_broadcast([P, B, E])
            dve.tensor_tensor(logit[:, :, :], logit_ps[:, 0:B * E].rearrange("p (b e) -> p b e", b=B),
                              over_b(gate_b[:, :]), ALU.add).then_inc(gate_step, 1)
            dve.wait_ge(gate_step, 1)
            dve.tensor_reduce(top[:, :], logit[:, :, :], axis=AX_X, op=ALU.max).then_inc(gate_step, 1)
            dve.wait_ge(gate_step, 2)
            dve.tensor_tensor(cand[:, :, :], logit[:, :, :], per_block(top[:, :], E), ALU.is_lt)\
                .then_inc(gate_step, 1)
            dve.wait_ge(gate_step, 3)
            dve.scalar_tensor_tensor(out=cand[:, :, :], in0=cand[:, :, :], scalar=float(E),
                                     in1=over_b(eid[:, 0:E]), op0=ALU.mult, op1=ALU.add).then_inc(gate_step, 1)
            dve.wait_ge(gate_step, 4)
            dve.tensor_reduce(first[:, :], cand[:, :, :], axis=AX_X, op=ALU.min).then_inc(gate_step, 1)
            dve.wait_ge(gate_step, 5)
            dve.tensor_tensor(hot[:, :, :], cand[:, :, :], per_block(first[:, :], E), ALU.is_equal)\
                .then_inc(hot_done, 1)
            dve.wait_ge(hot_done, 1)
            dve.tensor_reduce(hot_sum[:, :], hot[:, :, :].rearrange("p b e -> p e b"), axis=AX_X, op=ALU.add)\
                .then_inc(hot_summed, 1)
            dve.wait_ge(count_done, 1)
            dve.tensor_tensor(fuller[:, :, :], per_block(count_ps[:, 0:E], B),
                              steps[:, :].unsqueeze(1).to_broadcast([P, E, B]), ALU.is_gt).then_inc(gate_step, 1)
            dve.wait_ge(gate_step, 6)
            dve.tensor_reduce(tiles[:, :], fuller[:, :, :], axis=AX_X, op=ALU.add).then_inc(gate_step, 1)
            dve.wait_ge(gate_step, 7)
            dve.tensor_tensor(below[:, :, :], upto[:, :, :], tiles[:, :].unsqueeze(1).to_broadcast([P, E, E]),
                              ALU.mult).then_inc(gate_step, 1)
            dve.wait_ge(gate_step, 8)
            dve.tensor_reduce(end[:, :], below[:, :, :], axis=AX_X, op=ALU.add).then_inc(gate_step, 1)
            dve.wait_ge(gate_step, 9)
            dve.tensor_tensor(begin[:, :], end[:, :], tiles[:, :], ALU.subtract).then_inc(gate_step, 1)
            dve.wait_ge(gate_step, 10)
            dve.wait_ge(rank_done, 1)
            dve.scalar_tensor_tensor(out=place[:, :, :], in0=over_b(begin[:, :]), scalar=float(P),
                                     in1=rank_ps[:, 0:B * E].rearrange("p (b e) -> p b e", b=B),
                                     op0=ALU.mult, op1=ALU.add).then_inc(gate_step, 1)
            dve.wait_ge(gate_step, 11)
            dve.tensor_tensor(place[:, :, :], place[:, :, :], hot[:, :, :], ALU.mult).then_inc(gate_step, 1)
            dve.wait_ge(gate_step, 12)
            dve.tensor_reduce(pos[:, :], place[:, :, :], axis=AX_X, op=ALU.add).then_inc(gate_step, 1)
            dve.wait_ge(gate_step, 13)
            dve.tensor_copy(pos_i[:, :], pos[:, :]).then_inc(pos_done, 1)
            dve.tensor_tensor(past[:, :, :], per_block(eid[:, 0:SORTED], E),
                              end[:, :].unsqueeze(1).to_broadcast([P, SORTED, E]), ALU.is_ge).then_inc(gate_step, 1)
            dve.wait_ge(gate_step, 14)
            dve.tensor_reduce(tile_e[:, :], past[:, :, :], axis=AX_X, op=ALU.add).then_inc(gate_step, 1)
            dve.wait_ge(gate_step, 15)
            dve.tensor_scalar(tile_e[:, :], tile_e[:, :], float(E - 1), None, ALU.min).then_inc(gate_step, 1)
            dve.wait_ge(gate_step, 16)
            dve.tensor_copy(tile_i[:, :], tile_e[:, :]).then_inc(tile_done, 1)
            dve.wait_ge(exp_b_hi_done, 1)
            dve.tensor_tensor(exp_b_lo[:, :], exp_b[:, :], exp_b_hi[:, :].bitcast(F32), ALU.subtract)\
                .then_inc(exp_b_lo_done, 1)
            for b in range(B):
                dve.wait_ge(bias_done, b + 1)
                dve.scalar_tensor_tensor(out=s.x[:, b, :], in0=bias_ps[b % 2][:, :], scalar=s.tgates[:, 3:4],
                                         in1=s.x[:, b, :], op0=ALU.mult, op1=ALU.add).then_inc(bias_added, 1)

            def split_x(t, slot, r):
                dve.wait_ge(xsT_hi_done, t + 1)
                dve.tensor_tensor(xsT_lo[:, slot, :], xsT_ps[slot][:, :], xsT_hi[:, slot, :].bitcast(F32),
                                  ALU.subtract).then_inc(xsT_lo_done, 1)

            def split_w(t, slot, r):
                e = dve.value_load(tile_i[0:1, bass.ds(t, 1)], min_val=0, max_val=E - 1)
                for kt in (0, 1):
                    dve.wait_ge(w_hi_done, KT * t + kt + 1)
                    dve.tensor_tensor(w_lo[slot][:, kt, :], s.exp_w[:, e, kt, :],
                                      w_hi[slot][:, kt, :].bitcast(F32), ALU.subtract).then_inc(w_lo_done[0], 1)

            def copy_y(t, slot, r):
                dve.wait_ge(y_done, t + 1)
                if not isinstance(r, int) or r >= 1:
                    dve.wait_ge(y_stored[slot], 16 * r)
                dve.tensor_copy(ys[:, slot, :], y_ps[slot][:, :]).then_inc(y_copied, 1)

            dve.wait_ge(tile_done, 1)
            def split_next_w(t, slot, r):
                if not (isinstance(t, int) and t == 0):
                    split_w(t, slot, r)

            split_w(0, 0, 0)
            run(dve, [(split_x, 1), (copy_y, -1), (split_next_w, 1)])
            for b in range(B):
                dve.wait_ge(gathered[b], 16)
                dve.wait_ge(bias_added, b + 1)
                dve.scalar_tensor_tensor(out=s.x[:, b, :], in0=y_tok[:, b, :], scalar=s.tgates[:, 3:4],
                                         in1=s.x[:, b, :], op0=ALU.mult, op1=ALU.add).then_inc(x_done, 1)

        @block.tensor
        def _(pe):
            def keep_clock(n):
                for _ in range(n):
                    pe.matmul(s.ps[2][:, :], s.ident[:, :], s.ctx_nat[:, 0, :], start=True, stop=True)

            def transpose_x(b):
                pe.wait_ge(xln_done[b // HB], b % HB + 1)
                reached(pe, xT_copied, b - 3)
                for kt in range(KT):
                    last = pe.transpose(xT_ps[b % 4][:, kt * P:(kt + 1) * P], xln[:, b, kt * P:(kt + 1) * P],
                                        s.ident[:, :])
                last.then_inc(xT_done, 1)

            def gates(c):
                pe.wait_ge(xT_copied, HB * (c + 1))
                for kt in range(KT):
                    last = pe.matmul(gateT_ps[c][32 * kt:32 * kt + 32, :], gate_w[:, kt, :], xT[c][:, kt, :],
                                     start=True, stop=True)
                last.then_inc(gateT_done, 1)

            def logits(c):
                pe.wait_ge(gateT_copied, c + 1)
                for b in range(c * HB, (c + 1) * HB):
                    last = pe.matmul(logit_ps[:, b * E:(b + 1) * E], gateT[:, c, (b % HB) * P:(b % HB + 1) * P],
                                     fold[:, :], start=True, stop=True)
                last.then_inc(logit_done, 1)

            keep_clock(WARM)
            for b in range(HB):
                transpose_x(b)
            pe.wait_ge(small_ld, 16 * LOADS)
            gates(0)
            transpose_x(HB)
            transpose_x(HB + 1)
            logits(0)
            transpose_x(HB + 2)
            transpose_x(HB + 3)
            gates(1)
            logits(1)
            pe.wait_ge(ones_set, 1 + B)
            pe.wait_ge(hot_summed, 1)
            pe.matmul(count_ps[:, 0:E], ones[:, :], hot_sum[:, :], start=True, stop=True).then_inc(count_done, 1)
            flat = hot[:, :, :].rearrange("p b e -> p (b e)")
            pe.matmul(rank_ps[:, 0:B * E], rows_before[:, :], flat, start=True, stop=False)
            for k in range(1, B):
                last = pe.matmul(rank_ps[:, k * E:B * E], ones[:, :], flat[:, 0:(B - k) * E], start=False,
                                 stop=(k == B - 1))
            last.then_inc(rank_done, 1)
            for k in range(2):
                for i in range(HB):
                    last = pe.transpose(hotT_ps[k][0:E, i * P:(i + 1) * P], hot[:, k * HB + i, :], s.ident[:, :])
                last.then_inc(hotT_done, 1)
            for b in range(B):
                pe.wait_ge(hotT_copied, b // HB + 1)
                reached(pe, bias_added, b - 1)
                if b == 0:
                    pe.wait_ge(exp_b_lo_done, 1)
                pe.matmul(bias_ps[b % 2][:, :], hotT[:, b, :], exp_b_hi[:, :], start=True, stop=False)
                pe.matmul(bias_ps[b % 2][:, :], hotT[:, b, :], exp_b_lo[:, :], start=False, stop=True)\
                    .then_inc(bias_done, 1)
            keep_clock(WARM2)

            def transpose_tile(t, slot, r):
                pe.wait_ge(xs_ld[slot], 16 * r + 16)
                reached(pe, xsT_lo_done, t - 1)
                for kt in range(KT):
                    last = pe.transpose(xsT_ps[slot][:, kt * P:(kt + 1) * P], xs[:, slot, kt * P:(kt + 1) * P],
                                        s.ident[:, :])
                last.then_inc(xsT_done, 1)

            def multiply(t, slot, r):
                pe.wait_ge(xsT_lo_done, t + 1)
                reached(pe, y_copied, t - 1)
                out = y_ps[slot][:, :]
                for kt in range(KT):
                    pe.wait_ge(w_lo_done[kt // 2], 2 * t + kt % 2 + 1)
                    cols = slice(kt * P, (kt + 1) * P)
                    pe.matmul(out, xsT_hi[:, slot, cols], w_hi[slot][:, kt, :], start=(kt == 0), stop=False)
                    pe.matmul(out, xsT_lo[:, slot, cols], w_hi[slot][:, kt, :], start=False, stop=False)
                    last = pe.matmul(out, xsT_hi[:, slot, cols], w_lo[slot][:, kt, :], start=False, stop=(kt == KT - 1))
                last.then_inc(y_done, 1)

            run(pe, [(transpose_tile, 1), (multiply, 0)])

        stage.close()


class Names:
    pass


def flamingo(nc, a, out):
    d = Names()
    d.x = a["x"].rearrange("b t n -> t b n")
    d.ctx = a["ctx"].rearrange("b t n -> t b n")
    d.out = out.rearrange("b t n -> t b n")
    d.ctxT = a["ctxT"]
    d.kv_w = [a["kw_l"][0], a["kw_l"][1], a["vw_l"][0], a["vw_l"][1], a["wq_l"][0]]
    d.ident, d.qw, d.kw, d.mask = a["ident"], a["q_norm"], a["k_norm"], a["mask"]
    d.g_xattn, d.g_ffn = a["g_xattn"].to_broadcast([P, 2]), a["g_ffn"].to_broadcast([P, 2])
    d.wq, d.wo = a["wq_l"], a["wo_l"]
    d.perm_heads, d.perm_col = a["perm_heads"], a["perm_col"]
    d.up, d.down = a["up_l"], a["down_l"]
    d.wt, d.wzT, d.wgT, d.wpT = a["wt"], a["wzT"], a["wgT"], a["wpT"]
    d.group_mean, d.gn_w, d.gn_b = a["group_mean"], a["gn_w"], a["gn_b"]
    d.gate_w, d.gate_b = a["gate_w_l"], a["gate_b"].to_broadcast([P, E])
    d.eid = a["iota"].to_broadcast([P, SORTED])
    d.fold = a["fold"]
    d.rows_before, d.upto = a["rows_before"], a["upto"].to_broadcast([P, E, E])
    d.exp_b, d.exp_w = a["exp_b"], a["exp_w_l"]
    d.kT_scr = nc.dram_tensor("kT_scr", (G, P, T), F32, kind="Internal").ap()
    d.xT_scr = nc.dram_tensor("xT_scr", (2, KT, P, T), F32, kind="Internal").ap()
    d.xT_scr_rows = d.xT_scr.rearrange("a k p n -> (a k p) n")
    d.yT_scr = nc.dram_tensor("yT_scr", (D, T), F32, kind="Internal").ap()
    d.sorted_x = nc.dram_tensor("sorted_x", (SORTED, P, D), F32, kind="Internal").ap()
    d.sorted_y = nc.dram_tensor("sorted_y", (SORTED, P, D), F32, kind="Internal").ap()
    d.sorted_x_rows = d.sorted_x.rearrange("t p n -> (t p) n")
    d.sorted_y_rows = d.sorted_y.rearrange("t p n -> (t p) n")
    d.v_scr = nc.dram_tensor("v_scr", (G, P, B, P), F32, kind="Internal").ap()

    with ExitStack() as ctx:
        m = Mem(nc, ctx)
        s = Names()
        s.ps = [ctx.enter_context(nc.psum_tensor(f"bank{i}", [P, D], F32)) for i in range(8)]
        s.x = m.sb("x_sb", [P, B, D])
        s.xT_hi, s.xT_lo = m.sb("xT_hi", [P, KT, T], F32R), m.sb("xT_lo", [P, KT, T], F32R)
        s.ident = m.sb("ident_sb", [P, P])
        s.gates, s.tgates = m.sb("gates", [P, 4]), m.sb("tgates", [P, 4])
        s.eps, s.eps_set = m.sb("eps", [P, 1]), m.sem("eps_set")
        s.c15, s.c15_set = m.sb("three_halves", [P, B]), m.sem("three_halves_set")
        s.acc = m.sb("acc", [P, B, D])
        s.ctx_nat = m.sb("ctx_nat", [P, B, D])
        s.bn, s.mv, s.xval = m.sb("bn", [P, B, 6]), m.sb("mv", [P, B, 2]), m.sb("xval", [P, B])
        with ExitStack() as weights:
            w = Mem(nc, weights)
            s.w_raw = w.sb("w_raw", [P, 2, KT, D])
            s.w_hi, s.w_lo = w.sb("w_hi", [P, 2, KT, D], F32R), w.sb("w_lo", [P, 2, KT, D], F32R)
            s.kT, s.v_raw, s.mask = w.sb("kT", [P, T]), w.sb("v_raw", [P, B, P]), w.sb("mask", [P, P])
            s.v_st = w.sb("v_st", [P, 2, D])
            s.v_stored = [m.sem(f"v_stored{i}") for i in range(2)]
            project_kv(nc, d, s)
            attention(nc, d, s)
        s.z, s.g = s.acc, m.sb("g_sb", [P, B, D])
        s.group_mean, s.zmv = m.sb("group_mean", [P, P]), m.sb("zmv", [P, B, 2])
        s.gmean, s.gvar = m.sb("gmean", [P, B]), m.sb("gvar", [P, B])
        s.tw, s.a_col, s.wpT = m.sb("tw", [P, 1]), m.sb("a_col", [P, B]), m.sb("wpT", [P, P])
        s.hid = m.sb("hid", [P, 2 * HG, HALF])
        s.yU = s.hid[:, :, :].rearrange("p i t -> p (i t)").rearrange("p (k t) -> p k t", k=KT)
        s.yU_ld = [m.sem(f"yU_ld{c}") for c in range(2)]
        s.tb, s.nmean, s.wp_ld = m.sb("tb", [P, 1]), m.sb("nmean", [P, B]), m.sem("wp_ld")
        feed_forward(nc, d, s)
        s.exp_w, s.exp_ld = m.sb("exp_w", [P, E, KT, D]), m.sem("exp_ld")
        nonlocal_attention(nc, d, s)
        experts(nc, d, s)


def kernel(**inputs):
    import numpy as np
    import concourse.bacc as bacc
    from concourse.bass_utils import run_bass_kernel_spmd

    i = {k: np.asarray(v) for k, v in inputs.items()}
    wz = i["L1_xattn_Wz"].reshape(8, 16, 16)
    wzT = np.zeros((P, P), np.float32)
    for g in range(8):
        wzT[16 * g:16 * g + 16, 16 * g:16 * g + 16] = wz[g].T
    arrays = {
        "x": i["x"],
        "ctx": i["ctx_4096"],
        "ctxT": i["ctx_4096"].reshape(T, KT, P).transpose(2, 1, 0),
        "kw_l": i["L0_xattn_k_proj_w"].reshape(2, D, KT, P).transpose(0, 3, 2, 1),
        "vw_l": i["L0_xattn_v_proj_w"].reshape(2, D, KT, P).transpose(0, 3, 2, 1),
        "wq_l": i["L0_xattn_q_proj_w"].reshape(G, D, KT, P).transpose(0, 3, 2, 1),
        "wo_l": i["L0_xattn_o_proj_w"].reshape(D, G, HG, P).transpose(1, 3, 2, 0),
        "q_norm": i["L0_xattn_q_norm_w"].reshape(P, 1),
        "k_norm": i["L0_xattn_k_norm_w"].reshape(P, 1),
        "mask": i["mask_1x1xSxS2_ff0"].reshape(P, P),
        "g_xattn": i["g_xattn"].reshape(1, 2),
        "g_ffn": i["g_ffn"].reshape(1, 2),
        "perm_heads": i["L0_ffn_perm"].reshape(FH, FD).T,
        "perm_col": i["L0_ffn_perm"].reshape(KT, P).T,
        "up_l": i["L0_ffn_up"].transpose(1, 0, 2),
        "down_l": i["L0_ffn_down"].transpose(1, 0, 2).reshape(P, D),
        "wt": i["L1_xattn_Wt"],
        "wzT": wzT,
        "wgT": i["L1_xattn_Wg"].T,
        "wpT": i["L1_xattn_Wp"].T,
        "gn_w": i["L1_xattn_gn_w"].reshape(P, 1),
        "gn_b": i["L1_xattn_gn_b"].reshape(P, 1),
        "gate_w_l": i["L1_ffn_gate_w"].reshape(E, KT, P).transpose(2, 1, 0),
        "gate_b": i["L1_ffn_gate_b"].reshape(1, E),
        "exp_w_l": i["L1_ffn_expert_w"].reshape(E, D, KT, P).transpose(0, 3, 2, 1),
        "exp_b": i["L1_ffn_expert_b"],
        "ident": np.eye(P, dtype=np.float32),
        "iota": np.arange(SORTED, dtype=np.float32).reshape(1, SORTED),
        "fold": np.tile(np.eye(P // KT, E, dtype=np.float32), (KT, 1)),
        "rows_before": np.triu(np.ones((P, P), np.float32), 1),
        "upto": np.tril(np.ones((E, E), np.float32)).reshape(1, E, E),
        "group_mean": np.kron(np.eye(8), np.full((16, 16), 1 / 16)).astype(np.float32),
    }
    arrays = {k: np.ascontiguousarray(v) for k, v in arrays.items()}
    nc = bacc.Bacc("TRN2", target_bir_lowering=False, num_devices=1)
    aps = {k: nc.dram_tensor(f"in_{k}", v.shape, mybir.dt.from_np(v.dtype), kind="ExternalInput").ap()
           for k, v in arrays.items()}
    out = nc.dram_tensor("out", (B, P, D), F32, kind="ExternalOutput").ap()
    flamingo(nc, aps, out)
    r = run_bass_kernel_spmd(nc, [{f"in_{k}": v for k, v in arrays.items()}], core_ids=[0])
    return r.results[0]["out"]
```
